# Optimizing a Trainium2 kernel written in Bass

```python
import numpy as np
import jax
import jax.numpy as jnp

def _softmax(x, axis=-1):
    return jax.nn.softmax(x, axis=axis)

def _gelu(x):
    return jax.nn.gelu(x, approximate=True)

def _silu(x):
    return jax.nn.silu(x)

def _sigmoid(x):
    return jax.nn.sigmoid(x)

def _layernorm(x, axis=-1, eps=1e-05):
    m = jnp.mean(x, axis=axis, keepdims=True)
    v = jnp.var(x, axis=axis, keepdims=True)
    return (x - m) / jnp.sqrt(v + eps)

def _scatter_add(tgt, idx, src, axis=0):
    return tgt.at[idx].add(src)

def _segment_sum(src, seg, n):
    return jax.ops.segment_sum(src, seg, n)
kernel_name = 'mk_adaln_d1_jaxref_r4_2f674a'

def setup_inputs(seed: int=0):
    np.random.seed(seed)
    _w = jnp.asarray

    def _L0_attn_setup():
        import jax, jax.numpy as jnp
        import numpy as np
        NUM_HEADS = 16
        D_MODEL = 256
        HEAD_DIM = D_MODEL // NUM_HEADS
        EPS = 1e-06

        def _feature_map(x):
            return jax.nn.elu(x) + 1.0
        key = jax.random.key(seed)
        ks = jax.random.split(key, 9)
        B, S, D = (4, 2048, D_MODEL)
        scale = 1.0 / np.sqrt(D)
        inputs_q = jax.random.normal(ks[0], (B, S, D), dtype=jnp.float32)
        Wq = jax.random.normal(ks[1], (D, D), dtype=jnp.float32) * scale
        Wk = jax.random.normal(ks[2], (D, D), dtype=jnp.float32) * scale
        Wv = jax.random.normal(ks[3], (D, D), dtype=jnp.float32) * scale
        Wo = jax.random.normal(ks[4], (D, D), dtype=jnp.float32) * scale
        bq = jnp.zeros((D,), jnp.float32)
        bk = jnp.zeros((D,), jnp.float32)
        bv = jnp.zeros((D,), jnp.float32)
        bo = jnp.zeros((D,), jnp.float32)
        return {'inputs_q': inputs_q, 'Wq': Wq, 'bq': bq, 'Wk': Wk, 'bk': bk, 'Wv': Wv, 'bv': bv, 'Wo': Wo, 'bo': bo}
    _L0_attn_in = _L0_attn_setup()

    def _L0_ffn_setup():
        import jax, jax.numpy as jnp
        import numpy as np
        DIM = 256
        DEPTH = 2
        HEADS = 8
        DIM_HEAD = 64
        WINDOW = 128
        INNER = HEADS * DIM_HEAD
        HID = int(DIM * 4 * 2 / 3)
        B, N = (2, 2048)
        QK_SCALE = 8.0

        def shift_token(t):
            t1, t2 = jnp.split(t, 2, axis=-1)
            t2 = jnp.pad(t2, ((0, 0), (1, 0), (0, 0)))[:, :-1]
            return jnp.concatenate([t1, t2], axis=-1)

        def l2norm(t):
            return t / jnp.clip(jnp.linalg.norm(t, axis=-1, keepdims=True), 1e-12)

        def rotate_half(x):
            x1, x2 = jnp.split(x, 2, axis=-1)
            return jnp.concatenate([-x2, x1], axis=-1)

        def rotary_xpos(q, k):
            n = q.shape[-2]
            half_idx = jnp.arange(0, DIM_HEAD, 2, dtype=jnp.float32)
            inv_freq = 1.0 / 10000.0 ** (half_idx / DIM_HEAD)
            t = jnp.arange(n, dtype=jnp.float32)
            freqs = t[:, None] * inv_freq[None, :]
            freqs = jnp.concatenate([freqs, freqs], axis=-1)
            base = (half_idx + 0.4 * DIM_HEAD) / (1.4 * DIM_HEAD)
            power = (t - n // 2) / float(WINDOW // 2)
            scale = base[None, :] ** power[:, None]
            scale = jnp.concatenate([scale, scale], axis=-1)
            cos, sin = (jnp.cos(freqs), jnp.sin(freqs))
            q = q * cos * scale + rotate_half(q) * sin * scale
            k = k * cos / scale + rotate_half(k) * sin / scale
            return (q, k)

        def local_attention(q, k, v):
            b, h, n, d = q.shape
            w = n // WINDOW
            bq = q.reshape(b, h, w, WINDOW, d) * QK_SCALE
            bk = k.reshape(b, h, w, WINDOW, d)
            bv = v.reshape(b, h, w, WINDOW, d)

            def look_around(t):
                p = jnp.pad(t, ((0, 0), (0, 0), (1, 0), (0, 0), (0, 0)))
                return jnp.concatenate([p[:, :, :w], p[:, :, 1:]], axis=3)
            bk, bv = (look_around(bk), look_around(bv))
            bt = jnp.arange(n).reshape(w, WINDOW)
            btp = jnp.pad(bt, ((1, 0), (0, 0)), constant_values=-1)
            btk = jnp.concatenate([btp[:w], btp[1:]], axis=1)
            sim = jnp.einsum('bhwid,bhwjd->bhwij', bq, bk)
            i = bt[:, :, None]
            j = btk[:, None, :]
            mask = (i < j) | (i > j + WINDOW) | (j == -1)
            sim = jnp.where(mask, -jnp.finfo(sim.dtype).max, sim)
            attn = jax.nn.softmax(sim, axis=-1)
            out = jnp.einsum('bhwij,bhwjd->bhwid', attn, bv)
            return out.reshape(b, h, n, d)

        def _layer(x, wqkv, qs, ksc, wo, lg, lb, w1, b1, w2, b2):
            b, n, _ = x.shape
            h = shift_token(x)
            qkv = h @ wqkv
            q, k, v = jnp.split(qkv, 3, axis=-1)
            to_heads = lambda t: t.reshape(b, n, HEADS, DIM_HEAD).transpose(0, 2, 1, 3)
            q, k, v = (to_heads(q), to_heads(k), to_heads(v))
            q = l2norm(q) * qs
            k = l2norm(k) * ksc
            q, k = rotary_xpos(q, k)
            o = local_attention(q, k, v)
            o = o.transpose(0, 2, 1, 3).reshape(b, n, INNER)
            x = x + o @ wo
            h = shift_token(x)
            mu = h.mean(-1, keepdims=True)
            var = h.var(-1, keepdims=True)
            h = (h - mu) / jnp.sqrt(var + 1e-05) * lg + lb
            h = h @ w1 + b1
            a, g = jnp.split(h, 2, axis=-1)
            h = a * jax.nn.gelu(g, approximate=False)
            x = x + h @ w2 + b2
            return x
        key = jax.random.key(seed)
        ks = jax.random.split(key, 6)
        return {'x': jax.random.normal(ks[0], (B, N, DIM), jnp.float32), 'wqkv': jax.random.normal(ks[1], (DEPTH, DIM, 3 * INNER), jnp.float32) * 0.02, 'q_scale': jnp.ones((DEPTH, DIM_HEAD), jnp.float32), 'k_scale': jnp.ones((DEPTH, DIM_HEAD), jnp.float32), 'wo': jax.random.normal(ks[2], (DEPTH, INNER, DIM), jnp.float32) * 0.02, 'ln_g': jnp.ones((DEPTH, DIM), jnp.float32), 'ln_b': jnp.zeros((DEPTH, DIM), jnp.float32), 'w1': jax.random.normal(ks[3], (DEPTH, DIM, 2 * HID), jnp.float32) * 0.02, 'b1': jnp.zeros((DEPTH, 2 * HID), jnp.float32), 'w2': jax.random.normal(ks[4], (DEPTH, HID, DIM), jnp.float32) * 0.02, 'b2': jnp.zeros((DEPTH, DIM), jnp.float32)}
    _L0_ffn_in = _L0_ffn_setup()
    _L0_c = _w((lambda *s: np.random.randn(*s).astype(np.float32) * 0.05)(4, 256))
    _L0_wmod = _w((lambda *s: np.random.randn(*s).astype(np.float32) * 0.05)(256, 6 * 256) * 256 ** (-0.5))
    _d = {'L0_attn_inputs_q': _L0_attn_in['inputs_q'], 'L0_attn_Wq': _L0_attn_in['Wq'], 'L0_attn_bq': _L0_attn_in['bq'], 'L0_attn_Wk': _L0_attn_in['Wk'], 'L0_attn_bk': _L0_attn_in['bk'], 'L0_attn_Wv': _L0_attn_in['Wv'], 'L0_attn_bv': _L0_attn_in['bv'], 'L0_attn_Wo': _L0_attn_in['Wo'], 'L0_attn_bo': _L0_attn_in['bo'], 'L0_ffn_wqkv': _L0_ffn_in['wqkv'], 'L0_ffn_q_scale': _L0_ffn_in['q_scale'], 'L0_ffn_k_scale': _L0_ffn_in['k_scale'], 'L0_ffn_wo': _L0_ffn_in['wo'], 'L0_ffn_ln_g': _L0_ffn_in['ln_g'], 'L0_ffn_ln_b': _L0_ffn_in['ln_b'], 'L0_ffn_w1': _L0_ffn_in['w1'], 'L0_ffn_b1': _L0_ffn_in['b1'], 'L0_ffn_w2': _L0_ffn_in['w2'], 'L0_ffn_b2': _L0_ffn_in['b2'], 'L0_c': _L0_c, 'L0_wmod': _L0_wmod}
    _x0 = _d['L0_attn_inputs_q']
    _d['L0_attn_inputs_q'] = jax.random.normal(jax.random.fold_in(jax.random.key(seed), 1), (4, 2048, 256), dtype=_x0.dtype)
    del _x0
    return _d

def reference(L0_attn_inputs_q, L0_attn_Wq, L0_attn_bq, L0_attn_Wk, L0_attn_bk, L0_attn_Wv, L0_attn_bv, L0_attn_Wo, L0_attn_bo, L0_ffn_wqkv, L0_ffn_q_scale, L0_ffn_k_scale, L0_ffn_wo, L0_ffn_ln_g, L0_ffn_ln_b, L0_ffn_w1, L0_ffn_b1, L0_ffn_w2, L0_ffn_b2, L0_c, L0_wmod):

    def _L0_attn_ref(inputs_q, Wq, bq, Wk, bk, Wv, bv, Wo, bo):
        import jax, jax.numpy as jnp
        import numpy as np
        NUM_HEADS = 16
        D_MODEL = 256
        HEAD_DIM = D_MODEL // NUM_HEADS
        EPS = 1e-06

        def _feature_map(x):
            return jax.nn.elu(x) + 1.0
        B, S, D = inputs_q.shape
        H, Dh = (NUM_HEADS, HEAD_DIM)
        q = (inputs_q @ Wq + bq).reshape(B, S, H, Dh)
        k = (inputs_q @ Wk + bk).reshape(B, S, H, Dh)
        v = (inputs_q @ Wv + bv).reshape(B, S, H, Dh)
        q = _feature_map(q)
        k = _feature_map(k)
        kv = jnp.einsum('bkhd,bkhm->bhdm', k, v)
        out = jnp.einsum('bqhd,bhdm->bqhm', q, kv)
        normalizer = jnp.einsum('bqhd,bkhd->bqh', q, k)
        normalizer = jnp.maximum(normalizer, EPS)
        out = out / normalizer[..., None]
        out = out.reshape(B, S, D)
        return out @ Wo + bo

    def _L0_ffn_ref(x, wqkv, q_scale, k_scale, wo, ln_g, ln_b, w1, b1, w2, b2):
        import jax, jax.numpy as jnp
        import numpy as np
        DIM = 256
        DEPTH = 2
        HEADS = 8
        DIM_HEAD = 64
        WINDOW = 128
        INNER = HEADS * DIM_HEAD
        HID = int(DIM * 4 * 2 / 3)
        B, N = (2, 2048)
        QK_SCALE = 8.0

        def shift_token(t):
            t1, t2 = jnp.split(t, 2, axis=-1)
            t2 = jnp.pad(t2, ((0, 0), (1, 0), (0, 0)))[:, :-1]
            return jnp.concatenate([t1, t2], axis=-1)

        def l2norm(t):
            return t / jnp.clip(jnp.linalg.norm(t, axis=-1, keepdims=True), 1e-12)

        def rotate_half(x):
            x1, x2 = jnp.split(x, 2, axis=-1)
            return jnp.concatenate([-x2, x1], axis=-1)

        def rotary_xpos(q, k):
            n = q.shape[-2]
            half_idx = jnp.arange(0, DIM_HEAD, 2, dtype=jnp.float32)
            inv_freq = 1.0 / 10000.0 ** (half_idx / DIM_HEAD)
            t = jnp.arange(n, dtype=jnp.float32)
            freqs = t[:, None] * inv_freq[None, :]
            freqs = jnp.concatenate([freqs, freqs], axis=-1)
            base = (half_idx + 0.4 * DIM_HEAD) / (1.4 * DIM_HEAD)
            power = (t - n // 2) / float(WINDOW // 2)
            scale = base[None, :] ** power[:, None]
            scale = jnp.concatenate([scale, scale], axis=-1)
            cos, sin = (jnp.cos(freqs), jnp.sin(freqs))
            q = q * cos * scale + rotate_half(q) * sin * scale
            k = k * cos / scale + rotate_half(k) * sin / scale
            return (q, k)

        def local_attention(q, k, v):
            b, h, n, d = q.shape
            w = n // WINDOW
            bq = q.reshape(b, h, w, WINDOW, d) * QK_SCALE
            bk = k.reshape(b, h, w, WINDOW, d)
            bv = v.reshape(b, h, w, WINDOW, d)

            def look_around(t):
                p = jnp.pad(t, ((0, 0), (0, 0), (1, 0), (0, 0), (0, 0)))
                return jnp.concatenate([p[:, :, :w], p[:, :, 1:]], axis=3)
            bk, bv = (look_around(bk), look_around(bv))
            bt = jnp.arange(n).reshape(w, WINDOW)
            btp = jnp.pad(bt, ((1, 0), (0, 0)), constant_values=-1)
            btk = jnp.concatenate([btp[:w], btp[1:]], axis=1)
            sim = jnp.einsum('bhwid,bhwjd->bhwij', bq, bk)
            i = bt[:, :, None]
            j = btk[:, None, :]
            mask = (i < j) | (i > j + WINDOW) | (j == -1)
            sim = jnp.where(mask, -jnp.finfo(sim.dtype).max, sim)
            attn = jax.nn.softmax(sim, axis=-1)
            out = jnp.einsum('bhwij,bhwjd->bhwid', attn, bv)
            return out.reshape(b, h, n, d)

        def _layer(x, wqkv, qs, ksc, wo, lg, lb, w1, b1, w2, b2):
            b, n, _ = x.shape
            h = shift_token(x)
            qkv = h @ wqkv
            q, k, v = jnp.split(qkv, 3, axis=-1)
            to_heads = lambda t: t.reshape(b, n, HEADS, DIM_HEAD).transpose(0, 2, 1, 3)
            q, k, v = (to_heads(q), to_heads(k), to_heads(v))
            q = l2norm(q) * qs
            k = l2norm(k) * ksc
            q, k = rotary_xpos(q, k)
            o = local_attention(q, k, v)
            o = o.transpose(0, 2, 1, 3).reshape(b, n, INNER)
            x = x + o @ wo
            h = shift_token(x)
            mu = h.mean(-1, keepdims=True)
            var = h.var(-1, keepdims=True)
            h = (h - mu) / jnp.sqrt(var + 1e-05) * lg + lb
            h = h @ w1 + b1
            a, g = jnp.split(h, 2, axis=-1)
            h = a * jax.nn.gelu(g, approximate=False)
            x = x + h @ w2 + b2
            return x
        for l in range(DEPTH):
            x = _layer(x, wqkv[l], q_scale[l], k_scale[l], wo[l], ln_g[l], ln_b[l], w1[l], b1[l], w2[l], b2[l])
        return x
    x = L0_attn_inputs_q
    mod = (_silu(L0_c) @ L0_wmod).reshape(L0_c.shape[0], 6, 1, -1)
    sa, ca, ga, sb, cb, gb = (mod[:, 0], mod[:, 1], mod[:, 2], mod[:, 3], mod[:, 4], mod[:, 5])
    ga = (2 * (ga >= 0) - 1) * jnp.maximum(jnp.abs(ga), 0.25)
    gb = (2 * (gb >= 0) - 1) * jnp.maximum(jnp.abs(gb), 0.25)
    h = _layernorm(x, axis=-1) * (1 + ca) + sa
    x = x + ga * _L0_attn_ref(h, L0_attn_Wq, L0_attn_bq, L0_attn_Wk, L0_attn_bk, L0_attn_Wv, L0_attn_bv, L0_attn_Wo, L0_attn_bo)
    h = _layernorm(x, axis=-1) * (1 + cb) + sb
    x = x + gb * _L0_ffn_ref(h, L0_ffn_wqkv, L0_ffn_q_scale, L0_ffn_k_scale, L0_ffn_wo, L0_ffn_ln_g, L0_ffn_ln_b, L0_ffn_w1, L0_ffn_b1, L0_ffn_w2, L0_ffn_b2)
    return x

_drawn_inputs = setup_inputs


def setup_inputs(seed=0):
    import zlib

    import numpy as np

    out = dict(_drawn_inputs(seed))
    spreads = {'L0_attn_bq': (0.0, 2.0),
     'L0_attn_bk': (0.0, 2.0),
     'L0_attn_bv': (0.0, 0.313),
     'L0_attn_bo': (0.0, 0.332),
     'L0_ffn_q_scale': (1.0, 0.6),
     'L0_ffn_k_scale': (1.0, 0.6),
     'L0_ffn_ln_g': (1.0, 0.6),
     'L0_ffn_ln_b': (0.0, 0.8),
     'L0_ffn_b1': (0.0, 0.8),
     'L0_ffn_b2': (0.0, 0.522)}
    factors = {'L0_attn_Wq': 8.0,
     'L0_attn_Wk': 8.0,
     'L0_attn_Wv': 8.0,
     'L0_ffn_wqkv': 7.053,
     'L0_ffn_wo': 6.939,
     'L0_ffn_w1': 4.707,
     'L0_ffn_w2': 4.687}
    for name, (base, spread) in spreads.items():
        noise = np.random.default_rng([zlib.crc32(name.encode()), seed]).standard_normal(out[name].shape)
        drawn = base * np.exp(spread * noise) if base else spread * noise
        out[name] = jnp.asarray(drawn.astype(out[name].dtype))
    for name, factor in factors.items():
        out[name] = (out[name] * factor).astype(out[name].dtype)
    return out
```

```python
from contextlib import ExitStack, contextmanager

import concourse.bass as bass
from concourse import mybir

ALU = mybir.AluOpType
ACT = mybir.ActivationFunctionType
AXX = mybir.AxisListType.X
F32 = mybir.dt.float32
BF16 = mybir.dt.bfloat16

P = 128
B, S, D = 4, 2048, 256
DC = D // P
G = 512
TPG = G // P
GPB = S // G
NG = B * GPB
ST = 2
STEPS = NG // ST
H, DH = 8, 64
INNER = H * DH
PAIRS = H // 2
HID = int(D * 4 * 2 / 3)
HC = -(-HID // P)
TAIL = HID - (HC - 1) * P
AH, AD = 16, 16
QK_SCALE = 8.0
BLOCKED = -1.0e30
MODS = 6
LG, LB, B1A, B1G, B2 = 0, DC, 2 * DC, 2 * DC + HC, 2 * DC + 2 * HC
NCOL = B2 + DC


@contextmanager
def cleared_semaphores(nc):
    taken = []

    def take(name):
        taken.append(nc.alloc_semaphore(name=name))
        return taken[-1]

    yield take
    nc.clear_and_free_semaphores(taken)
    nc.all_engine_barrier()


def setup_program(nc, ctx, dram, keep):
    with ExitStack() as own:
        sb = lambda name, shape, dt=F32: own.enter_context(nc.sbuf_tensor(name, shape, dt))
        ps = lambda name, shape: own.enter_context(nc.psum_tensor(name, shape, F32))
        used = own.enter_context(cleared_semaphores(nc))
        sem = lambda name: used(name)
        wmod = sb("wmod", [P, DC, MODS * D])
        c_in = sb("c_in", [P, DC, B])
        c_act = sb("c_act", [P, DC, B])
        sign = sb("sign", [P, DC, B])
        mod_ps = ps("mod_ps", [P, MODS * DC, B])
        loaded, zeroed, selected = sem("loaded"), sem("zeroed"), sem("selected")
        silu_done, mod_ready, mod_step = sem("silu_done"), sem("mod_ready"), sem("mod_step")
        modv, ident, identb, blocks = keep["modv"], keep["ident"], keep["identb"], keep["blocks"]
        block = own.enter_context(nc.Block())

        @block.sync
        def _(sp):
            sp.dma_start(c_in[:, :, :], dram["c"]).then_inc(loaded, 16)
            sp.dma_start(wmod[:, :, :], dram["wmod"].rearrange("(c p) n -> p c n", p=P)).then_inc(loaded, 16)
            sp.dma_start(keep["acol"][:, :], dram["acol"]).then_inc(loaded, 16)
            sp.wait_ge(loaded, 48)

        @block.gpsimd
        def _(pool):
            nc.gpsimd.memset(ident[:, :], 0.0).then_inc(zeroed, 1)
            nc.gpsimd.memset(identb[:, :], 0.0).then_inc(zeroed, 1)
            nc.gpsimd.memset(blocks[:, :], 1.0).then_inc(zeroed, 1)
            nc.gpsimd.memset(keep["flags"][:, :], 1.0).then_inc(zeroed, 1)
            pool.wait_ge(zeroed, 4)
            for m in (ident, identb):
                nc.gpsimd.affine_select(out=m[:, :], in_=m[:, :], compare_op=ALU.not_equal, fill=1.0,
                                        base=0, pattern=[[-1, P]], channel_multiplier=1).then_inc(selected, 1)
            view = blocks[:, :].rearrange("p (h d) -> p h d", d=AD)
            nc.gpsimd.affine_select(out=view, in_=view, compare_op=ALU.is_ge, fill=0.0, base=0,
                                    pattern=[[-AD, P // AD], [0, AD]], channel_multiplier=1).then_inc(selected, 1)
            pool.wait_ge(selected, 3)
            nc.gpsimd.affine_select(out=view, in_=view, compare_op=ALU.is_ge, fill=0.0, base=AD - 1,
                                    pattern=[[AD, P // AD], [0, AD]], channel_multiplier=-1).then_inc(selected, 1)
            nc.gpsimd.memset(keep["flags"][:, 0:1], 0.0).then_inc(selected, 1)
            nc.gpsimd.memset(keep["eps"][:, :], 1e-5).then_inc(selected, 1)
            nc.gpsimd.memset(keep["mean_w"][:, :], 1.0 / D).then_inc(selected, 1)
            nc.gpsimd.memset(keep["ln2x10"][:, :], 6.931471805599453).then_inc(selected, 1)

        @block.scalar
        def _(act):
            act.wait_ge(loaded, 48)
            nc.scalar.activation(c_act[:, :, :], c_in[:, :, :], ACT.Silu).then_inc(silu_done, 1)

        @block.tensor
        def _(pe):
            pe.wait_ge(silu_done, 1)
            for j in range(MODS * DC):
                for c in range(DC):
                    mm = nc.tensor.matmul(mod_ps[:, j, :], wmod[:, c, j * P:(j + 1) * P], c_act[:, c, :],
                                          start=(c == 0), stop=(c == DC - 1))
            mm.then_inc(mod_ready, 1)

        @block.vector
        def _(dve):
            step = [0]

            def chained(instruction):
                step[0] += 1
                instruction.then_inc(mod_step, 1)
                dve.wait_ge(mod_step, step[0])

            dve.wait_ge(loaded, 48)
            dve.wait_ge(mod_ready, 1)
            chained(nc.vector.tensor_copy(modv[:, 0:MODS * DC, :], mod_ps[:, :, :]))
            for j in (1, 4):
                v = modv[:, j * DC:(j + 1) * DC, :]
                chained(nc.vector.tensor_scalar(v, v, 1.0, None, ALU.add))
            for j in (2, 5):
                v = modv[:, j * DC:(j + 1) * DC, :]
                chained(nc.vector.tensor_scalar(sign[:, :, :], v, 0.0, 2.0, ALU.is_ge, ALU.mult))
                chained(nc.vector.tensor_scalar(sign[:, :, :], sign[:, :, :], -1.0, None, ALU.add))
                chained(nc.vector.tensor_tensor(v, v, sign[:, :, :], ALU.mult))
                chained(nc.vector.tensor_scalar(v, v, 0.25, None, ALU.max))
                chained(nc.vector.tensor_tensor(v, v, sign[:, :, :], ALU.mult))
            for c in range(DC):
                chained(nc.vector.tensor_scalar(modv[:, MODS * DC + c, :], modv[:, 2 * DC + c, :],
                                                keep["acol"][:, DC + c:DC + c + 1], None, ALU.mult))
            for g in range(NG):
                chained(nc.vector.tensor_copy(keep["gbg"][:, g, :], modv[:, 5 * DC:6 * DC, g // GPB]))


def linear_attention_program(nc, ctx, dram, keep):
    with ExitStack() as own:
        sb = lambda name, shape, dt=F32: own.enter_context(nc.sbuf_tensor(name, shape, dt))
        ps = lambda name, shape: own.enter_context(nc.psum_tensor(name, shape, F32))
        used = own.enter_context(cleared_semaphores(nc))
        sem = lambda name: used(name)
        modv, acol, eps, ident, blocks, mean_w = (keep[k] for k in ("modv", "acol", "eps", "ident", "blocks", "mean_w"))
        SA, CA, GA, SB, CB, GABO = 0, DC, 2 * DC, 3 * DC, 4 * DC, MODS * DC

        wq = sb("a_wq", [P, DC, D])
        wkv = sb("a_wkv", [P, DC, 2 * D])
        wo = sb("a_wo", [P, DC, D])
        bkv = sb("a_bkv", [P, 2 * D])
        xt = sb("a_xt", [P, GPB, TPG, D])
        xn = sb("a_xn", [P, 2, TPG, D])
        stats = sb("a_stats", [P, TPG, 6])
        mv = sb("a_mv", [P, TPG, 2])
        lnv = sb("a_lnv", [P, TPG])
        rstd = sb("a_rstd", [P, TPG])
        xT = sb("a_xT", [P, DC, S])
        qT = sb("a_qT", [P, DC, S])
        hT = sb("a_hT", [P, 2, DC, G])
        kv = sb("a_kv", [P, 2, 2 * D])
        ek = sb("a_ek", [P, 2, D])
        kf = sb("a_kf", [P, 2, D])
        vo = sb("a_vo", [P, 2, DC, P + 1])
        eq = sb("a_eq", [P, 2, G])
        rq = sb("a_rq", [P, 2, G])
        kvb = sb("a_kvb", [P, DC, P])
        ksb = sb("a_ksb", [P, DC, P])
        ksum = sb("a_ksum", [P, DC])
        nrm = sb("a_nrm", [P, DC, G])
        oT = sb("a_oT", [P, DC, G])
        yT = sb("a_yT", [P, DC, G])
        x1 = sb("a_x1", [P, 2, DC, G])
        xc = sb("a_xc", [P, DC, G])
        sq = sb("a_sq", [P, DC, G])
        lnw = sb("a_lnw", [P, G])
        rsw = sb("a_rsw", [P, G])
        h0 = sb("a_h0", [P, 2, DC, G])
        modc = sb("a_modc", [P, MODS * DC + DC])
        idle = sb("a_idle", [P, 1])

        turn = ps("a_turn", [P, 2, G])
        kvp = ps("a_kvp", [P, 2, G])
        acc = ps("a_acc", [P, DC, G])
        qp = ps("a_qp", [P, 2, G])

        x_in = [sem(f"a_x_in{g}") for g in range(GPB)]
        names = ("w_in modc_set ones_set stat_done mv_done ln_done rstd_done xn_done turn_done turn_used kvp_done kv_set "
                 "ek_done ek_cut kf_done vo_done acc_done q_done eq_done rq_done qT_done ks_set kvb_done on_done "
                 "nrm_cut nrm_done o_done y_done ys_done x1_done mean_done xc_done sq_done var_done lnw_done rsw_done hn_done "
                 "h0_done stored").split()
        s = {name: sem("a_" + name) for name in names}
        block = own.enter_context(nc.Block())

        @block.sync
        def _(sp):
            for dst, src in ((wq, "Wq"), (wo, "Wo")):
                sp.dma_start(dst[:, :, :], dram[src].rearrange("(c p) n -> p c n", p=P)).then_inc(s["w_in"], 16)
            for j, src in enumerate(("Wk", "Wv")):
                sp.dma_start(wkv[:, :, j * D:(j + 1) * D], dram[src].rearrange("(c p) n -> p c n", p=P)).then_inc(s["w_in"], 16)
            for j, src in enumerate(("bk", "bv")):
                sp.dma_start(bkv[:, j * D:(j + 1) * D], dram[src].rearrange("(a n) -> a n", a=1).to_broadcast([P, D])).then_inc(s["w_in"], 16)
            with sp.Fori(0, B) as b:
                for g in range(GPB):
                    sp.wait_ge(s["xn_done"], b * GPB * TPG)
                    sp.wait_ge(s["turn_done"], b * GPB * 2 * DC)
                    sp.dma_start(xt[:, g, :, :], dram["x"][b, g * G:(g + 1) * G, :].rearrange("(t p) d -> p t d", p=P)).then_inc(x_in[g], 16)

        @block.scalar
        def _(act):
            act.wait_ge(s["w_in"], 96)
            nc.scalar.preload_act_table_set("natural_log_exp_and_others")
            with act.Fori(0, B) as b:
                for g in range(GPB):
                    n = b * GPB + g
                    act.wait_ge(s["mv_done"], (n + 1) * TPG)
                    nc.scalar.activation(lnv[:, :], mv[:, :, 1], ACT.Ln, bias=eps[:, 0:1]).then_inc(s["ln_done"], 1)
                    act.wait_ge(s["ln_done"], n + 1)
                    nc.scalar.activation(rstd[:, :], lnv[:, :], ACT.Exp, scale=-0.5).then_inc(s["rstd_done"], 1)
                    if g == 0:
                        act.wait_ge(s["modc_set"], b + 1)
                    for c in range(DC):
                        act.wait_ge(s["turn_done"], n * 2 * DC + c + 1)
                        nc.scalar.activation(xT[:, c, g * G:(g + 1) * G], turn[:, c, :], ACT.Copy).then_inc(s["turn_used"], 1)
                    for c in range(DC):
                        act.wait_ge(s["turn_done"], n * 2 * DC + DC + c + 1)
                        nc.scalar.activation(hT[:, g % 2, c, :], turn[:, c, :], ACT.Identity,
                                             scale=modc[:, CA + c:CA + c + 1], bias=modc[:, SA + c:SA + c + 1]).then_inc(s["turn_used"], 1)
                    for t in range(TPG):
                        m = n * TPG + t
                        act.wait_ge(s["kv_set"], m + 1)
                        nc.scalar.activation(ek[:, t % 2, :], kv[:, t % 2, 0:D], ACT.Exp).then_inc(s["ek_done"], 1)
                        nc.scalar.activation(vo[:, t % 2, :, 0:P], kv[:, t % 2, D:2 * D].rearrange("p (c d) -> p c d", c=DC), ACT.Copy).then_inc(s["vo_done"], 1)
                    for c in range(DC):
                        act.wait_ge(s["q_done"], n * DC + c + 1)
                        nc.scalar.activation(eq[:, c, :], qp[:, c, :], ACT.Exp, bias=acol[:, c:c + 1]).then_inc(s["eq_done"], 1)
                        nc.scalar.activation(rq[:, c, :], qp[:, c, :], ACT.Relu, bias=acol[:, c:c + 1]).then_inc(s["rq_done"], 1)
                for g in range(GPB):
                    n = b * GPB + g
                    for c in range(DC):
                        act.wait_ge(s["y_done"], n * DC + c + 1)
                        nc.scalar.activation(yT[:, c, :], qp[:, c, :], ACT.Identity,
                                             scale=modc[:, GA + c:GA + c + 1], bias=modc[:, GABO + c:GABO + c + 1]).then_inc(s["ys_done"], 1)
                    act.wait_ge(s["xc_done"], n + 1)
                    nc.scalar.activation(sq[:, :, :], xc[:, :, :], ACT.Square).then_inc(s["sq_done"], 1)
                    act.wait_ge(s["var_done"], n + 1)
                    nc.scalar.activation(lnw[:, :], acc[:, 1, :], ACT.Ln, bias=eps[:, 0:1]).then_inc(s["lnw_done"], 1)
                    act.wait_ge(s["lnw_done"], n + 1)
                    nc.scalar.activation(rsw[:, :], lnw[:, :], ACT.Exp, scale=-0.5).then_inc(s["rsw_done"], 1)
                    act.wait_ge(s["hn_done"], n + 1)
                    act.wait_ge(s["stored"], n * 32)
                    for c in range(DC):
                        nc.scalar.activation(h0[:, g % 2, c, :], xc[:, c, :], ACT.Identity,
                                             scale=modc[:, CB + c:CB + c + 1], bias=modc[:, SB + c:SB + c + 1]).then_inc(s["h0_done"], 1)
                    act.wait_ge(s["h0_done"], (n + 1) * DC)
                    act.dma_start(dram["h0"][bass.ds(n, 1)].rearrange("a p n -> (a p) n"), h0[:, g % 2, :, :].rearrange("p c n -> p (c n)")).then_inc(s["stored"], 16)
                    act.wait_ge(s["x1_done"], n + 1)
                    act.dma_start(dram["x1"][bass.ds(n, 1)].rearrange("a p n -> (a p) n"), x1[:, g % 2, :, :].rearrange("p c n -> p (c n)")).then_inc(s["stored"], 16)
            act.wait_ge(s["stored"], NG * 32)

        @block.tensor
        def _(pe):
            pe.wait_ge(s["w_in"], 96)
            with pe.Fori(0, B) as b:
                for g in range(GPB):
                    n = b * GPB + g
                    pe.wait_ge(x_in[g], b * 16 + 16)
                    for j in range(2):
                        src = xt[:, g] if j == 0 else xn[:, g % 2]
                        if j == 1:
                            pe.wait_ge(s["xn_done"], (n + 1) * TPG)
                        for c in range(DC):
                            if j == 1 or g > 0:
                                pe.wait_ge(s["turn_used"], n * 2 * DC + (j * DC + c) - 1)
                            for t in range(TPG):
                                mm = nc.tensor.transpose(turn[:, c, t * P:(t + 1) * P], src[:, t, c * P:(c + 1) * P], ident[:, :])
                            mm.then_inc(s["turn_done"], 1)
                    pe.wait_ge(s["turn_used"], (n + 1) * 2 * DC)
                    for m in range(DC):
                        if g > 0:
                            pe.wait_ge(s["eq_done"], n * DC + m - 1)
                            pe.wait_ge(s["rq_done"], n * DC + m - 1)
                        for c in range(DC):
                            mm = nc.tensor.matmul(qp[:, m, :], wq[:, c, m * P:(m + 1) * P], hT[:, g % 2, c, :],
                                                  start=(c == 0), stop=(c == DC - 1))
                        mm.then_inc(s["q_done"], 1)

                    def accumulate(t):
                        m = n * TPG + t
                        pe.wait_ge(s["kf_done"], m + 1)
                        pe.wait_ge(s["vo_done"], m + 1)
                        first, last = g == 0 and t == 0, g == GPB - 1 and t == TPG - 1
                        for c in range(DC):
                            mm = nc.tensor.matmul(acc[:, c, 0:P + 1], kf[:, t % 2, c * P:(c + 1) * P], vo[:, t % 2, c, :],
                                                  start=first, stop=last)
                        mm.then_inc(s["acc_done"], 1)

                    for t in range(TPG):
                        m = n * TPG + t
                        if g > 0 or t >= 2:
                            pe.wait_ge(s["kv_set"], m - 1)
                        for c in range(DC):
                            mm = nc.tensor.matmul(kvp[:, t % 2, :], hT[:, g % 2, c, t * P:(t + 1) * P], wkv[:, c, :],
                                                  start=(c == 0), stop=(c == DC - 1))
                        mm.then_inc(s["kvp_done"], 1)
                        if t >= 1:
                            accumulate(t - 1)
                    accumulate(TPG - 1)
                pe.wait_ge(s["kvb_done"], (b + 1) * 2)
                pe.wait_ge(s["qT_done"], (b + 1) * GPB * DC)
                for g in range(GPB):
                    n = b * GPB + g
                    if g > 0:
                        pe.wait_ge(s["on_done"], n)
                    for c in range(DC):
                        q = qT[:, c, g * G:(g + 1) * G]
                        nc.tensor.matmul(turn[:, c, :], kvb[:, c, :], q, start=True, stop=True)
                        mm = nc.tensor.matmul(kvp[:, c, :], ksb[:, c, :], q, start=True, stop=True)
                    mm.then_inc(s["o_done"], 1)
                    pe.wait_ge(s["on_done"], n + 1)
                    if g > 0:
                        pe.wait_ge(s["ys_done"], n * DC)
                    for m in range(DC):
                        for c in range(DC):
                            mm = nc.tensor.matmul(qp[:, m, :], wo[:, c, m * P:(m + 1) * P], oT[:, c, :],
                                                  start=(c == 0), stop=(c == DC - 1))
                        mm.then_inc(s["y_done"], 1)
                    pe.wait_ge(s["x1_done"], n + 1)
                    for c in range(DC):
                        mm = nc.tensor.matmul(acc[:, 0, :], mean_w[:, :], x1[:, g % 2, c, :], start=(c == 0), stop=(c == DC - 1))
                    mm.then_inc(s["mean_done"], 1)
                    pe.wait_ge(s["sq_done"], n + 1)
                    for c in range(DC):
                        mm = nc.tensor.matmul(acc[:, 1, :], mean_w[:, :], sq[:, c, :], start=(c == 0), stop=(c == DC - 1))
                    mm.then_inc(s["var_done"], 1)
                pe.wait_ge(s["h0_done"], (b + 1) * GPB * DC)

        @block.vector
        def _(dve):
            nc.vector.memset(vo[:, :, :, P:P + 1], 1.0).then_inc(s["ones_set"], 1)
            nc.vector.memset(idle[:, :], 0.0).then_inc(s["ones_set"], 1)
            dve.wait_ge(s["w_in"], 96)
            with dve.Fori(0, B) as b:
                dve.wait_ge(s["h0_done"], b * GPB * DC)
                nc.vector.tensor_scalar(modc[:, :], modv[:, :, bass.ds(b, 1)].rearrange("p m a -> p (m a)"), 1.0, None, ALU.mult).then_inc(s["modc_set"], 1)
                for g in range(GPB):
                    n = b * GPB + g
                    dve.wait_ge(x_in[g], b * 16 + 16)
                    for t in range(TPG):
                        nc.vector.bn_stats(stats[:, t, :], xt[:, g, t, :]).then_inc(s["stat_done"], 1)
                    dve.wait_ge(s["stat_done"], (n + 1) * TPG)
                    for t in range(TPG):
                        if t == 0:
                            nc.vector.tensor_scalar(idle[:, :], idle[:, :], 1.0, None, ALU.mult)
                        nc.vector.bn_aggr(mv[:, t, :], stats[:, t, :]).then_inc(s["mv_done"], 1)
                    dve.wait_ge(s["rstd_done"], n + 1)
                    for t in range(TPG):
                        nc.vector.tensor_scalar(xn[:, g % 2, t, :], xt[:, g, t, :], mv[:, t, 0:1], rstd[:, t:t + 1],
                                                ALU.subtract, ALU.mult).then_inc(s["xn_done"], 1)
                    for t in range(TPG):
                        m = n * TPG + t
                        dve.wait_ge(s["kvp_done"], m + 1)
                        nc.vector.tensor_tensor(kv[:, t % 2, :], kvp[:, t % 2, :], bkv[:, :], ALU.add).then_inc(s["kv_set"], 1)
                        dve.wait_ge(s["ek_done"], m + 1)
                        nc.vector.tensor_scalar(ek[:, t % 2, :], ek[:, t % 2, :], 1.0, None, ALU.min).then_inc(s["ek_cut"], 1)
                        dve.wait_ge(s["ek_cut"], m + 1)
                        nc.vector.scalar_tensor_tensor(out=kf[:, t % 2, :], in0=kv[:, t % 2, 0:D], scalar=0.0, in1=ek[:, t % 2, :],
                                                       op0=ALU.max, op1=ALU.add).then_inc(s["kf_done"], 1)
                    for c in range(DC):
                        dve.wait_ge(s["rq_done"], n * DC + c + 1)
                        nc.vector.scalar_tensor_tensor(out=qT[:, c, g * G:(g + 1) * G], in0=eq[:, c, :], scalar=1.0, in1=rq[:, c, :],
                                                       op0=ALU.min, op1=ALU.add).then_inc(s["qT_done"], 1)
                dve.wait_ge(s["acc_done"], (b + 1) * (S // P))
                nc.vector.tensor_copy(ksum[:, :], acc[:, :, P]).then_inc(s["ks_set"], 1)
                nc.vector.tensor_tensor(kvb[:, :, :], acc[:, :, 0:P], blocks[:, :].unsqueeze(1).to_broadcast([P, DC, P]), ALU.mult).then_inc(s["kvb_done"], 1)
                dve.wait_ge(s["ks_set"], b + 1)
                nc.vector.tensor_tensor(ksb[:, :, :], blocks[:, :].unsqueeze(1).to_broadcast([P, DC, P]),
                                        ksum[:, :].unsqueeze(2).to_broadcast([P, DC, P]), ALU.mult).then_inc(s["kvb_done"], 1)
                for g in range(GPB):
                    n = b * GPB + g
                    dve.wait_ge(s["o_done"], n + 1)
                    nc.vector.tensor_scalar(nrm[:, :, :], kvp[:, :, :], 1e-6, None, ALU.max).then_inc(s["nrm_cut"], 1)
                    dve.wait_ge(s["nrm_cut"], n + 1)
                    nc.vector.reciprocal(nrm[:, :, :], nrm[:, :, :]).then_inc(s["nrm_done"], 1)
                    dve.wait_ge(s["nrm_done"], n + 1)
                    nc.vector.tensor_tensor(oT[:, :, :], turn[:, :, :], nrm[:, :, :], ALU.mult).then_inc(s["on_done"], 1)
                    dve.wait_ge(s["ys_done"], (n + 1) * DC)
                    dve.wait_ge(s["stored"], n * 32)
                    nc.vector.tensor_tensor(x1[:, g % 2, :, :], xT[:, :, g * G:(g + 1) * G], yT[:, :, :], ALU.add).then_inc(s["x1_done"], 1)
                    dve.wait_ge(s["x1_done"], n + 1)
                    dve.wait_ge(s["mean_done"], n + 1)
                    if g > 0:
                        dve.wait_ge(s["h0_done"], n * DC)
                    nc.vector.tensor_tensor(xc[:, :, :], x1[:, g % 2, :, :], acc[:, 0, :].unsqueeze(1).to_broadcast([P, DC, G]), ALU.subtract).then_inc(s["xc_done"], 1)
                    dve.wait_ge(s["rsw_done"], n + 1)
                    nc.vector.tensor_tensor(xc[:, :, :], xc[:, :, :], rsw[:, :].unsqueeze(1).to_broadcast([P, DC, G]), ALU.mult).then_inc(s["hn_done"], 1)


def layer_program(nc, ctx, layer, dram, keep):
    last_layer = layer == 1
    source = dram["mid"] if last_layer else dram["h0"]
    UNITS = TPG * ST
    W_LOADS = 9
    with ExitStack() as own:
        pre = f"l{layer}_"
        sb = lambda name, shape, dt=F32: own.enter_context(nc.sbuf_tensor(pre + name, shape, dt))
        ps = lambda name, shape: own.enter_context(nc.psum_tensor(pre + name, shape, F32))
        used = own.enter_context(cleared_semaphores(nc))
        sem = lambda name: used(pre + name)
        ident, identb, eps, mean_w, flags, gbg = (keep[k] for k in ("ident", "identb", "eps", "mean_w", "flags", "gbg"))

        wqkv = sb("wqkv", [P, DC, 3 * INNER])
        wo = sb("wo", [P, PAIRS, D])
        w1 = sb("w1", [P, DC, 2, HC * P])
        w2 = sb("w2", [P, HC, D])
        col = sb("col", [P, NCOL])
        qks = sb("qks", [P, 4, DH])
        tab = sb("tab", [P, S // P, 4, DH])
        band = sb("band", [P, 2, 2, P], BF16)
        band0 = sb("band0", [P, GPB, 2, 2, P], BF16)
        xin = sb("xin", [P, ST, DC, 1 + G])
        x2 = sb("x2", [P, ST, DC, 1 + G])
        kT = sb("kT", [P, ST, PAIRS, TPG, P])
        v = sb("v", [P, ST, TPG, INNER])
        attn = sb("attn", [P, ST, PAIRS, G])
        qk = sb("qk", [P, 2, 2, H, DH])
        sq = sb("sq", [P, 2 * INNER])
        ss = sb("ss", [P, 2, 2 * H])
        lss = sb("lss", [P, 2 * H])
        rg = sb("rg", [P, 2 * H])
        nt = sb("nt", [P, 2 * H])
        rr = sb("rr", [P, 2, 2 * H])
        q8 = sb("q8", [P, 2, H])
        rot = sb("rot", [P, 2, 2, H, DH])
        qz = sb("qz", [P, 2, H, P])
        mx = sb("mx", [P, 4])
        nb = sb("nb", [P, 2, 4])
        rs = sb("rs", [P, 2, 4])
        ri = sb("ri", [P, 2, 4])
        pr = sb("pr", [P, 2, 4, 2 * P])
        prT = sb("prT", [P, 2, 4 * 2, P])
        lnw = sb("lnw", [P, G])
        rsw = sb("rsw", [P, G])
        act_g = sb("act_g", [P, 2, G])
        hid = sb("hid", [P, 3, G])
        fo = sb("fo", [P, ST, DC, G])
        if last_layer:
            x1 = sb("x1", [P, ST, DC, G])
            rows = sb("rows", [P, TPG, D])

        pj = ps("pj", [P, 2, G])
        sc = ps("sc", [P, 2, G])
        pt = ps("pt", [P, 2, G])
        tp = ps("tp", [P, G])
        ov = ps("ov", [P, G])
        HIDDEN_BANKS = [(sc[:, 0, :], sc[:, 1, :]), (pt[:, 0, :], pt[:, 1, :]), (tp[:, :], ov[:, :])]

        names = ("w_in t_in zeroed bands tab_set tabq proj_done qkv_set sq_done ss_done ln_done rr_done newton rn_done q8_done rot_cos rot_done "
                 "sum_done kn_done turn_done turn_set s_done mx_done nb_done exp_done rcp_done pn_done pt_done ptA ptB pv_done "
                 "o_set wo_done x2_halo x2_done mean_done xc_done sqm_done var_done lnw_done rsw_done hn_done h2_done "
                 "ag_done gelu_done hid_done w2_done y_used x3_done fin_done rows_set").split()
        s = {name: sem(name) for name in names}
        x_in = [sem(f"x_in{st}") for st in range(ST)]
        x1_in = [sem(f"x1_in{st}") for st in range(ST)]
        x_halo = [sem(f"x_halo{st}") for st in range(ST)]
        stored = [sem(f"stored{st}") for st in range(ST)]
        block = own.enter_context(nc.Block())
        ZEROED = 11

        @block.sync
        def _(sp):
            sp.wait_ge(s["zeroed"], ZEROED)
            with sp.Fori(0, STEPS) as i:
                for st in range(ST):
                    sp.wait_ge(x_halo[st], i)
                    sp.dma_start(xin[:, st, :, 1:], source[bass.ds(i + st * STEPS, 1)].rearrange("a p (c n) -> (a p) c n", c=DC)).then_inc(x_in[st], 16)
                if last_layer:
                    sp.wait_ge(s["x3_done"], i * ST)
                    for st in range(ST):
                        sp.dma_start(x1[:, st, :, :], dram["x1"][bass.ds(i + st * STEPS, 1)].rearrange("a p (c n) -> (a p) c n", c=DC)).then_inc(x1_in[st], 16)

        @block.gpsimd
        def _(pool):
            z = s["zeroed"]
            nc.gpsimd.memset(w1[:, :, :, HID:], 0.0).then_inc(z, 1)
            nc.gpsimd.memset(w2[:, HC - 1, :], 0.0).then_inc(z, 1)
            nc.gpsimd.memset(qz[:, :, :, :], 0.0).then_inc(z, 1)
            nc.gpsimd.memset(xin[:, :, :, 0:1], 0.0).then_inc(z, 1)
            nc.gpsimd.memset(x2[:, :, :, :], 0.0).then_inc(z, 1)
            nc.gpsimd.memset(kT[:, :, :, TPG - 1, :], 0.0).then_inc(z, 1)
            nc.gpsimd.memset(v[:, :, TPG - 1, :], 0.0).then_inc(z, 1)
            nc.gpsimd.memset(band[:, :, :, :], 0.0).then_inc(z, 1)
            nc.gpsimd.memset(band0[:, 1:, :, :, :], 0.0).then_inc(z, 1)
            nc.gpsimd.memset(band0[:, 0, :, 0, :], 0.0).then_inc(z, 1)
            nc.gpsimd.memset(band0[:, 0, :, 1, :], BLOCKED).then_inc(z, 1)
            pool.wait_ge(z, ZEROED)
            for view, pattern, cm in ((band[:, :, 0, :], [[0, 2], [1, P]], -1), (band[:, :, 1, :], [[0, 2], [-1, P]], 1),
                                      (band0[:, :, :, 0, :], [[0, GPB], [0, 2], [-1, P]], 1),
                                      (band0[:, 1:, :, 1, :], [[0, GPB - 1], [0, 2], [1, P]], -1)):
                nc.gpsimd.affine_select(out=view, in_=view, compare_op=ALU.is_ge, fill=BLOCKED, base=0,
                                        pattern=pattern, channel_multiplier=cm).then_inc(s["bands"], 1)
            pool.wait_ge(s["w_in"], W_LOADS * 16)
            for j in range(4):
                nc.gpsimd.tensor_tensor(tab[:, :, j, :], tab[:, :, j, :], qks[:, j, :].unsqueeze(1).to_broadcast([P, S // P, DH]), ALU.mult).then_inc(s["tab_set"], 1)
            with pool.Fori(0, STEPS) as i:
                def rotate(k):
                    u, r = i * UNITS + k, k % 2
                    pool.wait_ge(s["rot_done"], u * 2 + 2)
                    a, b = rot[:, 0, :, :, :], rot[:, 1, :, :, :]
                    nc.gpsimd.tensor_tensor(a, a, b, ALU.add).then_inc(s["sum_done"], 1)

                def norm_k(k):
                    u, r = i * UNITS + k, k % 2
                    pool.wait_ge(s["sum_done"], u + 1)
                    pool.wait_ge(s["rn_done"], u + 1)
                    kk = rot[:, 0, 1, :, :]
                    nc.gpsimd.tensor_tensor(kk, kk, rr[:, r, H:].unsqueeze(2).to_broadcast([P, H, DH]), ALU.mult).then_inc(s["kn_done"], 1)

                def norm_p(k, h):
                    u = i * UNITS + k
                    pool.wait_ge(s["rcp_done"], u * 2 + h + 1)
                    w = pr[:, h, :, :]
                    nc.gpsimd.tensor_tensor(w, w, ri[:, h, :].unsqueeze(2).to_broadcast([P, 4, 2 * P]), ALU.mult).then_inc(s["pn_done"], 1)

                rotate(0)
                norm_k(0)
                for k in range(UNITS):
                    norm_p(k, 0)
                    if k + 1 < UNITS:
                        rotate(k + 1)
                    norm_p(k, 1)
                    if k + 1 < UNITS:
                        norm_k(k + 1)

        @block.scalar
        def _(act):
            fl = lambda t: t.rearrange("(c p) n -> p c n", p=P)
            put = lambda dst, src: act.dma_start(dst, src).then_inc(s["w_in"], 16)
            put(tab[:, :, :, :], dram["tab"])
            put(qks[:, :, :], dram["qks"][layer:layer + 1].to_broadcast([P, 4, DH]))
            put(wqkv[:, :, :], fl(dram["wqkv"][layer]))
            put(wo[:, :, :], fl(dram["wo"][layer]))
            act.wait_ge(s["zeroed"], ZEROED)
            for j in range(2):
                put(w1[:, :, j, 0:HID], fl(dram["w1"][layer][:, j * HID:(j + 1) * HID]))
            put(w2[:, 0:HC - 1, :], fl(dram["w2"][layer][0:(HC - 1) * P, :]))
            put(w2[0:TAIL, HC - 1, :], dram["w2"][layer][(HC - 1) * P:HID, :])
            put(col[:, :], dram["cols"][layer])
            act.wait_ge(s["w_in"], W_LOADS * 16)
            with act.Fori(0, STEPS) as i:
                def take(k, j):
                    u, r, st, w = i * UNITS + k, k % 2, k % ST, k // ST
                    act.wait_ge(s["proj_done"], u * 3 + j + 1)
                    if j < 2:
                        if k >= 2:
                            act.wait_ge(s["rot_done"], u * 2 - 2)
                        dst = qk[:, r, j, :, :].rearrange("p h d -> p (h d)")
                    else:
                        if k >= 3:
                            act.wait_ge(s["pv_done"], u * 2 - 4)
                        dst = v[:, st, w, :]
                    nc.scalar.activation(dst, pj[:, (3 * k + j) % 2, :], ACT.Copy).then_inc(s["qkv_set"], 1)

                def squares(k):
                    u, r = i * UNITS + k, k % 2
                    act.wait_ge(s["qkv_set"], u * 3 + 2)
                    act.wait_ge(s["ss_done"], u)
                    nc.scalar.activation(sq[:, :], qk[:, r].rearrange("p j h d -> p (j h d)"), ACT.Square).then_inc(s["sq_done"], 1)

                def inverse_norms(k):
                    u, r = i * UNITS + k, k % 2
                    act.wait_ge(s["ss_done"], u + 1)
                    nc.scalar.activation(lss[:, :], ss[:, r, :], ACT.Ln, scale=float(2 ** 20)).then_inc(s["ln_done"], 1)
                    act.wait_ge(s["ln_done"], u + 1)
                    nc.scalar.activation(rg[:, :], lss[:, :], ACT.Exp, scale=-0.5, bias=keep["ln2x10"][:, 0:1]).then_inc(s["rr_done"], 1)

                def weights(k, h):
                    u, r = i * UNITS + k, k % 2
                    act.wait_ge(s["nb_done"], u * 2 + h + 1)
                    if k >= 1:
                        act.wait_ge(s["pt_done"], u * 2 + h - 1)
                    for d in range(4):
                        e = nc.scalar.activation(pr[:, h, d, :], sc[:, d // 2, (d % 2) * 2 * P:(d % 2 + 1) * 2 * P], ACT.Exp,
                                                 scale=q8[:, r, 4 * h + d:4 * h + d + 1], bias=nb[:, h, d:d + 1],
                                                 accum_out=rs[:, h, d:d + 1])
                    e.then_inc(s["exp_done"], 1)

                def take_pt(k, h):
                    u = i * UNITS + k
                    act.wait_ge(s["pt_done"], u * 2 + h + 1)
                    nc.scalar.activation(prT[:, h, 0:4, :].rearrange("p a q -> p (a q)"), pt[:, 0, :], ACT.Copy).then_inc(s["ptA"], 1)

                nc.scalar.preload_act_table_set("natural_log_exp_and_others")
                take(0, 0)
                take(0, 1)
                squares(0)
                take(0, 2)
                inverse_norms(0)
                for k in range(UNITS):
                    weights(k, 0)
                    if k >= 1:
                        take_pt(k - 1, 1)
                    if k + 1 < UNITS:
                        take(k + 1, 0)
                        take(k + 1, 1)
                        squares(k + 1)
                    weights(k, 1)
                    take_pt(k, 0)
                    if k + 1 < UNITS:
                        take(k + 1, 2)
                        inverse_norms(k + 1)
                take_pt(UNITS - 1, 1)

                for st in range(ST):
                    n = i * ST + st
                    act.wait_ge(s["xc_done"], n + 1)
                    nc.scalar.activation(attn[:, st, 2:4, :], attn[:, st, 0:2, :], ACT.Square).then_inc(s["sqm_done"], 1)
                for st in range(ST):
                    n = i * ST + st
                    act.wait_ge(s["var_done"], n + 1)
                    nc.scalar.activation(lnw[:, :], (tp, ov)[st][:, :], ACT.Ln, bias=eps[:, 0:1]).then_inc(s["lnw_done"], 1)
                    act.wait_ge(s["lnw_done"], n + 1)
                    act.wait_ge(s["hn_done"], n)
                    nc.scalar.activation(rsw[:, :], lnw[:, :], ACT.Exp, scale=-0.5).then_inc(s["rsw_done"], 1)
                    act.wait_ge(s["hn_done"], n + 1)
                    for c in range(DC):
                        nc.scalar.activation(attn[:, st, 2 + c, :], attn[:, st, c, :], ACT.Identity,
                                             scale=col[:, LG + c:LG + c + 1], bias=col[:, LB + c:LB + c + 1]).then_inc(s["h2_done"], 1)
                for st in range(ST):
                    n = i * ST + st
                    for c in range(HC):
                        m = n * HC + c
                        act.wait_ge(s["ag_done"], m + 1)
                        if st > 0 or c >= 2:
                            act.wait_ge(s["hid_done"], m - 1)
                        nc.scalar.activation(act_g[:, c % 2, :], HIDDEN_BANKS[c % 3][1], ACT.Gelu, bias=col[:, B1G + c:B1G + c + 1]).then_inc(s["gelu_done"], 1)
                if not last_layer:
                    for st in range(ST):
                        act.wait_ge(s["y_used"], i * ST + st + 1)
                        act.dma_start(dram["mid"][bass.ds(i + st * STEPS, 1)].rearrange("a p (c n) -> (a p) c n", c=DC), fo[:, st, :, :]).then_inc(stored[st], 16)
                if last_layer:
                    for st in range(ST):
                        n = i * ST + st
                        act.wait_ge(s["fin_done"], n + 1)
                        act.wait_ge(stored[0], n * 16)
                        for j in range(2):
                            nc.scalar.activation(rows[:, 2 * j:2 * j + 2, :].rearrange("p t d -> p (t d)"), (sc, pt)[st][:, j, :], ACT.Copy).then_inc(s["rows_set"], 1)
                        act.wait_ge(s["rows_set"], (n + 1) * 2)
                        act.dma_start(dram["out"][bass.ds(i + st * STEPS, 1)].rearrange("a (t p) d -> p (a t) d", p=P), rows[:, :, :]).then_inc(stored[0], 16)
            for st in range(ST):
                if st == 0 or not last_layer:
                    act.wait_ge(stored[st], STEPS * (ST if last_layer else 1) * 16)

        @block.tensor
        def _(pe):
            pe.wait_ge(s["w_in"], W_LOADS * 16)
            pe.wait_ge(s["zeroed"], ZEROED)
            pe.wait_ge(s["bands"], 4)
            with pe.Fori(0, STEPS) as i:
                def project(k, js):
                    u, st, w = i * UNITS + k, k % ST, k // ST
                    if w == 0:
                        pe.wait_ge(x_in[st], i * 16 + 16)
                    for j in js:
                        if k > 0 or j == 2:
                            pe.wait_ge(s["qkv_set"], u * 3 + j - 1)
                        for c in range(DC):
                            o = 1 + w * P - c
                            mm = nc.tensor.matmul(pj[:, (3 * k + j) % 2, :], xin[:, st, c, o:o + P], wqkv[:, c, j * INNER:(j + 1) * INNER],
                                                  start=(c == 0), stop=(c == DC - 1))
                        mm.then_inc(s["proj_done"], 1)

                def turn_qk(k):
                    u = i * UNITS + k
                    for j in range(2):
                        if j == 0:
                            pe.wait_ge(s["sum_done"], u + 1)
                            if k > 0:
                                pe.wait_ge(s["turn_set"], u * 3)
                        else:
                            pe.wait_ge(s["kn_done"], u + 1)
                            pe.wait_ge(s["turn_set"], u * 3 + 2)
                        for c in range(PAIRS):
                            mm = nc.tensor.transpose(tp[:, c * P:(c + 1) * P], rot[:, 0, j, 2 * c:2 * c + 2, :].rearrange("p h d -> p (h d)"), ident[:, :])
                        mm.then_inc(s["turn_done"], 1)

                def scores(k, h):
                    u, r, st, w = i * UNITS + k, k % 2, k % ST, k // ST
                    if h == 0:
                        pe.wait_ge(s["turn_set"], u * 3 + 3)
                    if k > 0 or h > 0:
                        pe.wait_ge(s["exp_done"], u * 2 + h)
                    for b in range(2):
                        mask = band[:, :, :, :] if w > 0 else band0[:, bass.ds(i % GPB, 1), :, :, :]
                        mask = mask.rearrange("p a b q -> p (a b q)") if w > 0 else mask.rearrange("p g a b q -> p (g a b q)")
                        nc.tensor.matmul(sc[:, b, :], identb[:, :], mask, start=True, stop=False)
                        for d in range(2):
                            hd = 4 * h + 2 * b + d
                            keys = kT[:, st, hd // 2, w - 1:w + 1, :] if w > 0 else kT[:, st, hd // 2, 0:TPG:TPG - 1, :]
                            mm = nc.tensor.matmul(sc[:, b, d * 2 * P:(d + 1) * 2 * P], qz[:, r, hd, :], keys, start=False, stop=(d == 1))
                    mm.then_inc(s["s_done"], 1)

                def turn_p(k, h):
                    u = i * UNITS + k
                    pe.wait_ge(s["pn_done"], u * 2 + h + 1)
                    if k > 0 or h > 0:
                        pe.wait_ge(s["ptA"], u * 2 + h)
                        pe.wait_ge(s["ptB"], u * 2 + h)
                    for a in range(8):
                        mm = nc.tensor.transpose(pt[:, a // 4, (a % 4) * P:(a % 4 + 1) * P], pr[:, h, a // 2, (a % 2) * P:(a % 2 + 1) * P], ident[:, :])
                    mm.then_inc(s["pt_done"], 1)

                def values(k, h):
                    u, st, w = i * UNITS + k, k % ST, k // ST
                    pe.wait_ge(s["ptA"], u * 2 + h + 1)
                    pe.wait_ge(s["ptB"], u * 2 + h + 1)
                    if h == 0 and k > 0:
                        pe.wait_ge(s["o_set"], u)
                    if h == 0:
                        pe.wait_ge(s["qkv_set"], u * 3 + 3)
                    slots = (w - 1, w) if w > 0 else (0, TPG - 1)
                    for c in range(2):
                        pair = 2 * h + c
                        for blk in range(2):
                            for e in range(2):
                                mm = nc.tensor.matmul(ov[e * DH:(e + 1) * DH, pair * P:(pair + 1) * P],
                                                      v[:, st, slots[blk], (2 * pair + e) * DH:(2 * pair + e + 1) * DH],
                                                      prT[:, h, (2 * c + e) * 2 + blk, :], start=(blk == 0), stop=(blk == 1))
                    mm.then_inc(s["pv_done"], 1)

                if True:
                    pe.wait_ge(s["y_used"], i * ST)
                    if last_layer:
                        pe.wait_ge(s["rows_set"], i * ST * 2)
                project(0, (0, 1, 2))
                turn_qk(0)
                for k in range(UNITS):
                    scores(k, 0)
                    if k > 0:
                        turn_p(k - 1, 1)
                    if k + 1 < UNITS:
                        project(k + 1, (0, 1))
                    if k > 0:
                        values(k - 1, 1)
                    scores(k, 1)
                    turn_p(k, 0)
                    if k + 1 < UNITS:
                        project(k + 1, (2,))
                    values(k, 0)
                    if k + 1 < UNITS:
                        turn_qk(k + 1)
                turn_p(UNITS - 1, 1)
                values(UNITS - 1, 1)

                for st in range(ST):
                    if st == 0:
                        pe.wait_ge(s["o_set"], (i + 1) * UNITS)
                        pe.wait_ge(s["qkv_set"], (i + 1) * UNITS * 3)
                    for m in range(DC):
                        for c in range(PAIRS):
                            mm = nc.tensor.matmul((pj, sc)[st][:, m, :], wo[:, c, m * P:(m + 1) * P], attn[:, st, c, :],
                                                  start=(c == 0), stop=(c == PAIRS - 1))
                    mm.then_inc(s["wo_done"], 1)
                for st in range(ST):
                    pe.wait_ge(s["x2_done"], i * ST + st + 1)
                    for c in range(DC):
                        mm = nc.tensor.matmul(pt[:, st, :], mean_w[:, :], x2[:, st, c, 1 - c:1 - c + G], start=(c == 0), stop=(c == DC - 1))
                    mm.then_inc(s["mean_done"], 1)
                for st in range(ST):
                    pe.wait_ge(s["sqm_done"], i * ST + st + 1)
                    for c in range(DC):
                        mm = nc.tensor.matmul((tp, ov)[st][:, :], mean_w[:, :], attn[:, st, 2 + c, :], start=(c == 0), stop=(c == DC - 1))
                    mm.then_inc(s["var_done"], 1)
                for st in range(ST):
                    n = i * ST + st
                    pe.wait_ge(s["h2_done"], (n + 1) * DC)
                    if st == 0:
                        pe.wait_ge(s["xc_done"], (i + 1) * ST)
                        pe.wait_ge(s["rsw_done"], (i + 1) * ST)

                    def down(c):
                        pe.wait_ge(s["hid_done"], n * HC + c + 1)
                        if c == 0 and st > 0:
                            pe.wait_ge(s["y_used"], n)
                        for m in range(DC):
                            mm = nc.tensor.matmul(pj[:, m, :], w2[:, c, m * P:(m + 1) * P], hid[:, c % 3, :], start=(c == 0), stop=(c == HC - 1))
                        mm.then_inc(s["w2_done"], 1)

                    for c in range(HC):
                        if st > 0 or c >= 3:
                            pe.wait_ge(s["hid_done"], n * HC + c - 2)
                        for j in range(2):
                            for d in range(DC):
                                mm = nc.tensor.matmul(HIDDEN_BANKS[c % 3][j], w1[:, d, j, c * P:(c + 1) * P], attn[:, st, 2 + d, :], start=(d == 0), stop=(d == DC - 1))
                        mm.then_inc(s["ag_done"], 1)
                        if c >= 2:
                            down(c - 2)
                    down(HC - 2)
                    down(HC - 1)
                if last_layer:
                    for st in range(ST):
                        n = i * ST + st
                        pe.wait_ge(s["x3_done"], n + 1)
                        if st == 0:
                            pe.wait_ge(s["hid_done"], (i + 1) * ST * HC)
                        for t in range(TPG):
                            for c in range(DC):
                                mm = nc.tensor.transpose((sc, pt)[st][:, t // 2, (t % 2) * D + c * P:(t % 2) * D + (c + 1) * P], fo[:, st, c, t * P:(t + 1) * P], ident[:, :])
                        mm.then_inc(s["fin_done"], 1)

        @block.vector
        def _(dve):
            dve.wait_ge(s["w_in"], W_LOADS * 16)
            dve.wait_ge(s["tab_set"], 4)
            dve.wait_ge(s["zeroed"], ZEROED)
            with dve.Fori(0, STEPS) as i:
                def rotate(k):
                    u, r, w = i * UNITS + k, k % 2, k // ST
                    dve.wait_ge(s["qkv_set"], u * 3 + 2)
                    if k > 0:
                        dve.wait_ge(s["turn_done"], u * 2)
                    t = tab[:, bass.ds((i % GPB) * TPG + w, 1), :, :].rearrange("p a j d -> p (a j) d")
                    nc.vector.tensor_tensor(rot[:, 0, :, :, :], qk[:, r], t[:, 0:2, :].unsqueeze(2).to_broadcast([P, 2, H, DH]), ALU.mult).then_inc(s["rot_done"], 1)
                    hw = DH // 2
                    for e in range(2):
                        m = nc.vector.tensor_tensor(rot[:, 1, :, :, e * hw:(e + 1) * hw], qk[:, r, :, :, (1 - e) * hw:(2 - e) * hw],
                                                    t[:, 2:4, e * hw:(e + 1) * hw].unsqueeze(2).to_broadcast([P, 2, H, hw]), ALU.mult)
                    m.then_inc(s["rot_done"], 1)

                def sums(k):
                    u, r = i * UNITS + k, k % 2
                    dve.wait_ge(s["sq_done"], u + 1)
                    nc.vector.tensor_reduce(ss[:, r, :], sq[:, :].rearrange("p (h d) -> p h d", d=DH), AXX, ALU.add).then_inc(s["mx_done"], 1)
                    dve.wait_ge(s["mx_done"], u * 3 + 1)
                    nc.vector.tensor_scalar(ss[:, r, :], ss[:, r, :], 1e-24, None, ALU.max).then_inc(s["ss_done"], 1)

                def scale_q(k):
                    u, r = i * UNITS + k, k % 2
                    dve.wait_ge(s["rr_done"], u + 1)
                    nc.vector.tensor_tensor(nt[:, :], rg[:, :], rg[:, :], ALU.mult).then_inc(s["newton"], 1)
                    dve.wait_ge(s["newton"], u * 2 + 1)
                    nc.vector.scalar_tensor_tensor(out=nt[:, :], in0=nt[:, :], scalar=-0.5, in1=ss[:, r, :], op0=ALU.mult, op1=ALU.mult).then_inc(s["newton"], 1)
                    dve.wait_ge(s["newton"], u * 2 + 2)
                    nc.vector.scalar_tensor_tensor(out=rr[:, r, :], in0=nt[:, :], scalar=1.5, in1=rg[:, :], op0=ALU.add, op1=ALU.mult).then_inc(s["rn_done"], 1)
                    dve.wait_ge(s["rn_done"], u + 1)
                    nc.vector.tensor_scalar(q8[:, r, :], rr[:, r, 0:H], QK_SCALE, None, ALU.mult).then_inc(s["q8_done"], 1)

                def take_qk(k):
                    u, r, st, w = i * UNITS + k, k % 2, k % ST, k // ST
                    dve.wait_ge(s["turn_done"], u * 2 + 1)
                    for e in range(2):
                        rows_ = slice(e * DH, (e + 1) * DH)
                        nc.vector.tensor_copy(qz[rows_, r, e::2, :], tp[rows_, :].rearrange("p (a q) -> p a q", q=P)).then_inc(s["turn_set"], 1)
                    dve.wait_ge(s["turn_done"], u * 2 + 2)
                    nc.vector.tensor_copy(kT[:, st, :, w, :], tp[:, :].rearrange("p (a q) -> p a q", q=P)).then_inc(s["turn_set"], 1)

                def maxima(k, h):
                    u, r = i * UNITS + k, k % 2
                    dve.wait_ge(s["s_done"], u * 2 + h + 1)
                    nc.vector.tensor_reduce(mx[:, :], sc[:, :, :].rearrange("p b (d j) -> p (b d) j", j=2 * P), AXX, ALU.max).then_inc(s["mx_done"], 1)
                    dve.wait_ge(s["mx_done"], u * 3 + 2 + h)
                    dve.wait_ge(s["q8_done"], u + 1)
                    nc.vector.scalar_tensor_tensor(out=nb[:, h, :], in0=mx[:, :], scalar=-1.0, in1=q8[:, r, 4 * h:4 * h + 4],
                                                   op0=ALU.mult, op1=ALU.mult).then_inc(s["nb_done"], 1)

                def inverse_sums(k, h):
                    u = i * UNITS + k
                    dve.wait_ge(s["exp_done"], u * 2 + h + 1)
                    nc.vector.reciprocal(ri[:, h, :], rs[:, h, :]).then_inc(s["rcp_done"], 1)

                def take_pt(k, h):
                    u = i * UNITS + k
                    dve.wait_ge(s["pt_done"], u * 2 + h + 1)
                    nc.vector.tensor_copy(prT[:, h, 4:8, :].rearrange("p a q -> p (a q)"), pt[:, 1, :]).then_inc(s["ptB"], 1)

                def take_o(k):
                    u, st, w = i * UNITS + k, k % ST, k // ST
                    dve.wait_ge(s["pv_done"], u * 2 + 2)
                    nc.vector.tensor_copy(attn[:, st, :, w * P:(w + 1) * P], ov[:, :].rearrange("p (a q) -> p a q", q=P)).then_inc(s["o_set"], 1)

                rotate(0)
                sums(0)
                scale_q(0)
                take_qk(0)
                for k in range(UNITS):
                    maxima(k, 0)
                    if k > 0:
                        take_pt(k - 1, 1)
                    inverse_sums(k, 0)
                    if k + 1 < UNITS:
                        rotate(k + 1)
                    maxima(k, 1)
                    if k > 0:
                        take_o(k - 1)
                    take_pt(k, 0)
                    if k + 1 < UNITS:
                        sums(k + 1)
                    inverse_sums(k, 1)
                    if k + 1 < UNITS:
                        scale_q(k + 1)
                        take_qk(k + 1)
                take_pt(UNITS - 1, 1)
                take_o(UNITS - 1)

                for st in range(ST):
                    n = i * ST + st
                    here = flags[:, bass.ds(i % GPB, 1)]
                    nxt = flags[:, bass.ds((i + 1) % GPB, 1)]
                    nc.vector.tensor_scalar(x2[:, st, 1, 0:1], x2[:, st, 1, G:G + 1], here, None, ALU.mult).then_inc(s["x2_halo"], 1)
                    dve.wait_ge(s["x2_halo"], n + 1)
                    dve.wait_ge(s["wo_done"], n + 1)
                    nc.vector.tensor_tensor(x2[:, st, :, 1:], xin[:, st, :, 1:], (pj, sc)[st][:, :, :], ALU.add).then_inc(s["x2_done"], 1)
                    dve.wait_ge(s["x2_done"], n + 1)
                    nc.vector.tensor_scalar(xin[:, st, 1, 0:1], xin[:, st, 1, G:G + 1], nxt, None, ALU.mult).then_inc(x_halo[st], 1)
                for st in range(ST):
                    n = i * ST + st
                    dve.wait_ge(s["mean_done"], n + 1)
                    for c in range(DC):
                        m = nc.vector.tensor_tensor(attn[:, st, c, :], x2[:, st, c, 1 - c:1 - c + G], pt[:, st, :], ALU.subtract)
                    m.then_inc(s["xc_done"], 1)
                for st in range(ST):
                    n = i * ST + st
                    dve.wait_ge(s["rsw_done"], n + 1)
                    nc.vector.tensor_tensor(attn[:, st, 0:2, :], attn[:, st, 0:2, :], rsw[:, :].unsqueeze(1).to_broadcast([P, DC, G]), ALU.mult).then_inc(s["hn_done"], 1)
                for st in range(ST):
                    n = i * ST + st
                    for c in range(HC):
                        m = n * HC + c
                        dve.wait_ge(s["gelu_done"], m + 1)
                        if st > 0 or c >= 3:
                            dve.wait_ge(s["w2_done"], m - 2)
                        nc.vector.scalar_tensor_tensor(out=hid[:, c % 3, :], in0=HIDDEN_BANKS[c % 3][0], scalar=col[:, B1A + c:B1A + c + 1],
                                                       in1=act_g[:, c % 2, :], op0=ALU.add, op1=ALU.mult).then_inc(s["hid_done"], 1)
                    dve.wait_ge(s["w2_done"], (n + 1) * HC)
                    if not last_layer:
                        dve.wait_ge(stored[st], i * 16)
                    else:
                        dve.wait_ge(s["fin_done"], i * ST)
                    for c in range(DC):
                        m = nc.vector.scalar_tensor_tensor(out=fo[:, st, c, :], in0=pj[:, c, :], scalar=col[:, B2 + c:B2 + c + 1],
                                                           in1=x2[:, st, c, 1:], op0=ALU.add, op1=ALU.add)
                    m.then_inc(s["y_used"], 1)
                    dve.wait_ge(s["y_used"], n + 1)
                    if last_layer:
                        dve.wait_ge(x1_in[st], i * 16 + 16)
                        for c in range(DC):
                            m = nc.vector.scalar_tensor_tensor(out=fo[:, st, c, :], in0=fo[:, st, c, :], scalar=gbg[:, bass.ds(i + st * STEPS, 1), c],
                                                               in1=x1[:, st, c, :], op0=ALU.mult, op1=ALU.add)
                        m.then_inc(s["x3_done"], 1)


PHASE_A = ("c", "wmod", "acol", "Wq", "Wk", "Wv", "Wo", "bk", "bv", "x")


def persistent(nc, ctx):
    sb = lambda name, shape, dt=F32: ctx.enter_context(nc.sbuf_tensor(name, shape, dt))
    return {
        "modv": sb("modv", [P, MODS * DC + DC, B]),
        "gbg": sb("gbg", [P, NG, DC]),
        "acol": sb("acol", [P, 2 * DC]),
        "ident": sb("ident", [P, P]),
        "identb": sb("identb", [P, P], BF16),
        "blocks": sb("blocks", [P, P]),
        "flags": sb("flags", [P, GPB]),
        "eps": sb("eps", [P, 1]),
        "mean_w": sb("mean_w", [P, P]),
        "ln2x10": sb("ln2x10", [P, 1]),
    }


def layout(inputs):
    import numpy as np

    a = {k.replace("L0_attn_", "").replace("L0_", ""): np.ascontiguousarray(v) for k, v in inputs.items()}
    cols = lambda v: v.reshape(-1, P).T
    out = {n: a[n] for n in ("Wq", "Wk", "Wv", "Wo", "bk", "bv", "wmod")}
    out["x"] = a["inputs_q"]
    out["c"] = np.ascontiguousarray(a["c"].reshape(B, DC, P).transpose(2, 1, 0))
    out["acol"] = np.ascontiguousarray(np.concatenate([cols(a["bq"]), cols(a["bo"])], axis=1))
    L = {k.replace("L0_ffn_", ""): np.ascontiguousarray(v) for k, v in inputs.items() if k.startswith("L0_ffn_")}
    for n in ("wqkv", "w1", "w2"):
        out[n] = L[n]
    out["wo"] = L["wo"]
    depth = L["w2"].shape[0]
    half = lambda v: np.concatenate([v[:, DH // 2:], v[:, :DH // 2]], axis=1)
    out["qks"] = np.ascontiguousarray(np.stack([L["q_scale"], L["k_scale"], half(L["q_scale"]), half(L["k_scale"])], axis=1))
    pad = lambda v: np.concatenate([v, np.zeros(HC * P - HID, np.float32)])
    out["cols"] = np.ascontiguousarray(np.stack([np.concatenate(
        [cols(L["ln_g"][l]), cols(L["ln_b"][l]), cols(pad(L["b1"][l][:HID])), cols(pad(L["b1"][l][HID:])), cols(L["b2"][l])], axis=1)
        for l in range(depth)]))
    out["tab"] = rotation_table()
    return out


def rotation_table():
    import numpy as np

    f = np.float32
    half_idx = np.arange(0, DH, 2, dtype=f)
    inv_freq = (f(1.0) / f(10000.0) ** (half_idx / f(DH))).astype(f)
    t = np.arange(S, dtype=f)
    freqs = t[:, None] * inv_freq[None, :]
    base = (half_idx + f(0.4 * DH)) / f(1.4 * DH)
    scale = (base[None, :] ** ((t - f(S // 2)) / f(P // 2))[:, None]).astype(f)
    cos, sin = np.cos(freqs).astype(f), np.sin(freqs).astype(f)
    two = lambda a, b: np.concatenate([a, b], axis=1)
    t4 = np.stack([two(cos * scale, cos * scale), two(cos / scale, cos / scale),
                   two(-sin * scale, sin * scale), two(-sin / scale, sin / scale)], axis=1)
    return np.ascontiguousarray(t4.reshape(S // P, P, 4, DH).transpose(1, 0, 2, 3).astype(f))


def build_program(nc, arrays, out):
    dram = dict(arrays)
    dram["out"] = out.rearrange("b (g t) d -> (b g) t d", t=G)
    for name in ("x1", "h0", "mid"):
        dram[name] = nc.dram_tensor(name + "_dram", (NG, P, DC * G), F32, kind="Internal").ap()
    with ExitStack() as ctx:
        keep = persistent(nc, ctx)
        setup_program(nc, ctx, dram, keep)
        linear_attention_program(nc, ctx, dram, keep)
        layer_program(nc, ctx, 0, dram, keep)
        layer_program(nc, ctx, 1, dram, keep)


def kernel(**inputs):
    import numpy as np
    import concourse.bacc as bacc
    from concourse.bass_utils import run_bass_kernel_spmd

    nc = bacc.Bacc("TRN2", target_bir_lowering=False, num_devices=1)
    arrays = layout({k: np.asarray(v) for k, v in inputs.items()})
    aps = {name: nc.dram_tensor(f"in_{name}_dram", a.shape, mybir.dt.from_np(a.dtype), kind="ExternalInput").ap()
           for name, a in arrays.items()}
    out = nc.dram_tensor("out_dram", (B, S, D), F32, kind="ExternalOutput").ap()
    build_program(nc, aps, out)
    r = run_bass_kernel_spmd(nc, [{f"in_{name}_dram": a for name, a in arrays.items()}], core_ids=[0])
    return r.results[0]["out_dram"]
```

```python
from contextlib import ExitStack, contextmanager

import concourse.bass as bass
from concourse import mybir

ALU = mybir.AluOpType
ACT = mybir.ActivationFunctionType
AXX = mybir.AxisListType.X
F32 = mybir.dt.float32
F32R = mybir.dt.float32r
BF16 = mybir.dt.bfloat16

P = 128
B, S, D = 4, 2048, 256
DC = D // P
G = 512
TPG = G // P
GPB = S // G
NG = B * GPB
ST = 2
STEPS = NG // ST
H, DH = 8, 64
INNER = H * DH
PAIRS = H // 2
HID = int(D * 4 * 2 / 3)
HC = -(-HID // P)
TAIL = HID - (HC - 1) * P
AH, AD = 16, 16
QK_SCALE = 8.0
BLOCKED = -1.0e30
MODS = 6
LG, LB, B1A, B1G, B2 = 0, DC, 2 * DC, 2 * DC + HC, 2 * DC + 2 * HC
NCOL = B2 + DC


@contextmanager
def cleared_semaphores(nc):
    taken = []

    def take(name):
        taken.append(nc.alloc_semaphore(name=name))
        return taken[-1]

    yield take
    nc.clear_and_free_semaphores(taken)
    nc.all_engine_barrier()


def setup_program(nc, ctx, dram, keep):
    with ExitStack() as own:
        sb = lambda name, shape, dt=F32: own.enter_context(nc.sbuf_tensor(name, shape, dt))
        ps = lambda name, shape: own.enter_context(nc.psum_tensor(name, shape, F32))
        used = own.enter_context(cleared_semaphores(nc))
        sem = lambda name: used(name)
        wmod = sb("wmod", [P, DC, MODS * D])
        c_in = sb("c_in", [P, DC, B])
        c_act = sb("c_act", [P, DC, B])
        sign = sb("sign", [P, DC, B])
        c_rep = sb("c_rep", [P, DC, B, P])
        row_sign = sb("row_sign", [P, B, D])
        mod_ps = ps("mod_ps", [P, MODS * DC, B])
        row_ps = ps("row_ps", [P, B, D])
        loaded, zeroed, selected = sem("loaded"), sem("zeroed"), sem("selected")
        silu_done, rep_done, mod_ready, mod_step = sem("silu_done"), sem("rep_done"), sem("mod_ready"), sem("mod_step")
        modv, ident, identb, blocks = keep["modv"], keep["ident"], keep["identb"], keep["blocks"]
        block = own.enter_context(nc.Block())

        @block.sync
        def _(sp):
            sp.dma_start(c_in[:, :, :], dram["c"]).then_inc(loaded, 16)
            sp.dma_start(wmod[:, :, :], dram["wmod"].rearrange("(c p) n -> p c n", p=P)).then_inc(loaded, 16)
            sp.dma_start(keep["acol"][:, :], dram["acol"]).then_inc(loaded, 16)
            sp.wait_ge(loaded, 48)

        @block.gpsimd
        def _(pool):
            nc.gpsimd.memset(ident[:, :], 0.0).then_inc(zeroed, 1)
            nc.gpsimd.memset(identb[:, :], 0.0).then_inc(zeroed, 1)
            nc.gpsimd.memset(blocks[:, :], 1.0).then_inc(zeroed, 1)
            nc.gpsimd.memset(keep["flags"][:, :], 1.0).then_inc(zeroed, 1)
            pool.wait_ge(zeroed, 4)
            for m in (ident, identb):
                nc.gpsimd.affine_select(out=m[:, :], in_=m[:, :], compare_op=ALU.not_equal, fill=1.0,
                                        base=0, pattern=[[-1, P]], channel_multiplier=1).then_inc(selected, 1)
            view = blocks[:, :].rearrange("p (h d) -> p h d", d=AD)
            nc.gpsimd.affine_select(out=view, in_=view, compare_op=ALU.is_ge, fill=0.0, base=0,
                                    pattern=[[-AD, P // AD], [0, AD]], channel_multiplier=1).then_inc(selected, 1)
            pool.wait_ge(selected, 3)
            nc.gpsimd.affine_select(out=view, in_=view, compare_op=ALU.is_ge, fill=0.0, base=AD - 1,
                                    pattern=[[AD, P // AD], [0, AD]], channel_multiplier=-1).then_inc(selected, 1)
            nc.gpsimd.memset(keep["flags"][:, 0:1], 0.0).then_inc(selected, 1)
            nc.gpsimd.memset(keep["eps"][:, :], 1e-5).then_inc(selected, 1)
            nc.gpsimd.memset(keep["mean_w"][:, :], 1.0 / D).then_inc(selected, 1)
            nc.gpsimd.memset(keep["ln2x10"][:, :], 6.931471805599453).then_inc(selected, 1)

        @block.scalar
        def _(act):
            act.wait_ge(loaded, 48)
            nc.scalar.activation(c_act[:, :, :], c_in[:, :, :], ACT.Silu).then_inc(silu_done, 1)

        @block.tensor
        def _(pe):
            pe.wait_ge(silu_done, 1)
            for j in range(MODS * DC):
                for c in range(DC):
                    mm = nc.tensor.matmul(mod_ps[:, j, :], wmod[:, c, j * P:(j + 1) * P], c_act[:, c, :],
                                          start=(c == 0), stop=(c == DC - 1))
            mm.then_inc(mod_ready, 1)
            pe.wait_ge(rep_done, 1)
            for b in range(B):
                for c in range(DC):
                    mm = nc.tensor.matmul(row_ps[:, b, :], c_rep[:, c, b, :], wmod[:, c, 2 * D:3 * D], start=(c == 0), stop=(c == DC - 1))
            mm.then_inc(mod_ready, 1)

        @block.vector
        def _(dve):
            step = [0]

            def chained(instruction):
                step[0] += 1
                instruction.then_inc(mod_step, 1)
                dve.wait_ge(mod_step, step[0])

            dve.wait_ge(silu_done, 1)
            nc.vector.tensor_copy(c_rep[:, :, :, :], c_act[:, :, :].unsqueeze(3).to_broadcast([P, DC, B, P])).then_inc(rep_done, 1)
            dve.wait_ge(loaded, 48)
            dve.wait_ge(mod_ready, 1)
            chained(nc.vector.tensor_copy(modv[:, :, :], mod_ps[:, :, :]))
            for j in (1, 4):
                v = modv[:, j * DC:(j + 1) * DC, :]
                chained(nc.vector.tensor_scalar(v, v, 1.0, None, ALU.add))
            dve.wait_ge(mod_ready, 2)
            chained(nc.vector.tensor_copy(keep["garow"][:, :, :], row_ps[:, :, :]))
            for v, sg in ((keep["garow"][:, :, :], row_sign[:, :, :]), (modv[:, 5 * DC:6 * DC, :], sign[:, :, :])):
                chained(nc.vector.tensor_scalar(sg, v, 0.0, 2.0, ALU.is_ge, ALU.mult))
                chained(nc.vector.tensor_scalar(sg, sg, -1.0, None, ALU.add))
                chained(nc.vector.tensor_tensor(v, v, sg, ALU.mult))
                chained(nc.vector.tensor_scalar(v, v, 0.25, None, ALU.max))
                chained(nc.vector.tensor_tensor(v, v, sg, ALU.mult))
            for g in range(NG):
                chained(nc.vector.tensor_copy(keep["gbg"][:, g, :], modv[:, 5 * DC:6 * DC, g // GPB]))


def linear_attention_program(nc, dram, keep):
    WPB = GPB * TPG
    HPC = P // AD
    with ExitStack() as own:
        sb = lambda name, shape, dt=F32: own.enter_context(nc.sbuf_tensor("a_" + name, shape, dt))
        ps = lambda name, shape: own.enter_context(nc.psum_tensor("a_" + name, shape, F32))
        used = own.enter_context(cleared_semaphores(nc))
        sem = lambda name: used("a_" + name)
        modv, acol, eps, ident, blocks, garow = (keep[k] for k in ("modv", "acol", "eps", "ident", "blocks", "garow"))
        SA, CA, SB, CB = 0, DC, 3 * DC, 4 * DC

        wq = sb("wq", [P, DC, D])
        wkv = sb("wkv", [P, DC, 2 * D])
        wo = sb("wo", [P, DC, D])
        wog = sb("wog", [P, B, DC, D])
        bkv = sb("bkv", [P, 2 * D])
        bo = sb("bo", [P, D])
        gabo = sb("gabo", [P, B, D])
        xt = sb("xt", [P, GPB, TPG, D])
        xr = sb("xr", [P, GPB, TPG, D])
        xn = sb("xn", [P, 2, TPG, D])
        stats = sb("stats", [P, TPG, 6])
        mv = sb("mv", [P, 2, TPG, 2])
        lnv = sb("lnv", [P, TPG])
        rstd = sb("rstd", [P, 2, TPG])
        stats2 = sb("stats2", [P, 6])
        mv2 = sb("mv2", [P, 2, TPG, 2])
        lnv2 = sb("lnv2", [P, TPG])
        rstd2 = sb("rstd2", [P, 2, TPG])
        hT = sb("hT", [P, 2, DC, P])
        kk = sb("kk", [P, 2, D])
        ek = sb("ek", [P, 2, D])
        kf = sb("kf", [P, 2, D])
        vo = sb("vo", [P, 2, DC, P + 1])
        eq = sb("eq", [P, 2, DC, P])
        rq = sb("rq", [P, 2, DC, P])
        qT = sb("qT", [P, WPB, DC, P])
        ksum = sb("ksum", [P, DC])
        kvd = sb("kvd", [P, DC, P + HPC])
        den = sb("den", [P, DC, HPC])
        o = sb("o", [P, 2, D])
        oT = sb("oT", [P, 2, DC, P])
        hn = sb("hn", [P, 2, TPG, D])
        h0 = sb("h0", [P, 2, DC, G])
        mod1 = sb("mod1", [P, MODS * DC])
        mod2 = sb("mod2", [P, MODS * DC])
        idle = sb("idle", [P, 1])
        idle2 = sb("idle2", [P, 1])
        seed = sb("seed", [P, 3])

        kvp = ps("kvp", [P, 2 * D])
        qp = ps("qp", [P, DC, P])
        acc = ps("acc", [P, DC, P + 1])
        nd = ps("nd", [P, DC, P + HPC])
        y = ps("y", [P, D])
        tx = ps("tx", [P, DC, P])
        to = ps("to", [P, DC, P])
        th = ps("th", [P, DC, P])

        x_in = [sem(f"x_in{g}") for g in range(GPB)]
        x1_stored = [sem(f"x1_stored{g}") for g in range(GPB)]
        h0_stored = [sem(f"h0_stored{r}") for r in range(2)]
        names = ("idled w_in wog_set gabo_set ones_set mod1_set mod2_set stat_done mv_done ln_done rstd_done xn_done tx_done hT_done kv_done "
                 "q_done k_set vo_done ek_done ek_cut kf_done eq_done rq_done qT_done acc_done ks_set kvd_done xr_done nd_done den_cut "
                 "rcp_done o_done to_done oT_done y_done x1_done stat2_done mv2_done ln2_done rstd2_done hn_done th_done h0_done").split()
        s = {name: sem(name) for name in names}
        SEED = 1
        block = own.enter_context(nc.Block())

        def bodies(engine, body):
            body(0, True, False, True)
            with engine.Fori(1, B - 1) as b:
                body(b, True, True, True)
            body(B - 1, True, True, False)
            body(B, False, True, False)

        @block.sync
        def _(sp):
            def load_x(b, g):
                sp.dma_start(xt[:, g, :, :], dram["x"][bass.ds(b, 1), g * G:(g + 1) * G, :].rearrange("a (t p) d -> p (a t) d", p=P)).then_inc(x_in[g], 16)

            def store_h0(b, g):
                sp.wait_ge(s["h0_done"], (b * GPB + g + 1) * TPG + SEED)
                sp.dma_start(dram["h0"][bass.ds(b * GPB + g, 1)].rearrange("a p n -> (a p) n"), h0[:, g % 2, :, :].rearrange("p c n -> p (c n)")).then_inc(h0_stored[g % 2], 16)

            def body(b, first, second, more):
                for g in range(GPB):
                    if second:
                        sp.wait_ge(s["x1_done"], ((b - 1) * GPB + g + 1) * TPG)
                        sp.dma_start(dram["x1"][bass.ds(b - 1, 1), g * G:(g + 1) * G, :].rearrange("a (t p) d -> p (a t) d", p=P), xr[:, g, :, :]).then_inc(x1_stored[g], 16)
                        if g > 0:
                            store_h0(b - 1, g - 1)
                    if first and more:
                        sp.wait_ge(s["xn_done"], (b * GPB + g + 1) * TPG)
                        if not second or g > 0:
                            h = g if not second else g - 1
                            sp.wait_ge(s["xr_done"], b * GPB + h + 1)
                            load_x(b + 1, h)
                if second:
                    store_h0(b - 1, GPB - 1)
                    if first and more:
                        sp.wait_ge(s["xr_done"], (b + 1) * GPB)
                        load_x(b + 1, GPB - 1)

            load_x(0, 0)
            for dst, src in ((wq, "Wq"), (wo, "Wo")):
                sp.dma_start(dst[:, :, :], dram[src].rearrange("(c p) n -> p c n", p=P)).then_inc(s["w_in"], 16)
            for j, src in enumerate(("Wk", "Wv")):
                sp.dma_start(wkv[:, :, j * D:(j + 1) * D], dram[src].rearrange("(c p) n -> p c n", p=P)).then_inc(s["w_in"], 16)
            row = lambda src: dram[src].rearrange("(a n) -> a n", a=1).to_broadcast([P, D])
            for j, src in enumerate(("bk", "bv")):
                sp.dma_start(bkv[:, j * D:(j + 1) * D], row(src)).then_inc(s["w_in"], 16)
            sp.dma_start(bo[:, :], row("bo")).then_inc(s["w_in"], 16)
            for g in range(1, GPB):
                load_x(0, g)
            bodies(sp, body)
            for g in range(GPB):
                sp.wait_ge(x1_stored[g], B * 16)
            for r in range(2):
                sp.wait_ge(h0_stored[r], B * GPB // 2 * 16 + SEED)

        @block.gpsimd
        def _(pool):
            for n, seeded in enumerate(h0_stored + [s["h0_done"]]):
                nc.gpsimd.memset(seed[:, n:n + 1], 0.0).then_inc(seeded, SEED)
            nc.gpsimd.memset(idle2[:, :], 0.0).then_inc(s["idled"], 1)
            pool.wait_ge(s["w_in"], 7 * 16)
            nc.gpsimd.tensor_tensor(gabo[:, :, :], garow[:, :, :], bo[:, :].unsqueeze(1).to_broadcast([P, B, D]), ALU.mult).then_inc(s["gabo_set"], 1)
            for b in range(B):
                nc.gpsimd.tensor_tensor(wog[:, b, :, :], wo[:, :, :], garow[:, b, :].unsqueeze(1).to_broadcast([P, DC, D]), ALU.mult).then_inc(s["wog_set"], 1)
            pool.wait_ge(s["gabo_set"], 1)

            def body(b, first, second, more):
                if not first:
                    return
                for g in range(GPB):
                    pool.wait_ge(x_in[g], b * 16 + 16)
                    if second:
                        pool.wait_ge(x1_stored[g], b * 16)
                        pool.wait_ge(s["hn_done"], ((b - 1) * GPB + g + 1) * TPG)
                    pool.wait_ge(s["idled"], b * GPB + g + 1)
                    nc.gpsimd.tensor_tensor(idle2[:, :], idle2[:, :], idle2[:, :], ALU.add).then_inc(s["idled"], 1)
                    nc.gpsimd.tensor_tensor(xr[:, g, :, :], xt[:, g, :, :], gabo[:, bass.ds(b, 1), :].to_broadcast([P, TPG, D]), ALU.add).then_inc(s["xr_done"], 1)

            bodies(pool, body)

        @block.scalar
        def _(act):
            def deviation(done, out_ln, ln_done, out, rstd_done, var, n, count):
                act.wait_ge(done, count)
                nc.scalar.activation(out_ln, var, ACT.Ln, bias=eps[:, 0:1]).then_inc(ln_done, 1)
                act.wait_ge(ln_done, n + 1)
                nc.scalar.activation(out, out_ln, ACT.Exp, scale=-0.5).then_inc(rstd_done, 1)

            def deviation1(n, g):
                deviation(s["mv_done"], lnv[:, :], s["ln_done"], rstd[:, g % 2, :], s["rstd_done"], mv[:, g % 2, :, 1], n, (n + 1) * TPG)

            def deviation2(n, g):
                deviation(s["mv2_done"], lnv2[:, :], s["ln2_done"], rstd2[:, g % 2, :], s["rstd2_done"], mv2[:, g % 2, :, 1], n, (n + 1) * TPG)

            def modulate(m, w):
                act.wait_ge(s["tx_done"], m + 1)
                for c in range(DC):
                    h = nc.scalar.activation(hT[:, w % 2, c, :], tx[:, c, :], ACT.Identity, scale=mod1[:, CA + c:CA + c + 1], bias=mod1[:, SA + c:SA + c + 1])
                h.then_inc(s["hT_done"], 1)

            def body(b, first, second, more):
                if first:
                    act.wait_ge(s["mod1_set"], b + 1)
                    modulate(b * WPB, 0)
                for w in range(WPB):
                    g, t = w // TPG, w % TPG
                    m, m2 = b * WPB + w, (b - 1) * WPB + w
                    if second:
                        if t == 0 and g > 0:
                            deviation2((b - 1) * GPB + g - 1, g - 1)
                        act.wait_ge(s["to_done"], m2 + 1)
                        nc.scalar.activation(oT[:, w % 2, :, :], to[:, :, :], ACT.Copy).then_inc(s["oT_done"], 1)
                    if first:
                        act.wait_ge(s["k_set"], m + 1)
                        nc.scalar.activation(ek[:, w % 2, :], kk[:, w % 2, :], ACT.Exp).then_inc(s["ek_done"], 1)
                        if w + 1 < WPB:
                            modulate(m + 1, w + 1)
                        act.wait_ge(s["q_done"], m + 1)
                        for fn, dst, done in ((ACT.Exp, eq, "eq_done"), (ACT.Relu, rq, "rq_done")):
                            for c in range(DC):
                                a = nc.scalar.activation(dst[:, w % 2, c, :], qp[:, c, :], fn, bias=acol[:, c:c + 1])
                            a.then_inc(s[done], 1)
                        if t == 2 and (g + 1 < GPB or more):
                            deviation1(b * GPB + g + 1, g + 1)
                    if second and g > 0:
                        modulate2(b, w - TPG)
                if second:
                    deviation2(b * GPB - 1, GPB - 1)
                    for t in range(TPG):
                        modulate2(b, WPB - TPG + t)

            def modulate2(b, w):
                g, t = w // TPG, w % TPG
                m = (b - 1) * WPB + w
                if t == 0:
                    act.wait_ge(h0_stored[g % 2], ((b - 1) * (GPB // 2) + g // 2) * 16 + SEED)
                if w == 0:
                    act.wait_ge(s["mod2_set"], b)
                act.wait_ge(s["th_done"], m + 1)
                for c in range(DC):
                    h = nc.scalar.activation(h0[:, g % 2, c, t * P:(t + 1) * P], th[:, c, :], ACT.Identity, scale=mod2[:, CB + c:CB + c + 1], bias=mod2[:, SB + c:SB + c + 1])
                h.then_inc(s["h0_done"], 1)

            nc.scalar.preload_act_table_set("natural_log_exp_and_others")
            deviation1(0, 0)
            bodies(act, body)

        @block.tensor
        def _(pe):
            def turn(dst, src, done):
                for c in range(DC):
                    mm = nc.tensor.transpose(dst[:, c, :], src[:, c * P:(c + 1) * P], ident[:, :])
                mm.then_inc(s[done], 1)

            def turn_x(m, w):
                pe.wait_ge(s["xn_done"], m + 1)
                if w > 0:
                    pe.wait_ge(s["hT_done"], m)
                turn(tx, xn[:, (w // TPG) % 2, w % TPG, :], "tx_done")

            def attend(m, w):
                if w > 0:
                    pe.wait_ge(s["o_done"], m)
                for c in range(DC):
                    mm = nc.tensor.matmul(nd[:, c, :], qT[:, w, c, :], kvd[:, c, :], start=True, stop=True)
                mm.then_inc(s["nd_done"], 1)

            def turn_h(m, w):
                pe.wait_ge(s["hn_done"], m + 1)
                if w > 0:
                    pe.wait_ge(s["h0_done"], m + SEED)
                turn(th, hn[:, (w // TPG) % 2, w % TPG, :], "th_done")

            def body(b, first, second, more):
                if first:
                    turn_x(b * WPB, 0)
                if second:
                    pe.wait_ge(s["kvd_done"], b * 3)
                    attend((b - 1) * WPB, 0)
                for w in range(WPB):
                    m, m2 = b * WPB + w, (b - 1) * WPB + w
                    if first:
                        pe.wait_ge(s["hT_done"], m + 1)
                        if w > 0:
                            pe.wait_ge(s["vo_done"], m)
                        for c in range(DC):
                            mm = nc.tensor.matmul(kvp[:, :], hT[:, w % 2, c, :], wkv[:, c, :], start=(c == 0), stop=(c == DC - 1))
                        mm.then_inc(s["kv_done"], 1)
                    if second:
                        pe.wait_ge(s["o_done"], m2 + 1)
                        if w > 0:
                            pe.wait_ge(s["oT_done"], m2)
                        turn(to, o[:, w % 2, :], "to_done")
                    if first:
                        if w > 0:
                            pe.wait_ge(s["rq_done"], m)
                        for d in range(DC):
                            for c in range(DC):
                                mm = nc.tensor.matmul(qp[:, d, :], wq[:, c, d * P:(d + 1) * P], hT[:, w % 2, c, :], start=(c == 0), stop=(c == DC - 1))
                        mm.then_inc(s["q_done"], 1)
                        if w + 1 < WPB:
                            turn_x(m + 1, w + 1)
                    if second:
                        if w + 1 < WPB:
                            attend(m2 + 1, w + 1)
                        pe.wait_ge(s["oT_done"], m2 + 1)
                        if w > 0:
                            pe.wait_ge(s["x1_done"], m2)
                        for c in range(DC):
                            mm = nc.tensor.matmul(y[:, :], oT[:, w % 2, c, :], wog[:, bass.ds(b - 1, 1), c, :].rearrange("p a n -> p (a n)"), start=(c == 0), stop=(c == DC - 1))
                        mm.then_inc(s["y_done"], 1)
                    if first:
                        pe.wait_ge(s["kf_done"], m + 1)
                        pe.wait_ge(s["vo_done"], m + 1)
                        if w == 0 and (not isinstance(b, int) or b > 0):
                            pe.wait_ge(s["kvd_done"], b * 3)
                        for c in range(DC):
                            mm = nc.tensor.matmul(acc[:, c, :], kf[:, w % 2, c * P:(c + 1) * P], vo[:, w % 2, c, :],
                                                  start=(w == 0 and c == 0), stop=(w == WPB - 1 and c == DC - 1))
                        mm.then_inc(s["acc_done"], 1)
                    if second and w >= TPG:
                        turn_h(m2 - TPG, w - TPG)
                if second:
                    for w in range(WPB - TPG, WPB):
                        turn_h((b - 1) * WPB + w, w)

            pe.wait_ge(s["w_in"], 7 * 16)
            pe.wait_ge(s["wog_set"], B)
            bodies(pe, body)

        @block.vector
        def _(dve):
            def statistics(b, g, t):
                n = b * GPB + g
                if t == 0:
                    dve.wait_ge(x_in[g % GPB], (b + g // GPB) * 16 + 16)
                nc.vector.bn_stats(stats[:, t, :], xt[:, g % GPB, t, :]).then_inc(s["stat_done"], 1)
                dve.wait_ge(s["stat_done"], n * TPG + t + 1)
                nc.vector.tensor_scalar(idle[:, :], idle[:, :], 1.0, None, ALU.mult)
                nc.vector.bn_aggr(mv[:, g % 2, t, :], stats[:, t, :]).then_inc(s["mv_done"], 1)

            def normalise(b, g, t):
                n = b * GPB + g
                if t == 0:
                    dve.wait_ge(s["rstd_done"], n + 1)
                nc.vector.tensor_scalar(xn[:, g % 2, t, :], xt[:, g % GPB, t, :], mv[:, g % 2, t, 0:1], rstd[:, g % 2, t:t + 1],
                                        ALU.subtract, ALU.mult).then_inc(s["xn_done"], 1)

            def normalise2(b, w):
                g, t = w // TPG, w % TPG
                if t == 0:
                    dve.wait_ge(s["rstd2_done"], (b - 1) * GPB + g + 1)
                nc.vector.tensor_scalar(hn[:, g % 2, t, :], xr[:, g, t, :], mv2[:, g % 2, t, 0:1], rstd2[:, g % 2, t:t + 1],
                                        ALU.subtract, ALU.mult).then_inc(s["hn_done"], 1)

            def divide(m, w):
                dve.wait_ge(s["nd_done"], m + 1)
                nc.vector.tensor_scalar(den[:, :, :], nd[:, :, P:], 1e-6, None, ALU.max).then_inc(s["den_cut"], 1)
                dve.wait_ge(s["den_cut"], m + 1)
                nc.vector.reciprocal(den[:, :, :], den[:, :, :]).then_inc(s["rcp_done"], 1)
                dve.wait_ge(s["rcp_done"], m + 1)
                nc.vector.tensor_tensor(o[:, w % 2, :].rearrange("p (c h d) -> p c h d", c=DC, d=AD), nd[:, :, 0:P].rearrange("p c (h d) -> p c h d", d=AD),
                                        den[:, :, :].unsqueeze(3).to_broadcast([P, DC, HPC, AD]), ALU.mult).then_inc(s["o_done"], 1)

            def body(b, first, second, more):
                if first:
                    if not isinstance(b, int) or b > 0:
                        dve.wait_ge(s["hT_done"], b * WPB)
                    nc.vector.tensor_scalar(mod1[:, :], modv[:, :, bass.ds(b, 1)].rearrange("p m a -> p (m a)"), 1.0, None, ALU.mult).then_inc(s["mod1_set"], 1)
                if second:
                    dve.wait_ge(s["h0_done"], (b - 1) * WPB + SEED)
                    nc.vector.tensor_scalar(mod2[:, :], modv[:, :, bass.ds(b - 1, 1)].rearrange("p m a -> p (m a)"), 1.0, None, ALU.mult).then_inc(s["mod2_set"], 1)
                    divide((b - 1) * WPB, 0)
                for w in range(WPB):
                    g, t = w // TPG, w % TPG
                    m, m2 = b * WPB + w, (b - 1) * WPB + w
                    if first:
                        dve.wait_ge(s["kv_done"], m + 1)
                        nc.vector.tensor_tensor(kk[:, w % 2, :], kvp[:, 0:D], bkv[:, 0:D], ALU.add).then_inc(s["k_set"], 1)
                        nc.vector.tensor_tensor(vo[:, w % 2, :, 0:P], kvp[:, D:].rearrange("p (c d) -> p c d", c=DC),
                                                bkv[:, D:].rearrange("p (c d) -> p c d", c=DC), ALU.add).then_inc(s["vo_done"], 1)
                    if second and g > 0:
                        normalise2(b, w - TPG)
                    if first:
                        dve.wait_ge(s["ek_done"], m + 1)
                        nc.vector.tensor_scalar(ek[:, w % 2, :], ek[:, w % 2, :], 1.0, None, ALU.min).then_inc(s["ek_cut"], 1)
                        dve.wait_ge(s["ek_cut"], m + 1)
                        nc.vector.scalar_tensor_tensor(out=kf[:, w % 2, :], in0=kk[:, w % 2, :], scalar=0.0, in1=ek[:, w % 2, :],
                                                       op0=ALU.max, op1=ALU.add).then_inc(s["kf_done"], 1)
                    if second and w + 1 < WPB:
                        divide(m2 + 1, w + 1)
                    if first:
                        dve.wait_ge(s["rq_done"], m + 1)
                        nc.vector.scalar_tensor_tensor(out=qT[:, w, :, :], in0=eq[:, w % 2, :, :], scalar=1.0, in1=rq[:, w % 2, :, :],
                                                       op0=ALU.min, op1=ALU.add).then_inc(s["qT_done"], 1)
                        if g + 1 < GPB or more:
                            if t < 2:
                                statistics(b, g + 1, 2 * t)
                                statistics(b, g + 1, 2 * t + 1)
                            else:
                                normalise(b, g + 1, 2 * t - 4)
                                normalise(b, g + 1, 2 * t - 3)
                    if second:
                        dve.wait_ge(s["y_done"], m2 + 1)
                        if t == 0:
                            dve.wait_ge(s["xr_done"], (b - 1) * GPB + g + 1)
                        nc.vector.tensor_tensor(xr[:, g, t, :], xr[:, g, t, :], y[:, :], ALU.add).then_inc(s["x1_done"], 1)
                        dve.wait_ge(s["x1_done"], m2 + 1)
                        nc.vector.bn_stats(stats2[:, :], xr[:, g, t, :]).then_inc(s["stat2_done"], 1)
                        dve.wait_ge(s["stat2_done"], m2 + 1)
                        nc.vector.tensor_scalar(idle[:, :], idle[:, :], 1.0, None, ALU.mult)
                        nc.vector.bn_aggr(mv2[:, g % 2, t, :], stats2[:, :]).then_inc(s["mv2_done"], 1)
                if second:
                    for w in range(WPB - TPG, WPB):
                        normalise2(b, w)
                if first:
                    dve.wait_ge(s["acc_done"], (b + 1) * WPB)
                    nc.vector.tensor_copy(ksum[:, :], acc[:, :, P]).then_inc(s["ks_set"], 1)
                    nc.vector.tensor_tensor(kvd[:, :, 0:P], acc[:, :, 0:P], blocks[:, :].unsqueeze(1).to_broadcast([P, DC, P]), ALU.mult).then_inc(s["kvd_done"], 1)
                    dve.wait_ge(s["ks_set"], b + 1)
                    for c in range(DC):
                        nc.vector.tensor_scalar(kvd[:, c, P:], blocks[:, 0:P:AD], ksum[:, c:c + 1], None, ALU.mult).then_inc(s["kvd_done"], 1)

            nc.vector.memset(vo[:, :, :, P:P + 1], 1.0).then_inc(s["ones_set"], 1)
            nc.vector.memset(idle[:, :], 0.0).then_inc(s["ones_set"], 1)
            dve.wait_ge(s["w_in"], 7 * 16)
            for t in range(TPG):
                statistics(0, 0, t)
            for t in range(TPG):
                normalise(0, 0, t)
            bodies(dve, body)


def layer_weights(nc, ctx):
    sb = lambda name, shape, dt=F32: ctx.enter_context(nc.sbuf_tensor(name, shape, dt))
    return {
        "wqkv": sb("wqkv", [P, 2, DC, 3 * INNER], F32R),
        "w1": sb("w1", [P, 2, DC, 2, HC * P], F32R),
        "w2": sb("w2", [P, 2, HC, D], F32R),
        "wo": sb("wo", [P, PAIRS, D]),
        "col": sb("col", [P, NCOL]),
        "qks": sb("qks", [P, 4, DH]),
    }


def weights_program(nc, layer, dram, keep, weights):
    with ExitStack() as own:
        pre = f"w{layer}_"
        sb = lambda name, shape, dt=F32: own.enter_context(nc.sbuf_tensor(pre + name, shape, dt))
        sem = own.enter_context(cleared_semaphores(nc))
        w1 = sb("w1", [P, DC, 2, HC * P])
        w1s = sb("w1s", [P, DC, 2, HC * P])
        w2 = sb("w2", [P, HC, D])
        wqkv = sb("wqkv", [P, DC, 3 * INNER])
        shift = own.enter_context(nc.psum_tensor(pre + "shift", [P, 2 * HC], F32))
        small_in, w1_in, w2_in = sem(pre + "small_in"), sem(pre + "w1_in"), sem(pre + "w2_in")
        wqkv_in = [sem(pre + f"wqkv_in{c}") for c in range(DC)]
        padded, scaled, high, low = sem(pre + "padded"), sem(pre + "scaled"), sem(pre + "high"), sem(pre + "low")
        shift_done, shifted = sem(pre + "shift_done"), sem(pre + "shifted")
        col = weights["col"]
        block = own.enter_context(nc.Block())
        parts = [(wqkv[:, c], weights["wqkv"][:, 0, c], weights["wqkv"][:, 1, c]) for c in range(DC)]
        parts += [(w1s[:, c], weights["w1"][:, 0, c], weights["w1"][:, 1, c]) for c in range(DC)]
        parts += [(w2[:, :], weights["w2"][:, 0], weights["w2"][:, 1])]

        @block.sync
        def _(sp):
            sp.dma_start(col[:, :], dram["cols"][layer]).then_inc(small_in, 16)
            sp.dma_start(weights["qks"][:, :, :], dram["qks"][layer:layer + 1].to_broadcast([P, 4, DH])).then_inc(small_in, 16)
            for c in range(DC):
                sp.dma_start(wqkv[:, c, :], dram["wqkv"][layer][c * P:(c + 1) * P, :]).then_inc(wqkv_in[c], 16)
            sp.dma_start(weights["wo"][:, :, :], dram["wo"][layer].rearrange("(c p) n -> p c n", p=P)).then_inc(small_in, 16)
            sp.wait_ge(small_in, 48)

        @block.scalar
        def _(act):
            for j in range(2):
                act.dma_start(w1[:, :, j, 0:HID], dram["w1"][layer][:, j * HID:(j + 1) * HID].rearrange("(c p) n -> p c n", p=P)).then_inc(w1_in, 16)
            act.dma_start(w2[:, 0:HC - 1, :], dram["w2"][layer][0:(HC - 1) * P, :].rearrange("(c p) n -> p c n", p=P)).then_inc(w2_in, 16)
            act.wait_ge(padded, 2)
            act.dma_start(w2[0:TAIL, HC - 1, :], dram["w2"][layer][(HC - 1) * P:HID, :]).then_inc(w2_in, 16)
            for n, (w, hi, lo) in enumerate(parts):
                if n < DC:
                    act.wait_ge(wqkv_in[n], 16)
                elif n < 2 * DC:
                    act.wait_ge(scaled, n - DC + 1)
                else:
                    act.wait_ge(w2_in, 32)
                nc.scalar.activation(hi, w, ACT.Copy).then_inc(high, 1)

        @block.gpsimd
        def _(pool):
            nc.gpsimd.memset(w1[:, :, :, HID:], 0.0).then_inc(padded, 1)
            nc.gpsimd.memset(w2[:, HC - 1, :], 0.0).then_inc(padded, 1)
            pool.wait_ge(small_in, 48)
            pool.wait_ge(w1_in, 32)
            pool.wait_ge(padded, 2)
            for c in range(DC):
                nc.gpsimd.tensor_scalar(w1s[:, c], w1[:, c], col[:, LG + c:LG + c + 1], None, ALU.mult).then_inc(scaled, 1)

        @block.tensor
        def _(pe):
            pe.wait_ge(small_in, 48)
            pe.wait_ge(w1_in, 32)
            pe.wait_ge(padded, 2)
            for j in range(2):
                for m in range(HC):
                    for c in range(DC):
                        mm = nc.tensor.matmul(shift[:, j * HC + m:j * HC + m + 1], w1[:, c, j, m * P:(m + 1) * P], col[:, LB + c:LB + c + 1],
                                              start=(c == 0), stop=(c == DC - 1))
            mm.then_inc(shift_done, 1)

        @block.vector
        def _(dve):
            for n, (w, hi, lo) in enumerate(parts):
                if n == len(parts) - 1:
                    dve.wait_ge(shift_done, 1)
                    nc.vector.tensor_tensor(col[:, B1A:B1A + 2 * HC], col[:, B1A:B1A + 2 * HC], shift[:, :], ALU.add).then_inc(shifted, 1)
                dve.wait_ge(high, n + 1)
                nc.vector.tensor_tensor(lo, w, hi.bitcast(F32), ALU.subtract).then_inc(low, 1)
            dve.wait_ge(low, len(parts))
            dve.wait_ge(shifted, 1)


def layer_program(nc, layer, dram, keep, weights):
    last_layer = layer == 1
    source = dram["mid"] if last_layer else dram["h0"]
    x1_rows = dram["x1"].rearrange("b (g t) d -> (b g) t d", t=G) if last_layer else None
    UNITS = TPG * ST
    PROJ = 3 * UNITS
    PASSES = ((0, 0), (0, 1), (1, 0))
    with ExitStack() as own:
        pre = f"l{layer}_"
        sb = lambda name, shape, dt=F32: own.enter_context(nc.sbuf_tensor(pre + name, shape, dt))
        ps = lambda name, shape: own.enter_context(nc.psum_tensor(pre + name, shape, F32))
        used = own.enter_context(cleared_semaphores(nc))
        sem = lambda name: used(pre + name)
        ident, identb, eps, mean_w, flags, gbg = (keep[k] for k in ("ident", "identb", "eps", "mean_w", "flags", "gbg"))
        wqkv, w1, w2, wo, col, qks = (weights[k] for k in ("wqkv", "w1", "w2", "wo", "col", "qks"))

        tab = sb("tab", [P, TPG, 4, DH])
        band = sb("band", [P, 2, P], BF16)
        band0 = sb("band0", [P, GPB, 2, P], BF16)
        xin = sb("xin", [P, ST, DC, 1 + G])
        x2 = sb("x2", [P, ST, DC, 1 + G])
        xw = sb("xw", [P, 2, 2, DC, P], F32R)
        kT = sb("kT", [P, ST, PAIRS, TPG, P])
        v = sb("v", [P, ST, TPG, INNER])
        attn = sb("attn", [P, ST, PAIRS, G])
        qk = sb("qk", [P, 2, 2, H, DH])
        sq = sb("sq", [P, 2 * INNER])
        ss = sb("ss", [P, 2, 2 * H])
        lss = sb("lss", [P, 2 * H])
        rg = sb("rg", [P, 2 * H])
        nt = sb("nt", [P, 2 * H])
        rr = sb("rr", [P, 2, 2 * H])
        q8 = sb("q8", [P, 2, H])
        rot = sb("rot", [P, 2, 2, H, DH])
        qz = sb("qz", [P, 2, H, P])
        mx = sb("mx", [P, 4])
        nb = sb("nb", [P, 2, 4])
        rs = sb("rs", [P, 2, 4])
        ri = sb("ri", [P, 2, 4])
        pr = sb("pr", [P, 2, 4, 2 * P])
        prT = sb("prT", [P, 2, 4 * 2, P])
        rsw = sb("rsw", [P, G])
        act_g = sb("act_g", [P, 2, G])
        hid = sb("hid", [P, 2, 2, G], F32R)
        hn = sb("hn", [P, 2, DC, G], F32R)
        seed = sb("seed", [P, 1 + ST])
        x1 = pr[:, :, :, :].rearrange("p s a n -> p s (a n)").rearrange("p s (t d) -> p s t d", t=TPG)
        rows = prT[:, :, :, :].rearrange("p s a n -> p s (a n)").rearrange("p s (t d) -> p s t d", t=TPG)

        pj = ps("pj", [P, 2, G])
        sc = ps("sc", [P, 2, G])
        pt = ps("pt", [P, 2, G])
        tp = ps("tp", [P, G])
        ov = ps("ov", [P, G])
        HIDDEN_BANKS = [(tp[:, :], ov[:, :]), (sc[:, 0, :], sc[:, 1, :]), (pt[:, 0, :], pt[:, 1, :])]

        names = ("tab_in zeroed bands tab_set xh_set xl_set proj_done qkv_set sq_done sums_done ss_done ln_done rr_done newton "
                 "rn_done q8_done rot_done sum_done kn_done turn_done turn_set s_done mx_done nb_done exp_done rcp_done pn_done "
                 "pt_done ptA ptB pv_done o_set wo_done x2_done x2_halo mean_done xc_done sqm_done var_done lnw_done rsw_done "
                 "hn_done nh_done nl_done ag_done gelu_done prod_done hh_done hl_done w2_done y_used x3_done fin_done rows_set").split()
        s = {name: sem(name) for name in names}
        x_in = [sem(f"x_in{st}") for st in range(ST)]
        x1_in = [sem(f"x1_in{st}") for st in range(ST)]
        x_halo = [sem(f"x_halo{st}") for st in range(ST)]
        stored = [sem(f"stored{st}") for st in range(ST)]
        SEED = 1
        SEEDED = [s["y_used"]] + stored
        block = own.enter_context(nc.Block())
        ZEROED = 9

        @block.sync
        def _(sp):
            def load_x(i, st):
                sp.dma_start(xin[:, st, :, 1:], source[bass.ds(i + st * STEPS, 1)].rearrange("a p (c n) -> (a p) c n", c=DC)).then_inc(x_in[st], 16)

            def load_tab(i):
                sp.dma_start(tab[:, :, :, :], dram["tab"][:, bass.ds((i % GPB) * TPG, TPG), :, :]).then_inc(s["tab_in"], 16)

            def step(i, more):
                if more:
                    sp.wait_ge(s["rot_done"], (i + 1) * UNITS * 2)
                    load_tab(i + 1)
                    sp.wait_ge(x_halo[0], i + 1)
                    load_x(i + 1, 0)
                if last_layer:
                    sp.wait_ge(s["pt_done"], (i + 1) * UNITS * 2)
                    for st in range(ST):
                        sp.dma_start(x1[:, st, :, :], x1_rows[bass.ds(i + st * STEPS, 1)].rearrange("a (t p) d -> p (a t) d", p=P)).then_inc(x1_in[st], 16)
                if more:
                    sp.wait_ge(x_halo[1], i + 1)
                    load_x(i + 1, 1)

            sp.wait_ge(s["zeroed"], ZEROED)
            load_x(0, 0)
            load_tab(0)
            load_x(0, 1)
            with sp.Fori(0, STEPS - 1) as i:
                step(i, True)
            step(STEPS - 1, False)

        @block.gpsimd
        def _(pool):
            z = s["zeroed"]
            nc.gpsimd.memset(xin[:, :, :, 0:1], 0.0).then_inc(z, 1)
            nc.gpsimd.memset(qz[:, :, :, :], 0.0).then_inc(z, 1)
            nc.gpsimd.memset(x2[:, :, :, 0:1], 0.0).then_inc(z, 1)
            nc.gpsimd.memset(kT[:, :, :, TPG - 1, :], 0.0).then_inc(z, 1)
            nc.gpsimd.memset(v[:, :, TPG - 1, :], 0.0).then_inc(z, 1)
            nc.gpsimd.memset(band[:, :, :], 0.0).then_inc(z, 1)
            nc.gpsimd.memset(band0[:, 1:, :, :], 0.0).then_inc(z, 1)
            nc.gpsimd.memset(band0[:, 0, 0, :], 0.0).then_inc(z, 1)
            nc.gpsimd.memset(band0[:, 0, 1, :], BLOCKED).then_inc(z, 1)
            for n, seeded in enumerate(SEEDED):
                nc.gpsimd.memset(seed[:, n:n + 1], 0.0).then_inc(seeded, SEED)
            pool.wait_ge(z, ZEROED)
            for view, pattern, cm in ((band[:, 0, :], [[1, P]], -1), (band[:, 1, :], [[-1, P]], 1),
                                      (band0[:, :, 0, :], [[0, GPB], [-1, P]], 1),
                                      (band0[:, 1:, 1, :], [[0, GPB - 1], [1, P]], -1)):
                nc.gpsimd.affine_select(out=view, in_=view, compare_op=ALU.is_ge, fill=BLOCKED, base=0,
                                        pattern=pattern, channel_multiplier=cm).then_inc(s["bands"], 1)

            def scale_tab(i):
                pool.wait_ge(s["tab_in"], i * 16 + 16)
                nc.gpsimd.tensor_tensor(tab[:, :, :, :], tab[:, :, :, :], qks[:, :, :].unsqueeze(1).to_broadcast([P, TPG, 4, DH]), ALU.mult).then_inc(s["tab_set"], 1)

            def low_x(i, k):
                u, r, st, w = i * UNITS + k, k % 2, k % ST, k // ST
                pool.wait_ge(s["xh_set"], (u + 1) * DC)
                for c in range(DC):
                    o = 1 + w * P - c
                    nc.gpsimd.tensor_tensor(xw[:, r, 1, c, :], xin[:, st, c, o:o + P], xw[:, r, 0, c, :].bitcast(F32), ALU.subtract).then_inc(s["xl_set"], 1)

            def rotate(i, k):
                u = i * UNITS + k
                pool.wait_ge(s["rot_done"], u * 2 + 2)
                a, b = rot[:, 0, :, :, :], rot[:, 1, :, :, :]
                nc.gpsimd.tensor_tensor(a, a, b, ALU.add).then_inc(s["sum_done"], 1)

            def norm_k(i, k):
                u, r = i * UNITS + k, k % 2
                pool.wait_ge(s["sum_done"], u + 1)
                pool.wait_ge(s["rn_done"], u + 1)
                kk = rot[:, 0, 1, :, :]
                nc.gpsimd.tensor_tensor(kk, kk, rr[:, r, H:].unsqueeze(2).to_broadcast([P, H, DH]), ALU.mult).then_inc(s["kn_done"], 1)

            def norm_p(i, k, h):
                u = i * UNITS + k
                pool.wait_ge(s["rcp_done"], u * 2 + h + 1)
                w = pr[:, h, :, :]
                nc.gpsimd.tensor_tensor(w, w, ri[:, h, :].unsqueeze(2).to_broadcast([P, 4, 2 * P]), ALU.mult).then_inc(s["pn_done"], 1)

            def ahead(i):
                low_x(i, 0)
                scale_tab(i)
                low_x(i, 1)
                rotate(i, 0)
                norm_k(i, 0)

            def step(i, more):
                for k in range(UNITS):
                    if k > 0:
                        norm_p(i, k - 1, 1)
                    if k + 2 < UNITS:
                        low_x(i, k + 2)
                    if k + 1 < UNITS:
                        rotate(i, k + 1)
                    norm_p(i, k, 0)
                    if k + 1 < UNITS:
                        norm_k(i, k + 1)
                norm_p(i, UNITS - 1, 1)
                if more:
                    ahead(i + 1)

            ahead(0)
            with pool.Fori(0, STEPS - 1) as i:
                step(i, True)
            step(STEPS - 1, False)

        @block.scalar
        def _(act):
            def high_x(i, k):
                u, r, st, w = i * UNITS + k, k % 2, k % ST, k // ST
                if w == 0:
                    act.wait_ge(x_in[st], i * 16 + 16)
                for c in range(DC):
                    o = 1 + w * P - c
                    nc.scalar.activation(xw[:, r, 0, c, :], xin[:, st, c, o:o + P], ACT.Copy).then_inc(s["xh_set"], 1)

            def take(i, k, j):
                u, r, st, w = i * UNITS + k, k % 2, k % ST, k // ST
                act.wait_ge(s["proj_done"], u * 3 + j + 1)
                dst = qk[:, r, j, :, :].rearrange("p h d -> p (h d)") if j < 2 else v[:, st, w, :]
                nc.scalar.activation(dst, pj[:, (3 * k + j) % 2, :], ACT.Copy).then_inc(s["qkv_set"], 1)

            def squares(i, k, first=False):
                u, r = i * UNITS + k, k % 2
                act.wait_ge(s["qkv_set"], u * 3 + 2)
                if not first:
                    act.wait_ge(s["sums_done"], u)
                nc.scalar.activation(sq[:, :], qk[:, r].rearrange("p j h d -> p (j h d)"), ACT.Square).then_inc(s["sq_done"], 1)

            def inverse_norms(i, k):
                u, r = i * UNITS + k, k % 2
                act.wait_ge(s["ss_done"], u + 1)
                nc.scalar.activation(lss[:, :], ss[:, r, :], ACT.Ln, scale=float(2 ** 20)).then_inc(s["ln_done"], 1)
                act.wait_ge(s["ln_done"], u + 1)
                nc.scalar.activation(rg[:, :], lss[:, :], ACT.Exp, scale=-0.5, bias=keep["ln2x10"][:, 0:1]).then_inc(s["rr_done"], 1)

            def softmax(i, k, h):
                u, r = i * UNITS + k, k % 2
                act.wait_ge(s["nb_done"], u * 2 + h + 1)
                if k >= 1:
                    act.wait_ge(s["pt_done"], u * 2 + h - 1)
                for d in range(4):
                    e = nc.scalar.activation(pr[:, h, d, :], sc[:, d // 2, (d % 2) * 2 * P:(d % 2 + 1) * 2 * P], ACT.Exp,
                                             scale=q8[:, r, 4 * h + d:4 * h + d + 1], bias=nb[:, h, d:d + 1],
                                             accum_out=rs[:, h, d:d + 1])
                e.then_inc(s["exp_done"], 1)

            def take_pt(i, k, h):
                u = i * UNITS + k
                act.wait_ge(s["pt_done"], u * 2 + h + 1)
                if last_layer and k == 0:
                    act.wait_ge(stored[h], i * 16 + SEED)
                nc.scalar.activation(prT[:, h, 0:4, :].rearrange("p a q -> p (a q)"), pt[:, 0, :], ACT.Copy).then_inc(s["ptA"], 1)

            def inverse_deviation(i, st):
                n = i * ST + st
                act.wait_ge(s["var_done"], n + 1)
                if st > 0:
                    act.wait_ge(s["hn_done"], n)
                nc.scalar.activation(rsw[:, :], pt[:, 0, :], ACT.Ln, bias=eps[:, 0:1]).then_inc(s["lnw_done"], 1)
                act.wait_ge(s["lnw_done"], n + 1)
                nc.scalar.activation(rsw[:, :], rsw[:, :], ACT.Exp, scale=-0.5).then_inc(s["rsw_done"], 1)

            def square_centred(i, st):
                act.wait_ge(s["xc_done"], i * ST + st + 1)
                nc.scalar.activation(attn[:, st, 2:4, :], attn[:, st, 0:2, :], ACT.Square).then_inc(s["sqm_done"], 1)

            def high_norm(i, st):
                act.wait_ge(s["hn_done"], i * ST + st + 1)
                if st > 0:
                    act.wait_ge(s["ag_done"], (i * ST + st) * HC)
                for c in range(DC):
                    nc.scalar.activation(hn[:, 0, c, :], attn[:, st, c, :], ACT.Copy).then_inc(s["nh_done"], 1)

            def gelu(i, st, c):
                m = (i * ST + st) * HC + c
                act.wait_ge(s["ag_done"], m + 1)
                if st > 0 or c >= 2:
                    act.wait_ge(s["hl_done"], m - 1)
                nc.scalar.activation(act_g[:, c % 2, :], HIDDEN_BANKS[c % 3][1], ACT.Gelu, bias=col[:, B1G + c:B1G + c + 1]).then_inc(s["gelu_done"], 1)

            def high_hidden(i, st, c):
                m = (i * ST + st) * HC + c
                act.wait_ge(s["prod_done"], m + 1)
                if st > 0 or c >= 2:
                    act.wait_ge(s["w2_done"], m - 1)
                nc.scalar.activation(hid[:, c % 2, 0, :], act_g[:, c % 2, :], ACT.Copy).then_inc(s["hh_done"], 1)

            def step(i, more):
                for k in range(UNITS):
                    if k + 2 < UNITS:
                        act.wait_ge(s["proj_done"], (i * UNITS + k + 1) * 3)
                        high_x(i, k + 2)
                    if k > 0:
                        take_pt(i, k - 1, 1)
                    softmax(i, k, 0)
                    if k + 1 < UNITS:
                        inverse_norms(i, k + 1)
                        take(i, k + 1, 2)
                    take_pt(i, k, 0)
                    softmax(i, k, 1)
                    if k + 2 < UNITS:
                        for j in range(2):
                            act.wait_ge(s["rot_done"], (i * UNITS + k + 1) * 2)
                            take(i, k + 2, j)
                        squares(i, k + 2)
                take_pt(i, UNITS - 1, 1)
                square_centred(i, 0)
                if more:
                    high_x(i + 1, 0)
                inverse_deviation(i, 0)
                high_norm(i, 0)
                if more:
                    act.wait_ge(s["rot_done"], (i + 1) * UNITS * 2)
                    take(i + 1, 0, 0)
                    take(i + 1, 0, 1)
                    squares(i + 1, 0)
                square_centred(i, 1)
                if more:
                    take(i + 1, 0, 2)
                    high_x(i + 1, 1)
                inverse_deviation(i, 1)
                if more:
                    inverse_norms(i + 1, 0)
                for st in range(ST):
                    for c in range(HC):
                        gelu(i, st, c)
                        if c > 0:
                            high_hidden(i, st, c - 1)
                        if st == 0 and c == HC - 1:
                            high_norm(i, 1)
                        if st == 0 and c == 2 and more:
                            take(i + 1, 1, 0)
                            take(i + 1, 1, 1)
                            squares(i + 1, 1)
                    high_hidden(i, st, HC - 1)
                    if not last_layer:
                        act.wait_ge(s["y_used"], i * ST + st + 1 + SEED)
                        act.dma_start(dram["mid"][bass.ds(i + st * STEPS, 1)].rearrange("a p (c n) -> (a p) c n", c=DC), x2[:, st, :, 1:]).then_inc(stored[st], 16)
                if more:
                    nc.scalar.preload_act_table_set("natural_log_exp_and_others")
                if last_layer:
                    for st in range(ST):
                        n = i * ST + st
                        act.wait_ge(s["rows_set"], n + 1)
                        act.dma_start(dram["out"][bass.ds(i + st * STEPS, 1)].rearrange("a (t p) d -> p (a t) d", p=P), rows[:, st, :, :]).then_inc(stored[st], 16)

            nc.scalar.preload_act_table_set("natural_log_exp_and_others")
            act.wait_ge(s["zeroed"], ZEROED)
            high_x(0, 0)
            take(0, 0, 0)
            take(0, 0, 1)
            squares(0, 0, first=True)
            take(0, 0, 2)
            high_x(0, 1)
            take(0, 1, 0)
            take(0, 1, 1)
            inverse_norms(0, 0)
            squares(0, 1)
            with act.Fori(0, STEPS - 1) as i:
                step(i, True)
            step(STEPS - 1, False)
            for st in range(ST):
                act.wait_ge(stored[st], STEPS * 16 + SEED)

        @block.tensor
        def _(pe):
            def project(i, k, js, bank_free=True):
                u, r = i * UNITS + k, k % 2
                pe.wait_ge(s["xl_set"], (u + 1) * DC)
                for j in js:
                    if bank_free:
                        pe.wait_ge(s["qkv_set"], u * 3 + j - 1)
                    n = 0
                    for c in range(DC):
                        for a, b in PASSES:
                            mm = nc.tensor.matmul(pj[:, (3 * k + j) % 2, :], xw[:, r, a, c, :], wqkv[:, b, c, j * INNER:(j + 1) * INNER],
                                                  start=(n == 0), stop=(n == DC * 3 - 1))
                            n += 1
                    mm.then_inc(s["proj_done"], 1)

            def turn_q(i, k, first=False):
                u = i * UNITS + k
                pe.wait_ge(s["sum_done"], u + 1)
                if not first:
                    pe.wait_ge(s["turn_set"], u * 3)
                turn(0)

            def turn_k(i, k):
                u = i * UNITS + k
                pe.wait_ge(s["kn_done"], u + 1)
                pe.wait_ge(s["turn_set"], u * 3 + 2)
                turn(1)

            def turn(j):
                for c in range(PAIRS):
                    mm = nc.tensor.transpose(tp[:, c * P:(c + 1) * P], rot[:, 0, j, 2 * c:2 * c + 2, :].rearrange("p h d -> p (h d)"), ident[:, :])
                mm.then_inc(s["turn_done"], 1)

            def scores(i, k, h):
                u, r, st, w = i * UNITS + k, k % 2, k % ST, k // ST
                if h == 0:
                    pe.wait_ge(s["turn_set"], u * 3 + 3)
                if k > 0 or h > 0:
                    pe.wait_ge(s["exp_done"], u * 2 + h)
                for b in range(2):
                    if w > 0:
                        mask = band[:, :, :].unsqueeze(1).to_broadcast([P, 2, 2, P])
                    else:
                        mask = band0[:, bass.ds(i % GPB, 1), :, :].to_broadcast([P, 2, 2, P])
                    nc.tensor.matmul(sc[:, b, :].rearrange("p (a b q) -> p a b q", a=2, b=2), identb[:, :], mask, start=True, stop=False)
                    for d in range(2):
                        hd = 4 * h + 2 * b + d
                        keys = kT[:, st, hd // 2, w - 1:w + 1, :] if w > 0 else kT[:, st, hd // 2, 0:TPG:TPG - 1, :]
                        mm = nc.tensor.matmul(sc[:, b, d * 2 * P:(d + 1) * 2 * P], qz[:, r, hd, :], keys, start=False, stop=(d == 1))
                mm.then_inc(s["s_done"], 1)

            def turn_p(i, k, h):
                u = i * UNITS + k
                pe.wait_ge(s["pn_done"], u * 2 + h + 1)
                if k > 0 or h > 0:
                    pe.wait_ge(s["ptA"], u * 2 + h)
                    pe.wait_ge(s["ptB"], u * 2 + h)
                for a in range(8):
                    mm = nc.tensor.transpose(pt[:, a // 4, (a % 4) * P:(a % 4 + 1) * P], pr[:, h, a // 2, (a % 2) * P:(a % 2 + 1) * P], ident[:, :])
                mm.then_inc(s["pt_done"], 1)

            def values(i, k, h):
                u, st, w = i * UNITS + k, k % ST, k // ST
                pe.wait_ge(s["ptA"], u * 2 + h + 1)
                pe.wait_ge(s["ptB"], u * 2 + h + 1)
                if h == 0:
                    if k > 0:
                        pe.wait_ge(s["o_set"], u)
                    pe.wait_ge(s["qkv_set"], u * 3 + 3)
                slots = (w - 1, w) if w > 0 else (0, TPG - 1)
                for c in range(2):
                    pair = 2 * h + c
                    for blk in range(2):
                        for e in range(2):
                            mm = nc.tensor.matmul(ov[e * DH:(e + 1) * DH, pair * P:(pair + 1) * P],
                                                  v[:, st, slots[blk], (2 * pair + e) * DH:(2 * pair + e + 1) * DH],
                                                  prT[:, h, (2 * c + e) * 2 + blk, :], start=(blk == 0), stop=(blk == 1))
                mm.then_inc(s["pv_done"], 1)

            def out_projection(st, m):
                for c in range(PAIRS):
                    mm = nc.tensor.matmul((pj, sc)[st][:, m, :], wo[:, c, m * P:(m + 1) * P], attn[:, st, c, :],
                                          start=(c == 0), stop=(c == PAIRS - 1))
                if m == DC - 1:
                    mm.then_inc(s["wo_done"], 1)

            def mean(i, st):
                pe.wait_ge(s["x2_done"], i * ST + st + 1)
                for c in range(DC):
                    mm = nc.tensor.matmul((tp[:, :], pt[:, 1, :])[st], mean_w[:, :], x2[:, st, c, 1 - c:1 - c + G], start=(c == 0), stop=(c == DC - 1))
                mm.then_inc(s["mean_done"], 1)

            def variance(i, st):
                pe.wait_ge(s["sqm_done"], i * ST + st + 1)
                for c in range(DC):
                    mm = nc.tensor.matmul(pt[:, 0, :], mean_w[:, :], attn[:, st, 2 + c, :], start=(c == 0), stop=(c == DC - 1))
                mm.then_inc(s["var_done"], 1)

            def up(i, st, c):
                m = (i * ST + st) * HC + c
                if st > 0 or c >= 3:
                    pe.wait_ge(s["prod_done"], m - 2)
                for j in range(2):
                    n = 0
                    for d in range(DC):
                        for a, b in PASSES:
                            mm = nc.tensor.matmul(HIDDEN_BANKS[c % 3][j], w1[:, a, d, j, c * P:(c + 1) * P], hn[:, b, d, :], start=(n == 0), stop=(n == DC * 3 - 1))
                            n += 1
                mm.then_inc(s["ag_done"], 1)

            def down(i, st, c):
                m = (i * ST + st) * HC + c
                pe.wait_ge(s["hl_done"], m + 1)
                for d in range(DC):
                    for n, (a, b) in enumerate(PASSES):
                        mm = nc.tensor.matmul(pj[:, d, :], w2[:, a, c, d * P:(d + 1) * P], hid[:, c % 2, b, :],
                                              start=(c == 0 and n == 0), stop=(c == HC - 1 and n == 2))
                mm.then_inc(s["w2_done"], 1)

            def finish(i, st):
                pe.wait_ge(s["x3_done"], i * ST + st + 1)
                for t in range(TPG):
                    for c in range(DC):
                        mm = nc.tensor.transpose((sc, pt)[st][:, t // 2, (t % 2) * D + c * P:(t % 2) * D + (c + 1) * P], x2[:, st, c, 1 + t * P:1 + (t + 1) * P], ident[:, :])
                mm.then_inc(s["fin_done"], 1)

            def step(i, more):
                for k in range(UNITS):
                    scores(i, k, 0)
                    if k > 0:
                        turn_p(i, k - 1, 1)
                    if k + 1 < UNITS:
                        if k == 0:
                            pe.wait_ge(s["y_used"], i * ST + SEED)
                        project(i, k + 1, (2,))
                        turn_q(i, k + 1)
                    if k > 0:
                        values(i, k - 1, 1)
                    scores(i, k, 1)
                    turn_p(i, k, 0)
                    if k + 2 < UNITS:
                        project(i, k + 2, (0, 1))
                    if k + 1 < UNITS:
                        turn_k(i, k + 1)
                    values(i, k, 0)
                pe.wait_ge(s["o_set"], (i + 1) * UNITS - 1)
                pe.wait_ge(s["qkv_set"], (i + 1) * PROJ)
                out_projection(0, 0)
                out_projection(0, 1)
                turn_p(i, UNITS - 1, 1)
                values(i, UNITS - 1, 1)
                pe.wait_ge(s["turn_set"], (i + 1) * UNITS * 3)
                mean(i, 0)
                pe.wait_ge(s["o_set"], (i + 1) * UNITS)
                out_projection(1, 0)
                variance(i, 0)
                out_projection(1, 1)
                if more:
                    project(i + 1, 0, (0, 1), bank_free=False)
                mean(i, 1)
                if more:
                    project(i + 1, 0, (2,))
                pe.wait_ge(s["nl_done"], i * ST * DC + DC)
                up(i, 0, 0)
                pe.wait_ge(s["rsw_done"], i * ST + 1)
                variance(i, 1)
                up(i, 0, 1)
                pe.wait_ge(s["rsw_done"], i * ST + 2)
                up(i, 0, 2)
                if more:
                    project(i + 1, 1, (0, 1))
                    pe.wait_ge(s["qkv_set"], (i + 1) * PROJ + 5)
                down(i, 0, 0)
                for c in range(3, HC):
                    up(i, 0, c)
                    down(i, 0, c - 2)
                down(i, 0, HC - 2)
                for c in range(HC):
                    if c == 0:
                        pe.wait_ge(s["nl_done"], (i + 1) * ST * DC)
                    up(i, 1, c)
                    if c == 0:
                        down(i, 0, HC - 1)
                    if c == 2:
                        pe.wait_ge(s["y_used"], i * ST + 1 + SEED)
                    if c >= 2 and c < HC - 1:
                        down(i, 1, c - 2)
                if more:
                    pe.wait_ge(s["prod_done"], (i + 1) * ST * HC - 2)
                    turn_q(i + 1, 0)
                down(i, 1, HC - 3)
                if more:
                    turn_k(i + 1, 0)
                down(i, 1, HC - 2)
                if last_layer:
                    pe.wait_ge(s["prod_done"], (i + 1) * ST * HC - 1)
                    finish(i, 0)
                down(i, 1, HC - 1)
                if last_layer:
                    finish(i, 1)
                    pe.wait_ge(s["rows_set"], i * ST + 1)

            pe.wait_ge(s["zeroed"], ZEROED)
            pe.wait_ge(s["bands"], 4)
            project(0, 0, (0, 1), bank_free=False)
            project(0, 0, (2,))
            project(0, 1, (0, 1))
            turn_q(0, 0, first=True)
            turn_k(0, 0)
            with pe.Fori(0, STEPS - 1) as i:
                step(i, True)
            step(STEPS - 1, False)

        @block.vector
        def _(dve):
            def rotate(i, k, first=False):
                u, r, w = i * UNITS + k, k % 2, k // ST
                if k == 0:
                    dve.wait_ge(s["tab_set"], i + 1)
                dve.wait_ge(s["qkv_set"], u * 3 + 2)
                if not first:
                    dve.wait_ge(s["turn_done"], u * 2)
                t = tab[:, w, :, :]
                nc.vector.tensor_tensor(rot[:, 0, :, :, :], qk[:, r], t[:, 0:2, :].unsqueeze(2).to_broadcast([P, 2, H, DH]), ALU.mult).then_inc(s["rot_done"], 1)
                hw = DH // 2
                for e in range(2):
                    m = nc.vector.tensor_tensor(rot[:, 1, :, :, e * hw:(e + 1) * hw], qk[:, r, :, :, (1 - e) * hw:(2 - e) * hw],
                                                t[:, 2:4, e * hw:(e + 1) * hw].unsqueeze(2).to_broadcast([P, 2, H, hw]), ALU.mult)
                m.then_inc(s["rot_done"], 1)

            def sums(i, k):
                u, r = i * UNITS + k, k % 2
                dve.wait_ge(s["sq_done"], u + 1)
                nc.vector.tensor_reduce(ss[:, r, :], sq[:, :].rearrange("p (h d) -> p h d", d=DH), AXX, ALU.add).then_inc(s["sums_done"], 1)
                dve.wait_ge(s["sums_done"], u + 1)
                nc.vector.tensor_scalar(ss[:, r, :], ss[:, r, :], 1e-24, None, ALU.max).then_inc(s["ss_done"], 1)

            def scale_q(i, k):
                u, r = i * UNITS + k, k % 2
                dve.wait_ge(s["rr_done"], u + 1)
                nc.vector.tensor_tensor(nt[:, :], rg[:, :], rg[:, :], ALU.mult).then_inc(s["newton"], 1)
                dve.wait_ge(s["newton"], u * 2 + 1)
                nc.vector.scalar_tensor_tensor(out=nt[:, :], in0=nt[:, :], scalar=-0.5, in1=ss[:, r, :], op0=ALU.mult, op1=ALU.mult).then_inc(s["newton"], 1)
                dve.wait_ge(s["newton"], u * 2 + 2)
                nc.vector.scalar_tensor_tensor(out=rr[:, r, :], in0=nt[:, :], scalar=1.5, in1=rg[:, :], op0=ALU.add, op1=ALU.mult).then_inc(s["rn_done"], 1)
                dve.wait_ge(s["rn_done"], u + 1)
                nc.vector.tensor_scalar(q8[:, r, :], rr[:, r, 0:H], QK_SCALE, None, ALU.mult).then_inc(s["q8_done"], 1)

            def take_q(i, k):
                u, r = i * UNITS + k, k % 2
                dve.wait_ge(s["turn_done"], u * 2 + 1)
                for e in range(2):
                    half = slice(e * DH, (e + 1) * DH)
                    nc.vector.tensor_copy(qz[half, r, e::2, :], tp[half, :].rearrange("p (a q) -> p a q", q=P)).then_inc(s["turn_set"], 1)

            def take_k(i, k):
                u, st, w = i * UNITS + k, k % ST, k // ST
                dve.wait_ge(s["turn_done"], u * 2 + 2)
                nc.vector.tensor_copy(kT[:, st, :, w, :], tp[:, :].rearrange("p (a q) -> p a q", q=P)).then_inc(s["turn_set"], 1)

            def maxima(i, k, h):
                u, r = i * UNITS + k, k % 2
                dve.wait_ge(s["s_done"], u * 2 + h + 1)
                nc.vector.tensor_reduce(mx[:, :], sc[:, :, :].rearrange("p b (d j) -> p (b d) j", j=2 * P), AXX, ALU.max).then_inc(s["mx_done"], 1)
                dve.wait_ge(s["mx_done"], u * 2 + 1 + h)
                dve.wait_ge(s["q8_done"], u + 1)
                nc.vector.scalar_tensor_tensor(out=nb[:, h, :], in0=mx[:, :], scalar=-1.0, in1=q8[:, r, 4 * h:4 * h + 4],
                                               op0=ALU.mult, op1=ALU.mult).then_inc(s["nb_done"], 1)

            def inverse_sums(i, k, h):
                u = i * UNITS + k
                dve.wait_ge(s["exp_done"], u * 2 + h + 1)
                nc.vector.reciprocal(ri[:, h, :], rs[:, h, :]).then_inc(s["rcp_done"], 1)

            def take_pt(i, k, h):
                u = i * UNITS + k
                dve.wait_ge(s["pt_done"], u * 2 + h + 1)
                if last_layer and k == 0:
                    dve.wait_ge(stored[h], i * 16 + SEED)
                nc.vector.tensor_copy(prT[:, h, 4:8, :].rearrange("p a q -> p (a q)"), pt[:, 1, :]).then_inc(s["ptB"], 1)

            def take_o(i, k):
                u, st, w = i * UNITS + k, k % ST, k // ST
                dve.wait_ge(s["pv_done"], u * 2 + 2)
                nc.vector.tensor_copy(attn[:, st, :, w * P:(w + 1) * P], ov[:, :].rearrange("p (a q) -> p a q", q=P)).then_inc(s["o_set"], 1)

            def residual(i, st):
                n = i * ST + st
                dve.wait_ge(s["wo_done"], n + 1)
                if not last_layer:
                    dve.wait_ge(stored[st], i * 16 + SEED)
                nc.vector.tensor_tensor(x2[:, st, :, 1:], xin[:, st, :, 1:], (pj, sc)[st][:, :, :], ALU.add).then_inc(s["x2_done"], 1)
                dve.wait_ge(s["x2_done"], n + 1)
                nc.vector.tensor_scalar(xin[:, st, 1, 0:1], xin[:, st, 1, G:G + 1], flags[:, bass.ds((i + 1) % GPB, 1)], None, ALU.mult).then_inc(x_halo[st], 1)

            def centre(i, st):
                n = i * ST + st
                dve.wait_ge(s["mean_done"], n + 1)
                for c in range(DC):
                    m = nc.vector.tensor_tensor(attn[:, st, c, :], x2[:, st, c, 1 - c:1 - c + G], (tp[:, :], pt[:, 1, :])[st], ALU.subtract)
                m.then_inc(s["xc_done"], 1)
                dve.wait_ge(s["xc_done"], n + 1)
                nc.vector.tensor_scalar(x2[:, st, 1, 0:1], x2[:, st, 1, G:G + 1], flags[:, bass.ds((i + 1) % GPB, 1)], None, ALU.mult).then_inc(s["x2_halo"], 1)

            def normalise(i, st):
                n = i * ST + st
                dve.wait_ge(s["rsw_done"], n + 1)
                nc.vector.tensor_tensor(attn[:, st, 0:2, :], attn[:, st, 0:2, :], rsw[:, :].unsqueeze(1).to_broadcast([P, DC, G]), ALU.mult).then_inc(s["hn_done"], 1)

            def low_norm(i, st):
                n = i * ST + st
                for c in range(DC):
                    dve.wait_ge(s["nh_done"], n * DC + c + 1)
                    nc.vector.tensor_tensor(hn[:, 1, c, :], attn[:, st, c, :], hn[:, 0, c, :].bitcast(F32), ALU.subtract).then_inc(s["nl_done"], 1)

            def hidden(i, st, c):
                dve.wait_ge(s["gelu_done"], (i * ST + st) * HC + c + 1)
                nc.vector.scalar_tensor_tensor(out=act_g[:, c % 2, :], in0=HIDDEN_BANKS[c % 3][0], scalar=col[:, B1A + c:B1A + c + 1],
                                               in1=act_g[:, c % 2, :], op0=ALU.add, op1=ALU.mult).then_inc(s["prod_done"], 1)

            def low_hidden(i, st, c):
                dve.wait_ge(s["hh_done"], (i * ST + st) * HC + c + 1)
                nc.vector.tensor_tensor(hid[:, c % 2, 1, :], act_g[:, c % 2, :], hid[:, c % 2, 0, :].bitcast(F32), ALU.subtract).then_inc(s["hl_done"], 1)

            def output(i, st):
                n = i * ST + st
                dve.wait_ge(s["w2_done"], (n + 1) * HC)
                dve.wait_ge(s["x2_halo"], n + 1)
                for c in range(DC):
                    m = nc.vector.scalar_tensor_tensor(out=x2[:, st, c, 1:], in0=pj[:, c, :], scalar=col[:, B2 + c:B2 + c + 1],
                                                       in1=x2[:, st, c, 1:], op0=ALU.add, op1=ALU.add)
                m.then_inc(s["y_used"], 1)
                if last_layer:
                    dve.wait_ge(s["y_used"], n + 1 + SEED)
                    for c in range(DC):
                        m = nc.vector.tensor_scalar(x2[:, st, c, 1:], x2[:, st, c, 1:], gbg[:, bass.ds(i + st * STEPS, 1), c], None, ALU.mult)
                    m.then_inc(s["x3_done"], 1)

            def add_x1(i, st):
                n = i * ST + st
                dve.wait_ge(s["fin_done"], n + 1)
                dve.wait_ge(x1_in[st], i * 16 + 16)
                nc.vector.tensor_tensor(rows[:, st, :, :], (sc, pt)[st][:, :, :].rearrange("p j n -> p (j n)").rearrange("p (t d) -> p t d", d=D), x1[:, st, :, :], ALU.add).then_inc(s["rows_set"], 1)

            def step(i, more):
                for k in range(UNITS):
                    if k + 1 < UNITS:
                        rotate(i, k + 1)
                    maxima(i, k, 0)
                    if k > 0:
                        take_pt(i, k - 1, 1)
                    if k + 1 < UNITS:
                        sums(i, k + 1)
                    inverse_sums(i, k, 0)
                    if k + 1 < UNITS:
                        take_q(i, k + 1)
                    if k > 0:
                        take_o(i, k - 1)
                    maxima(i, k, 1)
                    take_pt(i, k, 0)
                    if k + 1 < UNITS:
                        scale_q(i, k + 1)
                    inverse_sums(i, k, 1)
                    if k + 1 < UNITS:
                        take_k(i, k + 1)
                residual(i, 0)
                take_pt(i, UNITS - 1, 1)
                take_o(i, UNITS - 1)
                centre(i, 0)
                normalise(i, 0)
                residual(i, 1)
                low_norm(i, 0)
                centre(i, 1)
                if more:
                    sums(i + 1, 0)
                normalise(i, 1)
                if more:
                    scale_q(i + 1, 0)
                for st in range(ST):
                    for c in range(HC):
                        hidden(i, st, c)
                        if c > 0:
                            low_hidden(i, st, c - 1)
                        if st == 0 and c == HC - 1:
                            low_norm(i, 1)
                        if st == 0 and c == 4 and more:
                            rotate(i + 1, 0)
                    if st == 1 and more:
                        take_q(i + 1, 0)
                    low_hidden(i, st, HC - 1)
                    if st == 1 and more:
                        take_k(i + 1, 0)
                    output(i, st)
                if last_layer:
                    for st in range(ST):
                        add_x1(i, st)

            dve.wait_ge(s["zeroed"], ZEROED)
            rotate(0, 0, first=True)
            sums(0, 0)
            scale_q(0, 0)
            take_q(0, 0)
            take_k(0, 0)
            with dve.Fori(0, STEPS - 1) as i:
                step(i, True)
            step(STEPS - 1, False)


PHASE_A = ("c", "wmod", "acol", "Wq", "Wk", "Wv", "Wo", "bk", "bv", "bo", "x")


def persistent(nc, ctx):
    sb = lambda name, shape, dt=F32: ctx.enter_context(nc.sbuf_tensor(name, shape, dt))
    return {
        "gbg": sb("gbg", [P, NG, DC]),
        "ident": sb("ident", [P, P]),
        "identb": sb("identb", [P, P], BF16),
        "flags": sb("flags", [P, GPB]),
        "eps": sb("eps", [P, 1]),
        "mean_w": sb("mean_w", [P, P]),
        "ln2x10": sb("ln2x10", [P, 1]),
    }


def first_block(nc, ctx):
    sb = lambda name, shape, dt=F32: ctx.enter_context(nc.sbuf_tensor(name, shape, dt))
    return {
        "modv": sb("modv", [P, MODS * DC, B]),
        "garow": sb("garow", [P, B, D]),
        "acol": sb("acol", [P, DC]),
        "blocks": sb("blocks", [P, P]),
    }


def layout(inputs):
    import numpy as np

    a = {k.replace("L0_attn_", "").replace("L0_", ""): np.ascontiguousarray(v) for k, v in inputs.items()}
    cols = lambda v: v.reshape(-1, P).T
    out = {n: a[n] for n in ("Wq", "Wk", "Wv", "Wo", "bk", "bv", "bo", "wmod")}
    out["x"] = a["inputs_q"]
    out["c"] = np.ascontiguousarray(a["c"].reshape(B, DC, P).transpose(2, 1, 0))
    out["acol"] = np.ascontiguousarray(cols(a["bq"]))
    L = {k.replace("L0_ffn_", ""): np.ascontiguousarray(v) for k, v in inputs.items() if k.startswith("L0_ffn_")}
    for n in ("wqkv", "w1", "w2"):
        out[n] = L[n]
    out["wo"] = L["wo"]
    depth = L["w2"].shape[0]
    half = lambda v: np.concatenate([v[:, DH // 2:], v[:, :DH // 2]], axis=1)
    out["qks"] = np.ascontiguousarray(np.stack([L["q_scale"], L["k_scale"], half(L["q_scale"]), half(L["k_scale"])], axis=1))
    pad = lambda v: np.concatenate([v, np.zeros(HC * P - HID, np.float32)])
    out["cols"] = np.ascontiguousarray(np.stack([np.concatenate(
        [cols(L["ln_g"][l]), cols(L["ln_b"][l]), cols(pad(L["b1"][l][:HID])), cols(pad(L["b1"][l][HID:])), cols(L["b2"][l])], axis=1)
        for l in range(depth)]))
    out["tab"] = rotation_table()
    return out


def rotation_table():
    import numpy as np

    f = np.float32
    half_idx = np.arange(0, DH, 2, dtype=f)
    inv_freq = (f(1.0) / f(10000.0) ** (half_idx / f(DH))).astype(f)
    t = np.arange(S, dtype=f)
    freqs = t[:, None] * inv_freq[None, :]
    base = (half_idx + f(0.4 * DH)) / f(1.4 * DH)
    scale = (base[None, :] ** ((t - f(S // 2)) / f(P // 2))[:, None]).astype(f)
    cos, sin = np.cos(freqs).astype(f), np.sin(freqs).astype(f)
    two = lambda a, b: np.concatenate([a, b], axis=1)
    t4 = np.stack([two(cos * scale, cos * scale), two(cos / scale, cos / scale),
                   two(-sin * scale, sin * scale), two(-sin / scale, sin / scale)], axis=1)
    return np.ascontiguousarray(t4.reshape(S // P, P, 4, DH).transpose(1, 0, 2, 3).astype(f))


def build_program(nc, arrays, out):
    dram = dict(arrays)
    dram["out"] = out.rearrange("b (g t) d -> (b g) t d", t=G)
    dram["x1"] = nc.dram_tensor("x1_dram", (B, S, D), F32, kind="Internal").ap()
    for name in ("h0", "mid"):
        dram[name] = nc.dram_tensor(name + "_dram", (NG, P, DC * G), F32, kind="Internal").ap()
    with ExitStack() as ctx:
        keep = persistent(nc, ctx)
        with ExitStack() as first:
            known = {**keep, **first_block(nc, first)}
            setup_program(nc, ctx, dram, known)
            linear_attention_program(nc, dram, known)
        weights = layer_weights(nc, ctx)
        for layer in range(2):
            weights_program(nc, layer, dram, keep, weights)
            layer_program(nc, layer, dram, keep, weights)


def kernel(**inputs):
    import numpy as np
    import concourse.bacc as bacc
    from concourse.bass_utils import run_bass_kernel_spmd

    nc = bacc.Bacc("TRN2", target_bir_lowering=False, num_devices=1)
    arrays = layout({k: np.asarray(v) for k, v in inputs.items()})
    aps = {name: nc.dram_tensor(f"in_{name}_dram", a.shape, mybir.dt.from_np(a.dtype), kind="ExternalInput").ap()
           for name, a in arrays.items()}
    out = nc.dram_tensor("out_dram", (B, S, D), F32, kind="ExternalOutput").ap()
    build_program(nc, aps, out)
    r = run_bass_kernel_spmd(nc, [{f"in_{name}_dram": a for name, a in arrays.items()}], core_ids=[0])
    return r.results[0]["out_dram"]
```

```python
from contextlib import ExitStack, contextmanager

import concourse.bass as bass
from concourse import mybir

ALU = mybir.AluOpType
ACT = mybir.ActivationFunctionType
AXX = mybir.AxisListType.X
F32 = mybir.dt.float32
F32R = mybir.dt.float32r
BF16 = mybir.dt.bfloat16

P = 128
B, S, D = 4, 2048, 256
DC = D // P
G = 512
TPG = G // P
GPB = S // G
NG = B * GPB
ST = 2
STEPS = NG // ST
H, DH = 8, 64
INNER = H * DH
PAIRS = H // 2
HID = int(D * 4 * 2 / 3)
HC = -(-HID // P)
FULL = HC - 1
TAIL = HID - FULL * P
GATE = P // 2
NUP = 2 * FULL + 1
assert TAIL <= GATE
AH, AD = 16, 16
QK_SCALE = 8.0
BLOCKED = -1.0e30
MODS = 6
LG, LB, B1, B2 = 0, DC, 2 * DC, 2 * DC + NUP
NCOL = B2 + DC


@contextmanager
def cleared_semaphores(nc):
    taken = []

    def take(name):
        taken.append(nc.alloc_semaphore(name=name))
        return taken[-1]

    yield take
    nc.clear_and_free_semaphores(taken)
    nc.all_engine_barrier()


def guard_gate(engine, chained, v, sign):
    chained(engine.tensor_scalar(sign, v, 0.0, 2.0, ALU.is_ge, ALU.mult))
    chained(engine.tensor_scalar(sign, sign, -1.0, None, ALU.add))
    chained(engine.tensor_tensor(v, v, sign, ALU.mult))
    chained(engine.tensor_scalar(v, v, 0.25, None, ALU.max))
    chained(engine.tensor_tensor(v, v, sign, ALU.mult))


def setup_program(nc, ctx, dram, keep):
    with ExitStack() as own:
        sb = lambda name, shape, dt=F32: own.enter_context(nc.sbuf_tensor(name, shape, dt))
        ps = lambda name, shape: own.enter_context(nc.psum_tensor(name, shape, F32))
        used = own.enter_context(cleared_semaphores(nc))
        sem = lambda name: used(name)
        wmod = sb("wmod", [P, DC, MODS * D])
        c_in = sb("c_in", [P, DC, B])
        c_act = sb("c_act", [P, DC, B])
        sign = sb("sign", [P, DC, B])
        c_rep = sb("c_rep", [P, DC, B, P])
        mod_ps = ps("mod_ps", [P, MODS * DC, B])
        row_ps = ps("row_ps", [P, B, D])
        loaded, zeroed, selected = sem("loaded"), sem("zeroed"), sem("selected")
        silu_done, rep_done, mod_ready, mod_step = sem("silu_done"), sem("rep_done"), sem("mod_ready"), sem("mod_step")
        modv, ident, identb, blocks = keep["modv"], keep["ident"], keep["identb"], keep["blocks"]
        block = own.enter_context(nc.Block())

        @block.sync
        def _(sp):
            sp.dma_start(c_in[:, :, :], dram["c"]).then_inc(loaded, 16)
            sp.dma_start(wmod[:, :, :], dram["wmod"].rearrange("(c p) n -> p c n", p=P)).then_inc(loaded, 16)
            sp.dma_start(keep["acol"][:, :], dram["acol"]).then_inc(loaded, 16)
            sp.wait_ge(loaded, 48)

        @block.gpsimd
        def _(pool):
            nc.gpsimd.memset(ident[:, :], 0.0).then_inc(zeroed, 1)
            nc.gpsimd.memset(identb[:, :], 0.0).then_inc(zeroed, 1)
            nc.gpsimd.memset(blocks[:, :], 1.0).then_inc(zeroed, 1)
            nc.gpsimd.memset(keep["flags"][:, :], 1.0).then_inc(zeroed, 1)
            pool.wait_ge(zeroed, 4)
            for m in (ident, identb):
                nc.gpsimd.affine_select(out=m[:, :], in_=m[:, :], compare_op=ALU.not_equal, fill=1.0,
                                        base=0, pattern=[[-1, P]], channel_multiplier=1).then_inc(selected, 1)
            view = blocks[:, :].rearrange("p (h d) -> p h d", d=AD)
            nc.gpsimd.affine_select(out=view, in_=view, compare_op=ALU.is_ge, fill=0.0, base=0,
                                    pattern=[[-AD, P // AD], [0, AD]], channel_multiplier=1).then_inc(selected, 1)
            pool.wait_ge(selected, 3)
            nc.gpsimd.affine_select(out=view, in_=view, compare_op=ALU.is_ge, fill=0.0, base=AD - 1,
                                    pattern=[[AD, P // AD], [0, AD]], channel_multiplier=-1).then_inc(selected, 1)
            nc.gpsimd.memset(keep["flags"][:, 0:1], 0.0).then_inc(selected, 1)
            nc.gpsimd.memset(keep["eps"][:, :], 1e-5).then_inc(selected, 1)
            nc.gpsimd.memset(keep["mean_w"][:, :], 1.0 / D).then_inc(selected, 1)
            nc.gpsimd.memset(keep["ln2x10"][:, :], 6.931471805599453).then_inc(selected, 1)

        @block.scalar
        def _(act):
            act.wait_ge(loaded, 48)
            nc.scalar.activation(c_act[:, :, :], c_in[:, :, :], ACT.Silu).then_inc(silu_done, 1)

        @block.tensor
        def _(pe):
            pe.wait_ge(silu_done, 1)
            for j in range(MODS * DC):
                for c in range(DC):
                    mm = nc.tensor.matmul(mod_ps[:, j, :], wmod[:, c, j * P:(j + 1) * P], c_act[:, c, :],
                                          start=(c == 0), stop=(c == DC - 1))
            mm.then_inc(mod_ready, 1)
            pe.wait_ge(rep_done, 1)
            for b in range(B):
                for c in range(DC):
                    mm = nc.tensor.matmul(row_ps[:, b, :], c_rep[:, c, b, :], wmod[:, c, 2 * D:3 * D], start=(c == 0), stop=(c == DC - 1))
            mm.then_inc(mod_ready, 1)

        @block.vector
        def _(dve):
            step = [0]

            def chained(instruction):
                step[0] += 1
                instruction.then_inc(mod_step, 1)
                dve.wait_ge(mod_step, step[0])

            dve.wait_ge(silu_done, 1)
            nc.vector.tensor_copy(c_rep[:, :, :, :], c_act[:, :, :].unsqueeze(3).to_broadcast([P, DC, B, P])).then_inc(rep_done, 1)
            dve.wait_ge(loaded, 48)
            dve.wait_ge(mod_ready, 1)
            chained(nc.vector.tensor_copy(modv[:, :, :], mod_ps[:, :, :]))
            for j in (1, 4):
                v = modv[:, j * DC:(j + 1) * DC, :]
                chained(nc.vector.tensor_scalar(v, v, 1.0, None, ALU.add))
            dve.wait_ge(mod_ready, 2)
            chained(nc.vector.tensor_copy(keep["garow"][:, :, :], row_ps[:, :, :]))
            guard_gate(nc.vector, chained, modv[:, 5 * DC:6 * DC, :], sign[:, :, :])
            chained(nc.vector.tensor_copy(keep["gbg"][:, :, :].rearrange("p (b g) c -> p b g c", b=B),
                                          modv[:, 5 * DC:6 * DC, :].rearrange("p c b -> p b c").unsqueeze(2).to_broadcast([P, B, GPB, DC])))


def linear_attention_program(nc, dram, keep):
    WPB = GPB * TPG
    HPC = P // AD
    with ExitStack() as own:
        sb = lambda name, shape, dt=F32: own.enter_context(nc.sbuf_tensor("a_" + name, shape, dt))
        ps = lambda name, shape: own.enter_context(nc.psum_tensor("a_" + name, shape, F32))
        used = own.enter_context(cleared_semaphores(nc))
        sem = lambda name: used("a_" + name)
        modv, acol, eps, ident, blocks, garow = (keep[k] for k in ("modv", "acol", "eps", "ident", "blocks", "garow"))
        SA, CA, SB, CB = 0, DC, 3 * DC, 4 * DC

        wq = sb("wq", [P, DC, D])
        wkv = sb("wkv", [P, DC, 2 * D])
        wo = sb("wo", [P, DC, D])
        wog = sb("wog", [P, B, DC, D])
        bkv = sb("bkv", [P, 2 * D])
        bo = sb("bo", [P, D])
        gabo = sb("gabo", [P, B, D])
        ga_sign = sb("ga_sign", [P, B, D])
        xt = sb("xt", [P, GPB, TPG, D])
        xr = sb("xr", [P, GPB, TPG, D])
        xn = sb("xn", [P, 2, TPG, D])
        stats = sb("stats", [P, TPG, 6])
        mv = sb("mv", [P, 2, TPG, 2])
        lnv = sb("lnv", [P, TPG])
        rstd = sb("rstd", [P, 2, TPG])
        stats2 = sb("stats2", [P, 6])
        mv2 = sb("mv2", [P, 2, TPG, 2])
        lnv2 = sb("lnv2", [P, TPG])
        rstd2 = sb("rstd2", [P, 2, TPG])
        hT = sb("hT", [P, 2, DC, P])
        kk = sb("kk", [P, 2, D])
        ek = sb("ek", [P, 2, D])
        kf = sb("kf", [P, 2, D])
        vo = sb("vo", [P, 2, DC, P + 1])
        eq = sb("eq", [P, 2, DC, P])
        rq = sb("rq", [P, 2, DC, P])
        qT = sb("qT", [P, WPB, DC, P])
        ksum = sb("ksum", [P, DC])
        kvd = sb("kvd", [P, DC, P + HPC])
        den = sb("den", [P, DC, HPC])
        o = sb("o", [P, 2, D])
        oT = sb("oT", [P, 2, DC, P])
        hn = sb("hn", [P, 2, TPG, D])
        h0 = sb("h0", [P, 2, DC, G])
        mod1 = sb("mod1", [P, MODS * DC])
        mod2 = sb("mod2", [P, MODS * DC])
        idle = sb("idle", [P, 1])
        idle2 = sb("idle2", [P, 1])
        seed = sb("seed", [P, 3])

        kvp = ps("kvp", [P, 2 * D])
        qp = ps("qp", [P, DC, P])
        acc = ps("acc", [P, DC, P + 1])
        nd = ps("nd", [P, DC, P + HPC])
        y = ps("y", [P, D])
        tx = ps("tx", [P, DC, P])
        to = ps("to", [P, DC, P])
        th = ps("th", [P, DC, P])

        x_in = [sem(f"x_in{g}") for g in range(GPB)]
        x1_stored = [sem(f"x1_stored{g}") for g in range(GPB)]
        h0_stored = [sem(f"h0_stored{r}") for r in range(2)]
        names = ("idled kv_in wq_in wo_in ga_step wog_set gabo_set ones_set mod1_set mod2_set stat_done mv_done ln_done rstd_done xn_done tx_done hT_done kv_done "
                 "q_done k_set vo_done ek_done ek_cut kf_done eq_done rq_done qT_done acc_done ks_set kvd_done xr_done nd_done den_cut "
                 "rcp_done o_done to_done oT_done y_done x1_done stat2_done mv2_done ln2_done rstd2_done hn_done th_done h0_done").split()
        s = {name: sem(name) for name in names}
        SEED = 1
        block = own.enter_context(nc.Block())

        def h_bank(w):
            return y[:, :].rearrange("p (c n) -> p c n", c=DC) if w > WPB - TPG and w % 2 else th[:, :, :]

        def bodies(engine, body):
            body(0, True, False, True)
            with engine.Fori(1, B - 1) as b:
                body(b, True, True, True)
            body(B - 1, True, True, False)
            body(B, False, True, False)

        @block.sync
        def _(sp):
            def load_x(b, g):
                sp.dma_start(xt[:, g, :, :], dram["x"][bass.ds(b, 1), g * G:(g + 1) * G, :].rearrange("a (t p) d -> p (a t) d", p=P)).then_inc(x_in[g], 16)

            def store_h0(b, g):
                sp.wait_ge(s["h0_done"], (b * GPB + g + 1) * TPG + SEED)
                sp.dma_start(dram["h0"][bass.ds(b * GPB + g, 1)].rearrange("a p n -> (a p) n"), h0[:, g % 2, :, :].rearrange("p c n -> p (c n)")).then_inc(h0_stored[g % 2], 16)

            def body(b, first, second, more):
                for g in range(GPB):
                    if second:
                        sp.wait_ge(s["x1_done"], ((b - 1) * GPB + g + 1) * TPG)
                        sp.dma_start(dram["x1"][bass.ds(b - 1, 1), g * G:(g + 1) * G, :].rearrange("a (t p) d -> p (a t) d", p=P), xr[:, g, :, :]).then_inc(x1_stored[g], 16)
                        if g > 0:
                            store_h0(b - 1, g - 1)
                    if first and more:
                        sp.wait_ge(s["xn_done"], (b * GPB + g + 1) * TPG)
                        if not second or g > 0:
                            h = g if not second else g - 1
                            sp.wait_ge(s["xr_done"], b * GPB + h + 1)
                            load_x(b + 1, h)
                if second:
                    store_h0(b - 1, GPB - 1)
                    if first and more:
                        sp.wait_ge(s["xr_done"], (b + 1) * GPB)
                        load_x(b + 1, GPB - 1)

            load_x(0, 0)
            for j, src in enumerate(("Wk", "Wv")):
                sp.dma_start(wkv[:, :, j * D:(j + 1) * D], dram[src].rearrange("(c p) n -> p c n", p=P)).then_inc(s["kv_in"], 16)
            for g in range(1, GPB):
                load_x(0, g)
            bodies(sp, body)
            for g in range(GPB):
                sp.wait_ge(x1_stored[g], B * 16)
            for r in range(2):
                sp.wait_ge(h0_stored[r], B * GPB // 2 * 16 + SEED)

        @block.gpsimd
        def _(pool):
            for n, seeded in enumerate(h0_stored + [s["h0_done"]]):
                nc.gpsimd.memset(seed[:, n:n + 1], 0.0).then_inc(seeded, SEED)
            nc.gpsimd.memset(idle2[:, :], 0.0).then_inc(s["idled"], 1)
            step = [0]

            def chained(instruction):
                step[0] += 1
                instruction.then_inc(s["ga_step"], 1)
                pool.wait_ge(s["ga_step"], step[0])

            guard_gate(nc.gpsimd, chained, garow[:, :, :], ga_sign[:, :, :])
            pool.wait_ge(s["wo_in"], 2 * 16)
            nc.gpsimd.tensor_tensor(gabo[:, :, :], garow[:, :, :], bo[:, :].unsqueeze(1).to_broadcast([P, B, D]), ALU.mult).then_inc(s["gabo_set"], 1)
            for b in range(B):
                nc.gpsimd.tensor_tensor(wog[:, b, :, :], wo[:, :, :], garow[:, b, :].unsqueeze(1).to_broadcast([P, DC, D]), ALU.mult).then_inc(s["wog_set"], 1)
            pool.wait_ge(s["gabo_set"], 1)

            def body(b, first, second, more):
                if not first:
                    return
                for g in range(GPB):
                    pool.wait_ge(x_in[g], b * 16 + 16)
                    if second:
                        pool.wait_ge(x1_stored[g], b * 16)
                        pool.wait_ge(s["hn_done"], ((b - 1) * GPB + g + 1) * TPG)
                    pool.wait_ge(s["idled"], b * GPB + g + 1)
                    nc.gpsimd.tensor_tensor(idle2[:, :], idle2[:, :], idle2[:, :], ALU.add).then_inc(s["idled"], 1)
                    nc.gpsimd.tensor_tensor(xr[:, g, :, :], xt[:, g, :, :], gabo[:, bass.ds(b, 1), :].to_broadcast([P, TPG, D]), ALU.add).then_inc(s["xr_done"], 1)

            bodies(pool, body)

        @block.scalar
        def _(act):
            def deviation(done, out_ln, ln_done, out, rstd_done, var, n, count):
                act.wait_ge(done, count)
                nc.scalar.activation(out_ln, var, ACT.Ln, bias=eps[:, 0:1]).then_inc(ln_done, 1)
                act.wait_ge(ln_done, n + 1)
                nc.scalar.activation(out, out_ln, ACT.Exp, scale=-0.5).then_inc(rstd_done, 1)

            def deviation1(n, g):
                deviation(s["mv_done"], lnv[:, :], s["ln_done"], rstd[:, g % 2, :], s["rstd_done"], mv[:, g % 2, :, 1], n, (n + 1) * TPG)

            def deviation2(n, g):
                deviation(s["mv2_done"], lnv2[:, :], s["ln2_done"], rstd2[:, g % 2, :], s["rstd2_done"], mv2[:, g % 2, :, 1], n, (n + 1) * TPG)

            def modulate(m, w):
                act.wait_ge(s["tx_done"], m + 1)
                for c in range(DC):
                    h = nc.scalar.activation(hT[:, w % 2, c, :], tx[:, c, :], ACT.Identity, scale=mod1[:, CA + c:CA + c + 1], bias=mod1[:, SA + c:SA + c + 1])
                h.then_inc(s["hT_done"], 1)

            def body(b, first, second, more):
                if first:
                    act.wait_ge(s["mod1_set"], b + 1)
                    modulate(b * WPB, 0)
                for w in range(WPB):
                    g, t = w // TPG, w % TPG
                    m, m2 = b * WPB + w, (b - 1) * WPB + w
                    if first and w + 1 < WPB:
                        modulate(m + 1, w + 1)
                    if second:
                        if t == 0 and g > 0:
                            deviation2((b - 1) * GPB + g - 1, g - 1)
                        act.wait_ge(s["to_done"], m2 + 1)
                        nc.scalar.activation(oT[:, w % 2, :, :], to[:, :, :], ACT.Copy).then_inc(s["oT_done"], 1)
                    if first:
                        act.wait_ge(s["k_set"], m + 1)
                        nc.scalar.activation(ek[:, w % 2, :], kk[:, w % 2, :], ACT.Exp).then_inc(s["ek_done"], 1)
                        act.wait_ge(s["q_done"], m + 1)
                        for fn, dst, done in ((ACT.Exp, eq, "eq_done"), (ACT.Relu, rq, "rq_done")):
                            for c in range(DC):
                                a = nc.scalar.activation(dst[:, w % 2, c, :], qp[:, c, :], fn, bias=acol[:, c:c + 1])
                            a.then_inc(s[done], 1)
                        if t == 2 and (g + 1 < GPB or more):
                            deviation1(b * GPB + g + 1, g + 1)
                    if second and g > 0:
                        modulate2(b, w - TPG)
                if second:
                    deviation2(b * GPB - 1, GPB - 1)
                    for t in range(TPG):
                        modulate2(b, WPB - TPG + t)

            def modulate2(b, w):
                g, t = w // TPG, w % TPG
                m = (b - 1) * WPB + w
                if t == 0:
                    act.wait_ge(h0_stored[g % 2], ((b - 1) * (GPB // 2) + g // 2) * 16 + SEED)
                if w == 0:
                    act.wait_ge(s["mod2_set"], b)
                act.wait_ge(s["th_done"], m + 1)
                for c in range(DC):
                    h = nc.scalar.activation(h0[:, g % 2, c, t * P:(t + 1) * P], h_bank(w)[:, c, :], ACT.Identity, scale=mod2[:, CB + c:CB + c + 1], bias=mod2[:, SB + c:SB + c + 1])
                h.then_inc(s["h0_done"], 1)

            row = lambda src: dram[src].rearrange("(a n) -> a n", a=1).to_broadcast([P, D])
            for j, src in enumerate(("bk", "bv")):
                act.dma_start(bkv[:, j * D:(j + 1) * D], row(src)).then_inc(s["kv_in"], 16)
            for dst, src, done in ((wq, "Wq", "wq_in"), (wo, "Wo", "wo_in")):
                act.dma_start(dst[:, :, :], dram[src].rearrange("(c p) n -> p c n", p=P)).then_inc(s[done], 16)
            act.dma_start(bo[:, :], row("bo")).then_inc(s["wo_in"], 16)
            nc.scalar.preload_act_table_set("natural_log_exp_and_others")
            deviation1(0, 0)
            bodies(act, body)

        @block.tensor
        def _(pe):
            def turn(dst, src, done):
                for c in range(DC):
                    mm = nc.tensor.transpose(dst[:, c, :], src[:, c * P:(c + 1) * P], ident[:, :])
                mm.then_inc(s[done], 1)

            def turn_x(m, w):
                pe.wait_ge(s["xn_done"], m + 1)
                if w > 0:
                    pe.wait_ge(s["hT_done"], m)
                turn(tx, xn[:, (w // TPG) % 2, w % TPG, :], "tx_done")

            def attend(m, w):
                if w > 0:
                    pe.wait_ge(s["o_done"], m)
                for c in range(DC):
                    mm = nc.tensor.matmul(nd[:, c, :], qT[:, w, c, :], kvd[:, c, :], start=True, stop=True)
                mm.then_inc(s["nd_done"], 1)

            def accumulate(b, w):
                m = b * WPB + w
                pe.wait_ge(s["kf_done"], m + 1)
                pe.wait_ge(s["vo_done"], m + 1)
                if w == 0 and (not isinstance(b, int) or b > 0):
                    pe.wait_ge(s["kvd_done"], b * 3)
                for c in range(DC):
                    mm = nc.tensor.matmul(acc[:, c, :], kf[:, w % 2, c * P:(c + 1) * P], vo[:, w % 2, c, :],
                                          start=(w == 0 and c == 0), stop=(w == WPB - 1 and c == DC - 1))
                mm.then_inc(s["acc_done"], 1)

            def turn_h(m, w):
                pe.wait_ge(s["hn_done"], m + 1)
                if w > 0:
                    pe.wait_ge(s["h0_done"], m + SEED - (1 if w > WPB - TPG else 0))
                turn(h_bank(w), hn[:, (w // TPG) % 2, w % TPG, :], "th_done")

            def body(b, first, second, more):
                if first:
                    turn_x(b * WPB, 0)
                    pe.wait_ge(s["kv_in"], 4 * 16)
                    pe.wait_ge(s["wq_in"], 16)
                if second:
                    pe.wait_ge(s["wog_set"], B)
                    pe.wait_ge(s["kvd_done"], b * 3)
                    attend((b - 1) * WPB, 0)
                for w in range(WPB):
                    m, m2 = b * WPB + w, (b - 1) * WPB + w
                    if first:
                        pe.wait_ge(s["hT_done"], m + 1)
                        if w > 0:
                            pe.wait_ge(s["vo_done"], m)
                        for c in range(DC):
                            mm = nc.tensor.matmul(kvp[:, :], hT[:, w % 2, c, :], wkv[:, c, :], start=(c == 0), stop=(c == DC - 1))
                        mm.then_inc(s["kv_done"], 1)
                        if w + 1 < WPB:
                            turn_x(m + 1, w + 1)
                        if w > 0:
                            accumulate(b, w - 1)
                    if second:
                        pe.wait_ge(s["o_done"], m2 + 1)
                        if w > 0:
                            pe.wait_ge(s["oT_done"], m2)
                        turn(to, o[:, w % 2, :], "to_done")
                    if first:
                        if w > 0:
                            pe.wait_ge(s["rq_done"], m)
                        for d in range(DC):
                            for c in range(DC):
                                mm = nc.tensor.matmul(qp[:, d, :], wq[:, c, d * P:(d + 1) * P], hT[:, w % 2, c, :], start=(c == 0), stop=(c == DC - 1))
                        mm.then_inc(s["q_done"], 1)
                    if second:
                        if w + 1 < WPB:
                            attend(m2 + 1, w + 1)
                        pe.wait_ge(s["oT_done"], m2 + 1)
                        if w > 0:
                            pe.wait_ge(s["x1_done"], m2)
                        for c in range(DC):
                            mm = nc.tensor.matmul(y[:, :], oT[:, w % 2, c, :], wog[:, bass.ds(b - 1, 1), c, :].rearrange("p a n -> p (a n)"), start=(c == 0), stop=(c == DC - 1))
                        mm.then_inc(s["y_done"], 1)
                    if second and w >= TPG:
                        turn_h(m2 - TPG, w - TPG)
                if first:
                    accumulate(b, WPB - 1)
                if second:
                    for w in range(WPB - TPG, WPB):
                        turn_h((b - 1) * WPB + w, w)

            bodies(pe, body)

        @block.vector
        def _(dve):
            def statistics(b, g, t):
                n = b * GPB + g
                if t == 0:
                    dve.wait_ge(x_in[g % GPB], (b + g // GPB) * 16 + 16)
                nc.vector.bn_stats(stats[:, t, :], xt[:, g % GPB, t, :]).then_inc(s["stat_done"], 1)
                dve.wait_ge(s["stat_done"], n * TPG + t + 1)
                nc.vector.tensor_scalar(idle[:, :], idle[:, :], 1.0, None, ALU.mult)
                nc.vector.bn_aggr(mv[:, g % 2, t, :], stats[:, t, :]).then_inc(s["mv_done"], 1)

            def normalise(b, g, t):
                n = b * GPB + g
                if t == 0:
                    dve.wait_ge(s["rstd_done"], n + 1)
                nc.vector.tensor_scalar(xn[:, g % 2, t, :], xt[:, g % GPB, t, :], mv[:, g % 2, t, 0:1], rstd[:, g % 2, t:t + 1],
                                        ALU.subtract, ALU.mult).then_inc(s["xn_done"], 1)

            def normalise2(b, w):
                g, t = w // TPG, w % TPG
                if t == 0:
                    dve.wait_ge(s["rstd2_done"], (b - 1) * GPB + g + 1)
                nc.vector.tensor_scalar(hn[:, g % 2, t, :], xr[:, g, t, :], mv2[:, g % 2, t, 0:1], rstd2[:, g % 2, t:t + 1],
                                        ALU.subtract, ALU.mult).then_inc(s["hn_done"], 1)

            def divide(m, w):
                dve.wait_ge(s["nd_done"], m + 1)
                nc.vector.tensor_scalar(den[:, :, :], nd[:, :, P:], 1e-6, None, ALU.max).then_inc(s["den_cut"], 1)
                dve.wait_ge(s["den_cut"], m + 1)
                nc.vector.reciprocal(den[:, :, :], den[:, :, :]).then_inc(s["rcp_done"], 1)
                dve.wait_ge(s["rcp_done"], m + 1)
                nc.vector.tensor_tensor(o[:, w % 2, :].rearrange("p (c h d) -> p c h d", c=DC, d=AD), nd[:, :, 0:P].rearrange("p c (h d) -> p c h d", d=AD),
                                        den[:, :, :].unsqueeze(3).to_broadcast([P, DC, HPC, AD]), ALU.mult).then_inc(s["o_done"], 1)

            def body(b, first, second, more):
                if first:
                    if not isinstance(b, int) or b > 0:
                        dve.wait_ge(s["hT_done"], b * WPB)
                    nc.vector.tensor_scalar(mod1[:, :], modv[:, :, bass.ds(b, 1)].rearrange("p m a -> p (m a)"), 1.0, None, ALU.mult).then_inc(s["mod1_set"], 1)
                if second:
                    dve.wait_ge(s["h0_done"], (b - 1) * WPB + SEED)
                    nc.vector.tensor_scalar(mod2[:, :], modv[:, :, bass.ds(b - 1, 1)].rearrange("p m a -> p (m a)"), 1.0, None, ALU.mult).then_inc(s["mod2_set"], 1)
                    divide((b - 1) * WPB, 0)
                for w in range(WPB):
                    g, t = w // TPG, w % TPG
                    m, m2 = b * WPB + w, (b - 1) * WPB + w
                    if first:
                        dve.wait_ge(s["kv_done"], m + 1)
                        nc.vector.tensor_tensor(kk[:, w % 2, :], kvp[:, 0:D], bkv[:, 0:D], ALU.add).then_inc(s["k_set"], 1)
                        nc.vector.tensor_tensor(vo[:, w % 2, :, 0:P], kvp[:, D:].rearrange("p (c d) -> p c d", c=DC),
                                                bkv[:, D:].rearrange("p (c d) -> p c d", c=DC), ALU.add).then_inc(s["vo_done"], 1)
                    if second and g > 0:
                        normalise2(b, w - TPG)
                    if first:
                        dve.wait_ge(s["ek_done"], m + 1)
                        nc.vector.tensor_scalar(ek[:, w % 2, :], ek[:, w % 2, :], 1.0, None, ALU.min).then_inc(s["ek_cut"], 1)
                        dve.wait_ge(s["ek_cut"], m + 1)
                        nc.vector.scalar_tensor_tensor(out=kf[:, w % 2, :], in0=kk[:, w % 2, :], scalar=0.0, in1=ek[:, w % 2, :],
                                                       op0=ALU.max, op1=ALU.add).then_inc(s["kf_done"], 1)
                    if second and w + 1 < WPB:
                        divide(m2 + 1, w + 1)
                    if first:
                        dve.wait_ge(s["rq_done"], m + 1)
                        nc.vector.scalar_tensor_tensor(out=qT[:, w, :, :], in0=eq[:, w % 2, :, :], scalar=1.0, in1=rq[:, w % 2, :, :],
                                                       op0=ALU.min, op1=ALU.add).then_inc(s["qT_done"], 1)
                        if g + 1 < GPB or more:
                            if t < 2:
                                statistics(b, g + 1, 2 * t)
                                statistics(b, g + 1, 2 * t + 1)
                            else:
                                normalise(b, g + 1, 2 * t - 4)
                                normalise(b, g + 1, 2 * t - 3)
                    if second:
                        dve.wait_ge(s["y_done"], m2 + 1)
                        if t == 0:
                            dve.wait_ge(s["xr_done"], (b - 1) * GPB + g + 1)
                        nc.vector.tensor_tensor(xr[:, g, t, :], xr[:, g, t, :], y[:, :], ALU.add).then_inc(s["x1_done"], 1)
                        dve.wait_ge(s["x1_done"], m2 + 1)
                        nc.vector.bn_stats(stats2[:, :], xr[:, g, t, :]).then_inc(s["stat2_done"], 1)
                        dve.wait_ge(s["stat2_done"], m2 + 1)
                        nc.vector.tensor_scalar(idle[:, :], idle[:, :], 1.0, None, ALU.mult)
                        nc.vector.bn_aggr(mv2[:, g % 2, t, :], stats2[:, :]).then_inc(s["mv2_done"], 1)
                if second:
                    for w in range(WPB - TPG, WPB):
                        normalise2(b, w)
                if first:
                    dve.wait_ge(s["acc_done"], (b + 1) * WPB)
                    nc.vector.tensor_copy(ksum[:, :], acc[:, :, P]).then_inc(s["ks_set"], 1)
                    nc.vector.tensor_tensor(kvd[:, :, 0:P], acc[:, :, 0:P], blocks[:, :].unsqueeze(1).to_broadcast([P, DC, P]), ALU.mult).then_inc(s["kvd_done"], 1)
                    dve.wait_ge(s["ks_set"], b + 1)
                    for c in range(DC):
                        nc.vector.tensor_scalar(kvd[:, c, P:], blocks[:, 0:P:AD], ksum[:, c:c + 1], None, ALU.mult).then_inc(s["kvd_done"], 1)

            nc.vector.memset(vo[:, :, :, P:P + 1], 1.0).then_inc(s["ones_set"], 1)
            nc.vector.memset(idle[:, :], 0.0).then_inc(s["ones_set"], 1)
            dve.wait_ge(s["ones_set"], 2)
            for t in range(TPG):
                statistics(0, 0, t)
            for t in range(TPG):
                normalise(0, 0, t)
            dve.wait_ge(s["kv_in"], 4 * 16)
            bodies(dve, body)


def layer_weights(nc, ctx):
    sb = lambda name, shape, dt=F32: ctx.enter_context(nc.sbuf_tensor(name, shape, dt))
    return {
        "wqkv": sb("wqkv", [P, 2, DC, 3 * INNER], F32R),
        "w1": sb("w1", [P, 2, DC, NUP * P], F32R),
        "w2": sb("w2", [P, 2, HC, D], F32R),
        "wo": sb("wo", [P, PAIRS, D]),
        "col": sb("col", [P, NCOL]),
        "qks": sb("qks", [P, 4, DH]),
    }


def weights_program(nc, layer, dram, keep, weights):
    with ExitStack() as own:
        pre = f"w{layer}_"
        sb = lambda name, shape, dt=F32: own.enter_context(nc.sbuf_tensor(pre + name, shape, dt))
        sem = own.enter_context(cleared_semaphores(nc))
        w1 = sb("w1", [P, DC, NUP * P])
        w2 = sb("w2", [P, HC, D])
        wqkv = sb("wqkv", [P, DC, 3 * INNER])
        shift = own.enter_context(nc.psum_tensor(pre + "shift", [P, NUP], F32))
        small_in, w1_in, w2_in, wo_in = sem(pre + "small_in"), sem(pre + "w1_in"), sem(pre + "w2_in"), sem(pre + "wo_in")
        wqkv_in = [sem(pre + f"wqkv_in{c}") for c in range(DC)]
        padded, high, low = sem(pre + "padded"), sem(pre + "high"), sem(pre + "low")
        shift_done, shifted = sem(pre + "shift_done"), sem(pre + "shifted")
        col = weights["col"]
        block = own.enter_context(nc.Block())
        parts = [(wqkv[:, c], None, weights["wqkv"][:, 0, c], weights["wqkv"][:, 1, c]) for c in range(DC)]
        parts += [(w1[:, c], col[:, LG + c:LG + c + 1], weights["w1"][:, 0, c], weights["w1"][:, 1, c]) for c in range(DC)]
        parts += [(w2[:, :], None, weights["w2"][:, 0], weights["w2"][:, 1])]

        @block.sync
        def _(sp):
            sp.dma_start(col[:, :], dram["cols"][layer]).then_inc(small_in, 16)
            sp.dma_start(weights["qks"][:, :, :], dram["qks"][layer:layer + 1].to_broadcast([P, 4, DH])).then_inc(small_in, 16)
            for c in range(DC):
                sp.dma_start(wqkv[:, c, :], dram["wqkv"][layer][c * P:(c + 1) * P, :]).then_inc(wqkv_in[c], 16)
            sp.dma_start(weights["wo"][:, :, :], dram["wo"][layer].rearrange("(c p) n -> p c n", p=P)).then_inc(wo_in, 16)
            sp.wait_ge(wo_in, 16)

        @block.scalar
        def _(act):
            for j in range(2):
                for dst, src, width in ((j * FULL * P, j * HID, FULL * P), (2 * FULL * P + j * GATE, j * HID + FULL * P, TAIL)):
                    act.dma_start(w1[:, :, dst:dst + width], dram["w1"][layer][:, src:src + width].rearrange("(c p) n -> p c n", p=P)).then_inc(w1_in, 16)
            act.dma_start(w2[:, 0:HC - 1, :], dram["w2"][layer][0:(HC - 1) * P, :].rearrange("(c p) n -> p c n", p=P)).then_inc(w2_in, 16)
            act.wait_ge(padded, 3)
            act.dma_start(w2[0:TAIL, HC - 1, :], dram["w2"][layer][(HC - 1) * P:HID, :]).then_inc(w2_in, 16)
            for n, (w, scale, hi, lo) in enumerate(parts):
                if n < DC:
                    act.wait_ge(wqkv_in[n], 16)
                elif n < 2 * DC:
                    act.wait_ge(small_in, 32)
                    act.wait_ge(w1_in, 64)
                else:
                    act.wait_ge(w2_in, 32)
                if scale is None:
                    nc.scalar.activation(hi, w, ACT.Copy).then_inc(high, 1)
                else:
                    nc.scalar.activation(hi, w, ACT.Identity, scale=scale).then_inc(high, 1)

        @block.gpsimd
        def _(pool):
            for j in range(2):
                pad = 2 * FULL * P + j * GATE + TAIL
                nc.gpsimd.memset(w1[:, :, pad:pad + GATE - TAIL], 0.0).then_inc(padded, 1)
            nc.gpsimd.memset(w2[:, HC - 1, :], 0.0).then_inc(padded, 1)

        @block.tensor
        def _(pe):
            pe.wait_ge(small_in, 32)
            pe.wait_ge(w1_in, 64)
            pe.wait_ge(padded, 3)
            for m in range(NUP):
                for c in range(DC):
                    mm = nc.tensor.matmul(shift[:, m:m + 1], w1[:, c, m * P:(m + 1) * P], col[:, LB + c:LB + c + 1],
                                          start=(c == 0), stop=(c == DC - 1))
            mm.then_inc(shift_done, 1)

        @block.vector
        def _(dve):
            for n, (w, scale, hi, lo) in enumerate(parts):
                if n == len(parts) - 1:
                    dve.wait_ge(shift_done, 1)
                    nc.vector.tensor_tensor(col[:, B1:B1 + NUP], col[:, B1:B1 + NUP], shift[:, :], ALU.add).then_inc(shifted, 1)
                dve.wait_ge(high, n + 1)
                if scale is None:
                    nc.vector.tensor_tensor(lo, w, hi.bitcast(F32), ALU.subtract).then_inc(low, 1)
                else:
                    nc.vector.scalar_tensor_tensor(out=lo, in0=w, scalar=scale, in1=hi.bitcast(F32), op0=ALU.mult, op1=ALU.subtract).then_inc(low, 1)
            dve.wait_ge(low, len(parts))
            dve.wait_ge(shifted, 1)


def layer_program(nc, layer, dram, keep, weights):
    last_layer = layer == 1
    source = dram["mid"] if last_layer else dram["h0"]
    x1_rows = dram["x1"].rearrange("b (g t) d -> (b g) t d", t=G) if last_layer else None
    UNITS = TPG * ST
    PROJ = 3 * UNITS
    PASSES = ((0, 0), (0, 1), (1, 0))
    with ExitStack() as own:
        pre = f"l{layer}_"
        sb = lambda name, shape, dt=F32: own.enter_context(nc.sbuf_tensor(pre + name, shape, dt))
        ps = lambda name, shape: own.enter_context(nc.psum_tensor(pre + name, shape, F32))
        used = own.enter_context(cleared_semaphores(nc))
        sem = lambda name: used(pre + name)
        ident, identb, eps, mean_w, flags, gbg = (keep[k] for k in ("ident", "identb", "eps", "mean_w", "flags", "gbg"))
        wqkv, w1, w2, wo, col, qks = (weights[k] for k in ("wqkv", "w1", "w2", "wo", "col", "qks"))

        tab = sb("tab", [P, TPG, 4, DH])
        band = sb("band", [P, 2, P], BF16)
        band0 = sb("band0", [P, GPB, 2, P], BF16)
        xin = sb("xin", [P, ST, DC, 1 + G])
        x2 = sb("x2", [P, ST, DC, 1 + G])
        xw = sb("xw", [P, 2, 2, DC, P], F32R)
        kT = sb("kT", [P, ST, PAIRS, TPG, P])
        v = sb("v", [P, ST, TPG, INNER])
        attn = sb("attn", [P, ST, PAIRS, G])
        qk = sb("qk", [P, 2, 2, H, DH])
        sq = sb("sq", [P, 2 * INNER])
        ss = sb("ss", [P, 2, 2 * H])
        lss = sb("lss", [P, 2 * H])
        rg = sb("rg", [P, 2 * H])
        nt = sb("nt", [P, 2 * H])
        rr = sb("rr", [P, 2, 2 * H])
        q8 = sb("q8", [P, 2, H])
        rot = sb("rot", [P, 2, 2, H, DH])
        qz = sb("qz", [P, 2, H, P])
        mx = sb("mx", [P, 4])
        nb = sb("nb", [P, 2, 4])
        rs = sb("rs", [P, 2, 4])
        ri = sb("ri", [P, 2, 4])
        pr = sb("pr", [P, 2, 4, 2 * P])
        prT = sb("prT", [P, 2, 4 * 2, P])
        rsw = sb("rsw", [P, G])
        act_g = sb("act_g", [P, 2, G])
        hid = sb("hid", [P, 2, 2, G], F32R)
        hn = sb("hn", [P, 2, DC, G], F32R)
        const15 = sb("const15", [P, 1])
        seed = sb("seed", [P, 1 + ST])
        x1 = pr[:, :, :, :].rearrange("p s a n -> p s (a n)").rearrange("p s (t d) -> p s t d", t=TPG)
        rows = prT[:, :, :, :].rearrange("p s a n -> p s (a n)").rearrange("p s (t d) -> p s t d", t=TPG)

        pj = ps("pj", [P, 2, G])
        sc = ps("sc", [P, 2, G])
        pt = ps("pt", [P, 2, G])
        tp = ps("tp", [P, G])
        ov = ps("ov", [P, G])
        HIDDEN_BANKS = [(tp[:, :], ov[:, :]), (sc[:, 0, :], sc[:, 1, :]), (pt[:, 0, :], pt[:, 1, :])]

        names = ("tab_in halo_zeroed zeroed rest_zeroed bands tab_set xh_set xl_set proj_done qkv_set sq_done sums_done ss_done ln_done rr_done newton "
                 "rn_done q8_done rotq_done rotk_done sumq_done sumk_done kn_done turn_done turn_set s_done mx_done nb_done exp_done rcp_done pn_done "
                 "pt_done ptA ptB pv_done o_set wo_done x2_done x2_halo mean_done xs_done xc_done sqm_done sqs_done var_done lnw_done rsw_done "
                 "hn_done nh_done nl_done ag_done gelu_done prod_done hh_done hl_done w2_done y_used x3_done fin_done rows_set").split()
        s = {name: sem(name) for name in names}
        x_in = [sem(f"x_in{st}") for st in range(ST)]
        x1_in = [sem(f"x1_in{st}") for st in range(ST)]
        x_halo = [sem(f"x_halo{st}") for st in range(ST)]
        stored = [sem(f"stored{st}") for st in range(ST)]
        SEED = 1
        SEEDED = [s["y_used"]] + stored
        block = own.enter_context(nc.Block())
        ZEROED, REST_ZEROED = 5, 4

        @block.sync
        def _(sp):
            def load_x(i, st):
                sp.dma_start(xin[:, st, :, 1:], source[bass.ds(i + st * STEPS, 1)].rearrange("a p (c n) -> (a p) c n", c=DC)).then_inc(x_in[st], 16)

            def load_tab(i):
                sp.dma_start(tab[:, :, :, :], dram["tab"][:, bass.ds((i % GPB) * TPG, TPG), :, :]).then_inc(s["tab_in"], 16)

            def step(i, more):
                if more:
                    sp.wait_ge(s["rotk_done"], (i + 1) * UNITS)
                    load_tab(i + 1)
                    sp.wait_ge(x_halo[0], i + 1)
                    load_x(i + 1, 0)
                if last_layer:
                    sp.wait_ge(s["pt_done"], (i + 1) * UNITS * 2)
                    for st in range(ST):
                        sp.dma_start(x1[:, st, :, :], x1_rows[bass.ds(i + st * STEPS, 1)].rearrange("a (t p) d -> p (a t) d", p=P)).then_inc(x1_in[st], 16)
                if more:
                    sp.wait_ge(x_halo[1], i + 1)
                    load_x(i + 1, 1)

            load_x(0, 0)
            load_tab(0)
            load_x(0, 1)
            with sp.Fori(0, STEPS - 1) as i:
                step(i, True)
            step(STEPS - 1, False)

        @block.gpsimd
        def _(pool):
            z = s["zeroed"]
            nc.gpsimd.memset(xin[:, :, :, 0:1], 0.0).then_inc(s["halo_zeroed"], 1)
            nc.gpsimd.memset(const15[:, :], 1.5).then_inc(z, 1)
            nc.gpsimd.memset(band[:, :, :], 0.0).then_inc(z, 1)
            nc.gpsimd.memset(band0[:, 1:, :, :], 0.0).then_inc(z, 1)
            nc.gpsimd.memset(band0[:, 0, 0, :], 0.0).then_inc(z, 1)
            nc.gpsimd.memset(band0[:, 0, 1, :], BLOCKED).then_inc(z, 1)
            for n, seeded in enumerate(SEEDED):
                nc.gpsimd.memset(seed[:, n:n + 1], 0.0).then_inc(seeded, SEED)
            pool.wait_ge(z, ZEROED)
            pool.wait_ge(s["halo_zeroed"], 1)
            for view, pattern, cm in ((band[:, 0, :], [[1, P]], -1), (band[:, 1, :], [[-1, P]], 1),
                                      (band0[:, :, 0, :], [[0, GPB], [-1, P]], 1),
                                      (band0[:, 1:, 1, :], [[0, GPB - 1], [1, P]], -1)):
                nc.gpsimd.affine_select(out=view, in_=view, compare_op=ALU.is_ge, fill=BLOCKED, base=0,
                                        pattern=pattern, channel_multiplier=cm).then_inc(s["bands"], 1)

            def scale_tab(i):
                pool.wait_ge(s["tab_in"], i * 16 + 16)
                nc.gpsimd.tensor_tensor(tab[:, :, :, :], tab[:, :, :, :], qks[:, :, :].unsqueeze(1).to_broadcast([P, TPG, 4, DH]), ALU.mult).then_inc(s["tab_set"], 1)

            def low_x(i, k):
                u, r, st, w = i * UNITS + k, k % 2, k % ST, k // ST
                pool.wait_ge(s["xh_set"], (u + 1) * DC)
                for c in range(DC):
                    o = 1 + w * P - c
                    nc.gpsimd.tensor_tensor(xw[:, r, 1, c, :], xin[:, st, c, o:o + P], xw[:, r, 0, c, :].bitcast(F32), ALU.subtract).then_inc(s["xl_set"], 1)

            def rotate_q(i, k):
                u = i * UNITS + k
                pool.wait_ge(s["rotq_done"], u + 1)
                a, b = rot[:, 0, 0, :, :], rot[:, 1, 0, :, :]
                nc.gpsimd.tensor_tensor(a, a, b, ALU.add).then_inc(s["sumq_done"], 1)

            def refine_norms(i, k):
                u, r = i * UNITS + k, k % 2
                pool.wait_ge(s["rr_done"], u + 1)
                nc.gpsimd.tensor_tensor(nt[:, :], rg[:, :], rg[:, :], ALU.mult).then_inc(s["newton"], 1)
                pool.wait_ge(s["newton"], u * 3 + 1)
                nc.gpsimd.tensor_tensor(nt[:, :], nt[:, :], ss[:, r, :], ALU.mult).then_inc(s["newton"], 1)
                pool.wait_ge(s["newton"], u * 3 + 2)
                nc.gpsimd.tensor_tensor(nt[:, :], nt[:, :], const15[:, :].to_broadcast([P, 2 * H]), ALU.add).then_inc(s["newton"], 1)
                pool.wait_ge(s["newton"], u * 3 + 3)
                nc.gpsimd.tensor_tensor(rr[:, r, :], nt[:, :], rg[:, :], ALU.mult).then_inc(s["rn_done"], 1)

            def norm_k(i, k):
                u, r = i * UNITS + k, k % 2
                pool.wait_ge(s["sumk_done"], u + 1)
                pool.wait_ge(s["rn_done"], u + 1)
                kk = rot[:, 0, 1, :, :]
                nc.gpsimd.tensor_tensor(kk, kk, rr[:, r, H:].unsqueeze(2).to_broadcast([P, H, DH]), ALU.mult).then_inc(s["kn_done"], 1)

            def norm_p(i, k, h):
                u = i * UNITS + k
                pool.wait_ge(s["rcp_done"], u * 2 + h + 1)
                w = pr[:, h, :, :]
                nc.gpsimd.tensor_tensor(w, w, ri[:, h, :].unsqueeze(2).to_broadcast([P, 4, 2 * P]), ALU.mult).then_inc(s["pn_done"], 1)

            def ahead(i):
                low_x(i, 0)
                scale_tab(i)
                low_x(i, 1)
                refine_norms(i, 0)
                rotate_q(i, 0)
                norm_k(i, 0)

            def step(i, more):
                for k in range(UNITS):
                    if k > 0:
                        norm_p(i, k - 1, 1)
                    if k == 0:
                        rotate_q(i, 1)
                    if k + 2 < UNITS:
                        low_x(i, k + 2)
                    if 0 < k < UNITS - 1:
                        rotate_q(i, k + 1)
                    norm_p(i, k, 0)
                    if k + 1 < UNITS:
                        refine_norms(i, k + 1)
                        norm_k(i, k + 1)
                norm_p(i, UNITS - 1, 1)
                if more:
                    ahead(i + 1)

            ahead(0)
            with pool.Fori(0, STEPS - 1) as i:
                step(i, True)
            step(STEPS - 1, False)

        @block.scalar
        def _(act):
            def high_x(i, k):
                u, r, st, w = i * UNITS + k, k % 2, k % ST, k // ST
                if w == 0:
                    act.wait_ge(x_in[st], i * 16 + 16)
                for c in range(DC):
                    o = 1 + w * P - c
                    nc.scalar.activation(xw[:, r, 0, c, :], xin[:, st, c, o:o + P], ACT.Copy).then_inc(s["xh_set"], 1)

            def take(i, k, j):
                u, r, st, w = i * UNITS + k, k % 2, k % ST, k // ST
                act.wait_ge(s["proj_done"], u * 3 + j + 1)
                dst = qk[:, r, j, :, :].rearrange("p h d -> p (h d)") if j < 2 else v[:, st, w, :]
                nc.scalar.activation(dst, pj[:, (3 * k + j) % 2, :], ACT.Copy).then_inc(s["qkv_set"], 1)

            def squares(i, k, first=False):
                u, r = i * UNITS + k, k % 2
                act.wait_ge(s["qkv_set"], u * 3 + 2)
                if not first:
                    act.wait_ge(s["sums_done"], u)
                nc.scalar.activation(sq[:, :], qk[:, r].rearrange("p j h d -> p (j h d)"), ACT.Square).then_inc(s["sq_done"], 1)

            def inverse_norms(i, k):
                u, r = i * UNITS + k, k % 2
                act.wait_ge(s["ss_done"], u + 1)
                nc.scalar.activation(lss[:, :], ss[:, r, :], ACT.Ln, scale=-float(2 ** 21)).then_inc(s["ln_done"], 1)
                act.wait_ge(s["ln_done"], u + 1)
                nc.scalar.activation(rg[:, :], lss[:, :], ACT.Exp, scale=-0.5, bias=keep["ln2x10"][:, 0:1]).then_inc(s["rr_done"], 1)

            def softmax(i, k, h):
                u, r = i * UNITS + k, k % 2
                if k >= 1:
                    act.wait_ge(s["pt_done"], u * 2 + h - 1)
                for d in range(4):
                    if d % 2 == 0:
                        act.wait_ge(s["nb_done"], (u * 2 + h) * 2 + d // 2 + 1)
                    e = nc.scalar.activation(pr[:, h, d, :], sc[:, d // 2, (d % 2) * 2 * P:(d % 2 + 1) * 2 * P], ACT.Exp,
                                             scale=q8[:, r, 4 * h + d:4 * h + d + 1], bias=nb[:, h, d:d + 1],
                                             accum_out=rs[:, h, d:d + 1])
                    if d % 2 == 1:
                        e.then_inc(s["exp_done"], 1)

            def take_pt(i, k, h):
                u = i * UNITS + k
                act.wait_ge(s["pt_done"], u * 2 + h + 1)
                if last_layer and k == 0:
                    act.wait_ge(stored[h], i * 16 + SEED)
                nc.scalar.activation(prT[:, h, 0:4, :].rearrange("p a q -> p (a q)"), pt[:, 0, :], ACT.Copy).then_inc(s["ptA"], 1)

            def take_o(i, k):
                u, st, w = i * UNITS + k, k % ST, k // ST
                act.wait_ge(s["pv_done"], u * 2 + 2)
                nc.scalar.activation(attn[:, st, :, w * P:(w + 1) * P], ov[:, :].rearrange("p (a q) -> p a q", q=P), ACT.Copy).then_inc(s["o_set"], 1)

            def inverse_deviation(i, st):
                n = i * ST + st
                act.wait_ge(s["var_done"], n + 1)
                if st > 0:
                    act.wait_ge(s["hn_done"], n)
                nc.scalar.activation(rsw[:, :], pt[:, 0, :], ACT.Ln, bias=eps[:, 0:1]).then_inc(s["lnw_done"], 1)
                act.wait_ge(s["lnw_done"], n + 1)
                nc.scalar.activation(rsw[:, :], rsw[:, :], ACT.Exp, scale=-0.5).then_inc(s["rsw_done"], 1)

            def square_centred(i, st):
                act.wait_ge(s["xc_done"], i * ST + st + 1)
                nc.scalar.activation(attn[:, st, 2:4, :], attn[:, st, 0:2, :], ACT.Square).then_inc(s["sqm_done"], 1)

            def high_norm(i, st):
                act.wait_ge(s["hn_done"], i * ST + st + 1)
                if st > 0:
                    act.wait_ge(s["ag_done"], (i * ST + st) * HC)
                for c in range(DC):
                    nc.scalar.activation(hn[:, 0, c, :], attn[:, st, c, :], ACT.Copy).then_inc(s["nh_done"], 1)

            def gelu(i, st, c):
                m = (i * ST + st) * HC + c
                act.wait_ge(s["ag_done"], m + 1)
                if st > 0 or c >= 2:
                    act.wait_ge(s["hl_done"], m - 1)
                if c < FULL:
                    out, gate, bias = act_g[:, c % 2, :], HIDDEN_BANKS[c % 3][1], col[:, B1 + FULL + c:B1 + FULL + c + 1]
                else:
                    tail = slice(GATE, GATE + TAIL)
                    out, gate, bias = act_g[0:TAIL, c % 2, :], HIDDEN_BANKS[c % 3][0][tail, :], col[tail, B1 + 2 * FULL:B1 + NUP]
                nc.scalar.activation(out, gate, ACT.Gelu, bias=bias).then_inc(s["gelu_done"], 1)

            def high_hidden(i, st, c):
                m = (i * ST + st) * HC + c
                act.wait_ge(s["prod_done"], m + 1)
                if st > 0 or c >= 2:
                    act.wait_ge(s["w2_done"], m - 1)
                n = P if c < FULL else TAIL
                nc.scalar.activation(hid[0:n, c % 2, 0, :], act_g[0:n, c % 2, :], ACT.Copy).then_inc(s["hh_done"], 1)

            def step(i, more):
                for k in range(UNITS):
                    if k + 2 < UNITS:
                        act.wait_ge(s["proj_done"], (i * UNITS + k + 1) * 3)
                        high_x(i, k + 2)
                    if k > 0:
                        take_pt(i, k - 1, 1)
                    softmax(i, k, 0)
                    if k + 1 < UNITS:
                        take(i, k + 1, 2)
                        inverse_norms(i, k + 1)
                    if k > 0:
                        take_o(i, k - 1)
                    if k + 1 < UNITS:
                        take_pt(i, k, 0)
                    softmax(i, k, 1)
                    if k + 2 < UNITS:
                        for j in range(2):
                            act.wait_ge(s["rotk_done"], i * UNITS + k + 1)
                            take(i, k + 2, j)
                        squares(i, k + 2)
                take_pt(i, UNITS - 1, 0)
                take_pt(i, UNITS - 1, 1)
                take_o(i, UNITS - 1)
                square_centred(i, 0)
                if more:
                    high_x(i + 1, 0)
                inverse_deviation(i, 0)
                high_norm(i, 0)
                if more:
                    act.wait_ge(s["rotk_done"], (i + 1) * UNITS)
                    take(i + 1, 0, 0)
                    take(i + 1, 0, 1)
                    squares(i + 1, 0)
                square_centred(i, 1)
                if more:
                    take(i + 1, 0, 2)
                    high_x(i + 1, 1)
                inverse_deviation(i, 1)
                if more:
                    inverse_norms(i + 1, 0)
                for st in range(ST):
                    for c in range(HC):
                        if c > 0:
                            high_hidden(i, st, c - 1)
                        gelu(i, st, c)
                        if st == 0 and c == HC - 1:
                            high_norm(i, 1)
                        if st == 0 and c == 2 and more:
                            take(i + 1, 1, 0)
                            take(i + 1, 1, 1)
                            squares(i + 1, 1)
                    high_hidden(i, st, HC - 1)
                    if st == 1 and more:
                        nc.scalar.preload_act_table_set("natural_log_exp_and_others")
                    if not last_layer:
                        act.wait_ge(s["y_used"], i * ST + st + 1 + SEED)
                        act.dma_start(dram["mid"][bass.ds(i + st * STEPS, 1)].rearrange("a p (c n) -> (a p) c n", c=DC), x2[:, st, :, 1:]).then_inc(stored[st], 16)
                if last_layer:
                    for st in range(ST):
                        n = i * ST + st
                        act.wait_ge(s["rows_set"], n + 1)
                        act.dma_start(dram["out"][bass.ds(i + st * STEPS, 1)].rearrange("a (t p) d -> p (a t) d", p=P), rows[:, st, :, :]).then_inc(stored[st], 16)

            nc.scalar.preload_act_table_set("natural_log_exp_and_others")
            act.wait_ge(s["halo_zeroed"], 1)
            high_x(0, 0)
            take(0, 0, 0)
            take(0, 0, 1)
            squares(0, 0, first=True)
            take(0, 0, 2)
            high_x(0, 1)
            take(0, 1, 0)
            take(0, 1, 1)
            inverse_norms(0, 0)
            squares(0, 1)
            with act.Fori(0, STEPS - 1) as i:
                step(i, True)
            step(STEPS - 1, False)
            for st in range(ST):
                act.wait_ge(stored[st], STEPS * 16 + SEED)

        @block.tensor
        def _(pe):
            def project(i, k, js, bank_free=True):
                u, r = i * UNITS + k, k % 2
                pe.wait_ge(s["xl_set"], (u + 1) * DC)
                for j in js:
                    if bank_free:
                        pe.wait_ge(s["qkv_set"], u * 3 + j - 1)
                    n = 0
                    for c in range(DC):
                        for a, b in PASSES:
                            mm = nc.tensor.matmul(pj[:, (3 * k + j) % 2, :], xw[:, r, a, c, :], wqkv[:, b, c, j * INNER:(j + 1) * INNER],
                                                  start=(n == 0), stop=(n == DC * 3 - 1))
                            n += 1
                    mm.then_inc(s["proj_done"], 1)

            def turn_q(i, k, first=False):
                u = i * UNITS + k
                pe.wait_ge(s["sumq_done"], u + 1)
                if not first:
                    pe.wait_ge(s["turn_set"], u * 3)
                turn(0)

            def turn_k(i, k):
                u = i * UNITS + k
                pe.wait_ge(s["kn_done"], u + 1)
                pe.wait_ge(s["turn_set"], u * 3 + 2)
                turn(1)

            def turn(j):
                for c in range(PAIRS):
                    mm = nc.tensor.transpose(tp[:, c * P:(c + 1) * P], rot[:, 0, j, 2 * c:2 * c + 2, :].rearrange("p h d -> p (h d)"), ident[:, :])
                mm.then_inc(s["turn_done"], 1)

            def scores(i, k, h):
                u, r, st, w = i * UNITS + k, k % 2, k % ST, k // ST
                if h == 0:
                    pe.wait_ge(s["turn_set"], u * 3 + 3)
                for b in range(2):
                    if k > 0 or h > 0:
                        pe.wait_ge(s["exp_done"], (u * 2 + h) * 2 + b - 1)
                    if w > 0:
                        mask = band[:, :, :].unsqueeze(1).to_broadcast([P, 2, 2, P])
                    else:
                        mask = band0[:, bass.ds(i % GPB, 1), :, :].to_broadcast([P, 2, 2, P])
                    nc.tensor.matmul(sc[:, b, :].rearrange("p (a b q) -> p a b q", a=2, b=2), identb[:, :], mask, start=True, stop=False)
                    for d in range(2):
                        hd = 4 * h + 2 * b + d
                        keys = kT[:, st, hd // 2, w - 1:w + 1, :] if w > 0 else kT[:, st, hd // 2, 0:TPG:TPG - 1, :]
                        mm = nc.tensor.matmul(sc[:, b, d * 2 * P:(d + 1) * 2 * P], qz[:, r, hd, :], keys, start=False, stop=(d == 1))
                    mm.then_inc(s["s_done"], 1)

            def turn_p(i, k, h):
                u = i * UNITS + k
                pe.wait_ge(s["pn_done"], u * 2 + h + 1)
                if k > 0 or h > 0:
                    pe.wait_ge(s["ptA"], u * 2 + h)
                    pe.wait_ge(s["ptB"], u * 2 + h)
                for a in range(8):
                    mm = nc.tensor.transpose(pt[:, a // 4, (a % 4) * P:(a % 4 + 1) * P], pr[:, h, a // 2, (a % 2) * P:(a % 2 + 1) * P], ident[:, :])
                mm.then_inc(s["pt_done"], 1)

            def values(i, k, h):
                u, st, w = i * UNITS + k, k % ST, k // ST
                pe.wait_ge(s["ptA"], u * 2 + h + 1)
                pe.wait_ge(s["ptB"], u * 2 + h + 1)
                if h == 0:
                    if k > 0:
                        pe.wait_ge(s["o_set"], u)
                    pe.wait_ge(s["qkv_set"], u * 3 + 3)
                slots = (w - 1, w) if w > 0 else (0, TPG - 1)
                for c in range(2):
                    pair = 2 * h + c
                    for blk in range(2):
                        for e in range(2):
                            mm = nc.tensor.matmul(ov[e * DH:(e + 1) * DH, pair * P:(pair + 1) * P],
                                                  v[:, st, slots[blk], (2 * pair + e) * DH:(2 * pair + e + 1) * DH],
                                                  prT[:, h, (2 * c + e) * 2 + blk, :], start=(blk == 0), stop=(blk == 1))
                mm.then_inc(s["pv_done"], 1)

            def out_projection(st, m):
                for c in range(PAIRS):
                    mm = nc.tensor.matmul((pj, sc)[st][:, m, :], wo[:, c, m * P:(m + 1) * P], attn[:, st, c, :],
                                          start=(c == 0), stop=(c == PAIRS - 1))
                if m == DC - 1:
                    mm.then_inc(s["wo_done"], 1)

            def mean(i, st):
                pe.wait_ge(s["xs_done"], i * ST + st + 1)
                nc.tensor.matmul((tp[:, :], pt[:, 1, :])[st], mean_w[:, :], attn[:, st, 2, :], start=True, stop=True).then_inc(s["mean_done"], 1)

            def variance(i, st):
                pe.wait_ge(s["sqs_done"], i * ST + st + 1)
                nc.tensor.matmul(pt[:, 0, :], mean_w[:, :], attn[:, st, 2, :], start=True, stop=True).then_inc(s["var_done"], 1)

            def up(i, st, c):
                m = (i * ST + st) * HC + c
                if st > 0 or c >= 3:
                    pe.wait_ge(s["prod_done"], m - 2)
                for j in range(2 if c < FULL else 1):
                    n = 0
                    at = (j * FULL + c if c < FULL else 2 * FULL) * P
                    for d in range(DC):
                        for a, b in PASSES:
                            mm = nc.tensor.matmul(HIDDEN_BANKS[c % 3][j], w1[:, a, d, at:at + P], hn[:, b, d, :], start=(n == 0), stop=(n == DC * 3 - 1))
                            n += 1
                mm.then_inc(s["ag_done"], 1)

            def down(i, st, c):
                m = (i * ST + st) * HC + c
                pe.wait_ge(s["hl_done"], m + 1)
                for d in range(DC):
                    for n, (a, b) in enumerate(PASSES):
                        mm = nc.tensor.matmul(pj[:, d, :], w2[:, a, c, d * P:(d + 1) * P], hid[:, c % 2, b, :],
                                              start=(c == 0 and n == 0), stop=(c == HC - 1 and n == 2))
                mm.then_inc(s["w2_done"], 1)

            def finish(i, st):
                pe.wait_ge(s["x3_done"], i * ST + st + 1)
                for t in range(TPG):
                    for c in range(DC):
                        mm = nc.tensor.transpose((sc, pt)[st][:, t // 2, (t % 2) * D + c * P:(t % 2) * D + (c + 1) * P], x2[:, st, c, 1 + t * P:1 + (t + 1) * P], ident[:, :])
                mm.then_inc(s["fin_done"], 1)

            def step(i, more):
                for k in range(UNITS):
                    scores(i, k, 0)
                    if k > 0:
                        turn_p(i, k - 1, 1)
                    if k + 1 < UNITS:
                        if k == 0:
                            pe.wait_ge(s["y_used"], i * ST + SEED)
                        project(i, k + 1, (2,))
                    if k > 0:
                        values(i, k - 1, 1)
                    if k + 1 < UNITS:
                        turn_q(i, k + 1)
                    scores(i, k, 1)
                    if k == UNITS - 1:
                        pe.wait_ge(s["o_set"], (i + 1) * UNITS - 1)
                        pe.wait_ge(s["qkv_set"], (i + 1) * PROJ)
                        out_projection(0, 0)
                    turn_p(i, k, 0)
                    if k == UNITS - 1:
                        out_projection(0, 1)
                    if k + 2 < UNITS:
                        project(i, k + 2, (0, 1))
                    if k + 2 < UNITS:
                        turn_k(i, k + 1)
                    values(i, k, 0)
                    if k + 2 == UNITS:
                        turn_k(i, k + 1)
                turn_p(i, UNITS - 1, 1)
                pe.wait_ge(s["turn_set"], (i + 1) * UNITS * 3)
                mean(i, 0)
                values(i, UNITS - 1, 1)
                pe.wait_ge(s["o_set"], (i + 1) * UNITS)
                out_projection(1, 0)
                variance(i, 0)
                out_projection(1, 1)
                if more:
                    project(i + 1, 0, (0, 1), bank_free=False)
                mean(i, 1)
                if more:
                    project(i + 1, 0, (2,))
                pe.wait_ge(s["nl_done"], i * ST * DC + DC)
                up(i, 0, 0)
                pe.wait_ge(s["rsw_done"], i * ST + 1)
                variance(i, 1)
                up(i, 0, 1)
                pe.wait_ge(s["rsw_done"], i * ST + 2)
                up(i, 0, 2)
                if more:
                    project(i + 1, 1, (0, 1))
                    pe.wait_ge(s["qkv_set"], (i + 1) * PROJ + 5)
                down(i, 0, 0)
                for c in range(3, HC):
                    up(i, 0, c)
                    down(i, 0, c - 2)
                down(i, 0, HC - 2)
                for c in range(HC):
                    if c == 0:
                        pe.wait_ge(s["nl_done"], (i + 1) * ST * DC)
                    up(i, 1, c)
                    if c == 0:
                        down(i, 0, HC - 1)
                    if c == 2:
                        pe.wait_ge(s["y_used"], i * ST + 1 + SEED)
                    if c >= 2 and c < HC - 1:
                        down(i, 1, c - 2)
                if more:
                    pe.wait_ge(s["prod_done"], (i + 1) * ST * HC - 2)
                    turn_q(i + 1, 0)
                down(i, 1, HC - 3)
                down(i, 1, HC - 2)
                if more:
                    turn_k(i + 1, 0)
                if last_layer:
                    pe.wait_ge(s["prod_done"], (i + 1) * ST * HC - 1)
                    finish(i, 0)
                down(i, 1, HC - 1)
                if last_layer:
                    finish(i, 1)
                    pe.wait_ge(s["rows_set"], i * ST + 1)

            project(0, 0, (0, 1), bank_free=False)
            project(0, 0, (2,))
            project(0, 1, (0, 1))
            turn_q(0, 0, first=True)
            turn_k(0, 0)
            pe.wait_ge(s["rest_zeroed"], REST_ZEROED)
            pe.wait_ge(s["bands"], 4)
            with pe.Fori(0, STEPS - 1) as i:
                step(i, True)
            step(STEPS - 1, False)

        @block.vector
        def _(dve):
            def rotate(i, k, j, done, first=False):
                u, r, w = i * UNITS + k, k % 2, k // ST
                if k == 0 and j == 0:
                    dve.wait_ge(s["tab_set"], i + 1)
                dve.wait_ge(s["qkv_set"], u * 3 + j + 1)
                if not first:
                    dve.wait_ge(s["turn_done"], u * 2 + j - 1)
                nc.vector.tensor_tensor(rot[:, 0, j, :, :], qk[:, r, j], tab[:, w, j, :].unsqueeze(1).to_broadcast([P, H, DH]), ALU.mult)
                hw = DH // 2
                for e in range(2):
                    m = nc.vector.tensor_tensor(rot[:, 1, j, :, e * hw:(e + 1) * hw], qk[:, r, j, :, (1 - e) * hw:(2 - e) * hw],
                                                tab[:, w, 2 + j, e * hw:(e + 1) * hw].unsqueeze(1).to_broadcast([P, H, hw]), ALU.mult)
                m.then_inc(done, 1)

            def rotate_q(i, k, first=False):
                rotate(i, k, 0, s["rotq_done"], first)

            def rotate_k(i, k, first=False):
                rotate(i, k, 1, s["rotk_done"], first)
                dve.wait_ge(s["rotk_done"], i * UNITS + k + 1)
                a, b = rot[:, 0, 1, :, :], rot[:, 1, 1, :, :]
                nc.vector.tensor_tensor(a, a, b, ALU.add).then_inc(s["sumk_done"], 1)

            def sums(i, k):
                u, r = i * UNITS + k, k % 2
                dve.wait_ge(s["sq_done"], u + 1)
                nc.vector.tensor_reduce(ss[:, r, :], sq[:, :].rearrange("p (h d) -> p h d", d=DH), AXX, ALU.add).then_inc(s["sums_done"], 1)
                dve.wait_ge(s["sums_done"], u + 1)
                nc.vector.tensor_scalar(ss[:, r, :], ss[:, r, :], 1e-24, -0.5, ALU.max, ALU.mult).then_inc(s["ss_done"], 1)

            def scale_q(i, k):
                u, r = i * UNITS + k, k % 2
                dve.wait_ge(s["rn_done"], u + 1)
                nc.vector.tensor_scalar(q8[:, r, :], rr[:, r, 0:H], QK_SCALE, None, ALU.mult).then_inc(s["q8_done"], 1)

            def take_q(i, k):
                u, r = i * UNITS + k, k % 2
                dve.wait_ge(s["turn_done"], u * 2 + 1)
                for e in range(2):
                    half = slice(e * DH, (e + 1) * DH)
                    nc.vector.tensor_copy(qz[half, r, e::2, :], tp[half, :].rearrange("p (a q) -> p a q", q=P)).then_inc(s["turn_set"], 1)

            def take_k(i, k):
                u, st, w = i * UNITS + k, k % ST, k // ST
                dve.wait_ge(s["turn_done"], u * 2 + 2)
                nc.vector.tensor_copy(kT[:, st, :, w, :], tp[:, :].rearrange("p (a q) -> p a q", q=P)).then_inc(s["turn_set"], 1)

            def maxima(i, k, h):
                u, r = i * UNITS + k, k % 2
                dve.wait_ge(s["q8_done"], u + 1)
                for b in range(2):
                    n = (u * 2 + h) * 2 + b + 1
                    heads = slice(2 * b, 2 * b + 2)
                    dve.wait_ge(s["s_done"], n)
                    nc.vector.tensor_reduce(mx[:, heads], sc[:, b, :].rearrange("p (d j) -> p d j", j=2 * P), AXX, ALU.max).then_inc(s["mx_done"], 1)
                    dve.wait_ge(s["mx_done"], n)
                    nc.vector.scalar_tensor_tensor(out=nb[:, h, heads], in0=mx[:, heads], scalar=-1.0, in1=q8[:, r, 4 * h + 2 * b:4 * h + 2 * b + 2],
                                                   op0=ALU.mult, op1=ALU.mult).then_inc(s["nb_done"], 1)

            def inverse_sums(i, k, h):
                u = i * UNITS + k
                dve.wait_ge(s["exp_done"], (u * 2 + h + 1) * 2)
                nc.vector.reciprocal(ri[:, h, :], rs[:, h, :]).then_inc(s["rcp_done"], 1)

            def take_pt(i, k, h):
                u = i * UNITS + k
                dve.wait_ge(s["pt_done"], u * 2 + h + 1)
                if last_layer and k == 0:
                    dve.wait_ge(stored[h], i * 16 + SEED)
                nc.vector.tensor_copy(prT[:, h, 4:8, :].rearrange("p a q -> p (a q)"), pt[:, 1, :]).then_inc(s["ptB"], 1)

            def residual(i, st):
                n = i * ST + st
                dve.wait_ge(s["wo_done"], n + 1)
                if not last_layer:
                    dve.wait_ge(stored[st], i * 16 + SEED)
                nc.vector.tensor_tensor(x2[:, st, :, 1:], xin[:, st, :, 1:], (pj, sc)[st][:, :, :], ALU.add).then_inc(s["x2_done"], 1)
                dve.wait_ge(s["x2_done"], n + 1)
                nc.vector.tensor_tensor(attn[:, st, 2, :], x2[:, st, 0, 1:], x2[:, st, 1, 0:G], ALU.add).then_inc(s["xs_done"], 1)
                nc.vector.tensor_scalar(xin[:, st, 1, 0:1], xin[:, st, 1, G:G + 1], flags[:, bass.ds((i + 1) % GPB, 1)], None, ALU.mult).then_inc(x_halo[st], 1)

            def centre(i, st):
                n = i * ST + st
                dve.wait_ge(s["mean_done"], n + 1)
                for c in range(DC):
                    m = nc.vector.tensor_tensor(attn[:, st, c, :], x2[:, st, c, 1 - c:1 - c + G], (tp[:, :], pt[:, 1, :])[st], ALU.subtract)
                m.then_inc(s["xc_done"], 1)
                dve.wait_ge(s["xc_done"], n + 1)
                nc.vector.tensor_scalar(x2[:, st, 1, 0:1], x2[:, st, 1, G:G + 1], flags[:, bass.ds((i + 1) % GPB, 1)], None, ALU.mult).then_inc(s["x2_halo"], 1)

            def add_squares(i, st):
                n = i * ST + st
                dve.wait_ge(s["sqm_done"], n + 1)
                nc.vector.tensor_tensor(attn[:, st, 2, :], attn[:, st, 2, :], attn[:, st, 3, :], ALU.add).then_inc(s["sqs_done"], 1)

            def normalise(i, st):
                n = i * ST + st
                dve.wait_ge(s["rsw_done"], n + 1)
                nc.vector.tensor_tensor(attn[:, st, 0:2, :], attn[:, st, 0:2, :], rsw[:, :].unsqueeze(1).to_broadcast([P, DC, G]), ALU.mult).then_inc(s["hn_done"], 1)

            def low_norm(i, st):
                n = i * ST + st
                for c in range(DC):
                    dve.wait_ge(s["nh_done"], n * DC + c + 1)
                    nc.vector.tensor_tensor(hn[:, 1, c, :], attn[:, st, c, :], hn[:, 0, c, :].bitcast(F32), ALU.subtract).then_inc(s["nl_done"], 1)

            def hidden(i, st, c):
                dve.wait_ge(s["gelu_done"], (i * ST + st) * HC + c + 1)
                n, at = (P, B1 + c) if c < FULL else (TAIL, B1 + 2 * FULL)
                nc.vector.scalar_tensor_tensor(out=act_g[0:n, c % 2, :], in0=HIDDEN_BANKS[c % 3][0][0:n, :], scalar=col[0:n, at:at + 1],
                                               in1=act_g[0:n, c % 2, :], op0=ALU.add, op1=ALU.mult).then_inc(s["prod_done"], 1)

            def low_hidden(i, st, c):
                dve.wait_ge(s["hh_done"], (i * ST + st) * HC + c + 1)
                n = P if c < FULL else TAIL
                nc.vector.tensor_tensor(hid[0:n, c % 2, 1, :], act_g[0:n, c % 2, :], hid[0:n, c % 2, 0, :].bitcast(F32), ALU.subtract).then_inc(s["hl_done"], 1)

            def output(i, st):
                n = i * ST + st
                dve.wait_ge(s["w2_done"], (n + 1) * HC)
                dve.wait_ge(s["x2_halo"], n + 1)
                for c in range(DC):
                    m = nc.vector.scalar_tensor_tensor(out=x2[:, st, c, 1:], in0=pj[:, c, :], scalar=col[:, B2 + c:B2 + c + 1],
                                                       in1=x2[:, st, c, 1:], op0=ALU.add, op1=ALU.add)
                m.then_inc(s["y_used"], 1)
                if last_layer:
                    dve.wait_ge(s["y_used"], n + 1 + SEED)
                    for c in range(DC):
                        m = nc.vector.tensor_scalar(x2[:, st, c, 1:], x2[:, st, c, 1:], gbg[:, bass.ds(i + st * STEPS, 1), c], None, ALU.mult)
                    m.then_inc(s["x3_done"], 1)

            def add_x1(i, st):
                n = i * ST + st
                dve.wait_ge(s["fin_done"], n + 1)
                dve.wait_ge(x1_in[st], i * 16 + 16)
                nc.vector.tensor_tensor(rows[:, st, :, :], (sc, pt)[st][:, :, :].rearrange("p j n -> p (j n)").rearrange("p (t d) -> p t d", d=D), x1[:, st, :, :], ALU.add).then_inc(s["rows_set"], 1)

            def step(i, more):
                for k in range(UNITS):
                    if 0 < k < UNITS - 1:
                        rotate_q(i, k + 1)
                    maxima(i, k, 0)
                    if k > 0:
                        take_pt(i, k - 1, 1)
                    if k + 1 < UNITS:
                        rotate_k(i, k + 1)
                    inverse_sums(i, k, 0)
                    if k + 1 < UNITS:
                        sums(i, k + 1)
                        take_q(i, k + 1)
                    maxima(i, k, 1)
                    take_pt(i, k, 0)
                    inverse_sums(i, k, 1)
                    if k + 1 < UNITS:
                        take_k(i, k + 1)
                        scale_q(i, k + 1)
                residual(i, 0)
                take_pt(i, UNITS - 1, 1)
                centre(i, 0)
                add_squares(i, 0)
                normalise(i, 0)
                residual(i, 1)
                low_norm(i, 0)
                centre(i, 1)
                if more:
                    sums(i + 1, 0)
                add_squares(i, 1)
                normalise(i, 1)
                for st in range(ST):
                    for c in range(HC):
                        if c > 0:
                            low_hidden(i, st, c - 1)
                        hidden(i, st, c)
                        if st == 0 and c == HC - 1:
                            low_norm(i, 1)
                        if st == 1 and c == 1 and more:
                            rotate_q(i + 1, 0)
                        if st == 1 and c == 2 and more:
                            scale_q(i + 1, 0)
                            rotate_k(i + 1, 0)
                        if st == 1 and c == HC - 1 and more:
                            take_q(i + 1, 0)
                    low_hidden(i, st, HC - 1)
                    if st == 1 and more:
                        take_k(i + 1, 0)
                    if st == 1 and not last_layer and more:
                        rotate_q(i + 1, 1)
                    if st == 1 and last_layer:
                        add_x1(i, 0)
                    output(i, st)
                if last_layer:
                    if more:
                        rotate_q(i + 1, 1)
                    add_x1(i, 1)

            for zero in (qz[:, :, :, :], x2[:, :, :, 0:1], kT[:, :, :, TPG - 1, :], v[:, :, TPG - 1, :]):
                nc.vector.memset(zero, 0.0).then_inc(s["rest_zeroed"], 1)
            dve.wait_ge(s["rest_zeroed"], REST_ZEROED)
            rotate_q(0, 0, first=True)
            rotate_k(0, 0, first=True)
            sums(0, 0)
            scale_q(0, 0)
            take_q(0, 0)
            take_k(0, 0)
            rotate_q(0, 1)
            with dve.Fori(0, STEPS - 1) as i:
                step(i, True)
            step(STEPS - 1, False)


PHASE_A = ("c", "wmod", "acol", "Wq", "Wk", "Wv", "Wo", "bk", "bv", "bo", "x")


def persistent(nc, ctx):
    sb = lambda name, shape, dt=F32: ctx.enter_context(nc.sbuf_tensor(name, shape, dt))
    return {
        "gbg": sb("gbg", [P, NG, DC]),
        "ident": sb("ident", [P, P]),
        "identb": sb("identb", [P, P], BF16),
        "flags": sb("flags", [P, GPB]),
        "eps": sb("eps", [P, 1]),
        "mean_w": sb("mean_w", [P, P]),
        "ln2x10": sb("ln2x10", [P, 1]),
    }


def first_block(nc, ctx):
    sb = lambda name, shape, dt=F32: ctx.enter_context(nc.sbuf_tensor(name, shape, dt))
    return {
        "modv": sb("modv", [P, MODS * DC, B]),
        "garow": sb("garow", [P, B, D]),
        "acol": sb("acol", [P, DC]),
        "blocks": sb("blocks", [P, P]),
    }


def layout(inputs):
    import numpy as np

    a = {k.replace("L0_attn_", "").replace("L0_", ""): np.ascontiguousarray(v) for k, v in inputs.items()}
    cols = lambda v: v.reshape(-1, P).T
    out = {n: a[n] for n in ("Wq", "Wk", "Wv", "Wo", "bk", "bv", "bo", "wmod")}
    out["x"] = a["inputs_q"]
    out["c"] = np.ascontiguousarray(a["c"].reshape(B, DC, P).transpose(2, 1, 0))
    out["acol"] = np.ascontiguousarray(cols(a["bq"]))
    L = {k.replace("L0_ffn_", ""): np.ascontiguousarray(v) for k, v in inputs.items() if k.startswith("L0_ffn_")}
    for n in ("wqkv", "w1", "w2"):
        out[n] = L[n]
    out["wo"] = L["wo"]
    depth = L["w2"].shape[0]
    half = lambda v: np.concatenate([v[:, DH // 2:], v[:, :DH // 2]], axis=1)
    out["qks"] = np.ascontiguousarray(np.stack([L["q_scale"], L["k_scale"], half(L["q_scale"]), half(L["k_scale"])], axis=1))
    gap = np.zeros(GATE - TAIL, np.float32)

    def up_bias(b):
        value, gate = b[:HID], b[HID:]
        return cols(np.concatenate([value[:FULL * P], gate[:FULL * P], value[FULL * P:], gap, gate[FULL * P:], gap]))

    out["cols"] = np.ascontiguousarray(np.stack([np.concatenate(
        [cols(L["ln_g"][l]), cols(L["ln_b"][l]), up_bias(L["b1"][l]), cols(L["b2"][l])], axis=1) for l in range(depth)]))
    out["tab"] = rotation_table()
    return out


def rotation_table():
    import numpy as np

    f = np.float32
    half_idx = np.arange(0, DH, 2, dtype=f)
    inv_freq = (f(1.0) / f(10000.0) ** (half_idx / f(DH))).astype(f)
    t = np.arange(S, dtype=f)
    freqs = t[:, None] * inv_freq[None, :]
    base = (half_idx + f(0.4 * DH)) / f(1.4 * DH)
    scale = (base[None, :] ** ((t - f(S // 2)) / f(P // 2))[:, None]).astype(f)
    cos, sin = np.cos(freqs).astype(f), np.sin(freqs).astype(f)
    two = lambda a, b: np.concatenate([a, b], axis=1)
    t4 = np.stack([two(cos * scale, cos * scale), two(cos / scale, cos / scale),
                   two(-sin * scale, sin * scale), two(-sin / scale, sin / scale)], axis=1)
    return np.ascontiguousarray(t4.reshape(S // P, P, 4, DH).transpose(1, 0, 2, 3).astype(f))


def build_program(nc, arrays, out):
    dram = dict(arrays)
    dram["out"] = out.rearrange("b (g t) d -> (b g) t d", t=G)
    dram["x1"] = nc.dram_tensor("x1_dram", (B, S, D), F32, kind="Internal").ap()
    for name in ("h0", "mid"):
        dram[name] = nc.dram_tensor(name + "_dram", (NG, P, DC * G), F32, kind="Internal").ap()
    with ExitStack() as ctx:
        keep = persistent(nc, ctx)
        with ExitStack() as first:
            known = {**keep, **first_block(nc, first)}
            setup_program(nc, ctx, dram, known)
            linear_attention_program(nc, dram, known)
        weights = layer_weights(nc, ctx)
        for layer in range(2):
            weights_program(nc, layer, dram, keep, weights)
            layer_program(nc, layer, dram, keep, weights)


def kernel(**inputs):
    import numpy as np
    import concourse.bacc as bacc
    from concourse.bass_utils import run_bass_kernel_spmd

    nc = bacc.Bacc("TRN2", target_bir_lowering=False, num_devices=1)
    arrays = layout({k: np.asarray(v) for k, v in inputs.items()})
    aps = {name: nc.dram_tensor(f"in_{name}_dram", a.shape, mybir.dt.from_np(a.dtype), kind="ExternalInput").ap()
           for name, a in arrays.items()}
    out = nc.dram_tensor("out_dram", (B, S, D), F32, kind="ExternalOutput").ap()
    build_program(nc, aps, out)
    r = run_bass_kernel_spmd(nc, [{f"in_{name}_dram": a for name, a in arrays.items()}], core_ids=[0])
    return r.results[0]["out_dram"]
```
